# Optimizing a Trainium2 kernel written in Bass

```python
import numpy as np
import jax
import jax.numpy as jnp

def _softmax(x, axis=-1):
    return jax.nn.softmax(x, axis=axis)

def _gelu(x):
    return jax.nn.gelu(x, approximate=True)

def _silu(x):
    return jax.nn.silu(x)

def _sigmoid(x):
    return jax.nn.sigmoid(x)

def _layernorm(x, axis=-1, eps=1e-05):
    m = jnp.mean(x, axis=axis, keepdims=True)
    v = jnp.var(x, axis=axis, keepdims=True)
    return (x - m) / jnp.sqrt(v + eps)

def _scatter_add(tgt, idx, src, axis=0):
    return tgt.at[idx].add(src)

def _segment_sum(src, seg, n):
    return jax.ops.segment_sum(src, seg, n)
kernel_name = 'mk_decoder_preln_d1_seqx_r4_54d5a9'

def setup_inputs(seed: int=0):
    np.random.seed(seed)
    _w = jnp.asarray

    def _rec_inputs():
        import jax
        import jax.numpy as jnp
        _rk = jax.random.key(seed)
        x = 7.22e-05 + 1 * jax.random.normal(jax.random.fold_in(_rk, 1), (128, 128, 256), jnp.float32)
        _lenS = 128 - jax.random.randint(jax.random.fold_in(_rk, 7), (128,), 0, max(1, 128 // 4) + 1, jnp.int32)
        _lenS2 = 128 - jax.random.randint(jax.random.fold_in(_rk, 8), (128,), 0, max(1, 128 // 4) + 1, jnp.int32)
        _ctx_1024P = jax.random.normal(jax.random.fold_in(_rk, 11), (128, 16, 256), jnp.float32)
        _ctx_1024c = jax.random.dirichlet(jax.random.fold_in(_rk, 511), 0.3 * jnp.ones((16,), jnp.float32), (128, 128))
        _ctx_1024t = jnp.einsum('bsk,bkd->bsd', _ctx_1024c, _ctx_1024P)
        _ctx_1024t = _ctx_1024t * jax.lax.rsqrt(jnp.mean(jnp.square(_ctx_1024t)) + 1e-12) * 0.953939
        ctx_1024 = 4.13588e-05 + 0.999923 * (_ctx_1024t + 0.3 * jax.random.normal(jax.random.fold_in(_rk, 611), (128, 128, 256), jnp.float32))
        return (x, ctx_1024)
    x, ctx_1024 = _rec_inputs()

    def _L0_attn_setup():
        import jax, jax.numpy as jnp
        import numpy as np

        def _gla_forward(hidden_state, Wq, bq, Wk, bk, Wv, bv, Wg, bg, Wo, bo):
            q = hidden_state @ Wq + bq
            k = jax.nn.sigmoid(hidden_state @ Wk + bk)
            g = jax.nn.sigmoid(hidden_state @ Wg + bg)
            v = hidden_state @ Wv + bv
            B = hidden_state.shape[0]
            K = Wq.shape[1]
            V = Wv.shape[1]
            state0 = jnp.zeros((B, K, V), dtype=hidden_state.dtype)

            def step(state, inp):
                q_t, k_t, g_t, v_t = inp
                state = state * g_t[:, :, None] + k_t[:, :, None] * v_t[:, None, :]
                out_t = jnp.einsum('bkv,bk->bv', state, q_t)
                return (state, out_t)
            xs = (jnp.swapaxes(q, 0, 1), jnp.swapaxes(k, 0, 1), jnp.swapaxes(g, 0, 1), jnp.swapaxes(v, 0, 1))
            final_state, outs = jax.lax.scan(step, state0, xs)
            out = jnp.swapaxes(outs, 0, 1)
            out = out @ Wo + bo
            return (out, final_state)

        def _reference_tuple_inner(hidden_state, Wq, bq, Wk, bk, Wv, bv, Wg, bg, Wo, bo):
            return _gla_forward(hidden_state, Wq, bq, Wk, bk, Wv, bv, Wg, bg, Wo, bo)
        key = jax.random.key(seed)
        ks = jax.random.split(key, 12)
        B, T, H, K, V, O = (8, 512, 256, 64, 64, 256)
        s = 0.02
        return {'hidden_state': jax.random.normal(ks[0], (B, T, H), dtype=jnp.float32), 'Wq': jax.random.normal(ks[1], (H, K), dtype=jnp.float32) * s, 'bq': jax.random.normal(ks[2], (K,), dtype=jnp.float32) * s, 'Wk': jax.random.normal(ks[3], (H, K), dtype=jnp.float32) * s, 'bk': jax.random.normal(ks[4], (K,), dtype=jnp.float32) * s, 'Wv': jax.random.normal(ks[5], (H, V), dtype=jnp.float32) * s, 'bv': jax.random.normal(ks[6], (V,), dtype=jnp.float32) * s, 'Wg': jax.random.normal(ks[7], (H, K), dtype=jnp.float32) * s, 'bg': jax.random.normal(ks[8], (K,), dtype=jnp.float32) * s, 'Wo': jax.random.normal(ks[9], (V, O), dtype=jnp.float32) * s, 'bo': jax.random.normal(ks[10], (O,), dtype=jnp.float32) * s}
    _L0_attn_all = _L0_attn_setup()
    _L0_attn_in = {k: v for k, v in _L0_attn_all.items() if k in ('Wq', 'bq', 'Wk', 'bk', 'Wv', 'bv', 'Wg', 'bg', 'Wo', 'bo')}
    del _L0_attn_all

    def _L0_xattn_setup():
        import jax, jax.numpy as jnp
        import numpy as np
        D_MODEL = 256
        N_HEADS = 16
        HEAD_DIM = D_MODEL // N_HEADS
        SCALE = HEAD_DIM ** (-0.5)
        key = jax.random.key(seed)
        ks = jax.random.split(key, 11)
        B, L = (4, 512)
        s = 1.0 / np.sqrt(D_MODEL)
        inp = {'queries': jax.random.normal(ks[0], (B, L, D_MODEL), jnp.float32), 'keys': jax.random.normal(ks[1], (B, L, D_MODEL), jnp.float32), 'values': jax.random.normal(ks[2], (B, L, D_MODEL), jnp.float32), 'Wq': jax.random.normal(ks[3], (D_MODEL, D_MODEL), jnp.float32) * s, 'bq': jnp.zeros((D_MODEL,), jnp.float32), 'Wk': jax.random.normal(ks[4], (D_MODEL, D_MODEL), jnp.float32) * s, 'bk': jnp.zeros((D_MODEL,), jnp.float32), 'Wv': jax.random.normal(ks[5], (D_MODEL, D_MODEL), jnp.float32) * s, 'bv': jnp.zeros((D_MODEL,), jnp.float32), 'Wo': jax.random.normal(ks[6], (D_MODEL, D_MODEL), jnp.float32) * s, 'bo': jnp.zeros((D_MODEL,), jnp.float32)}
        return inp
    _L0_xattn_all = _L0_xattn_setup()
    _L0_xattn_in = {k: v for k, v in _L0_xattn_all.items() if k in ('Wq', 'bq', 'Wk', 'bk', 'Wv', 'bv', 'Wo', 'bo')}
    del _L0_xattn_all

    def _L0_ffn_setup():
        import jax, jax.numpy as jnp
        import numpy as np
        B, S, D, H, F = (4, 1024, 256, 16, 1024)
        CAP = 0.125
        ROPE_BASE = 10000.0

        def rmsnorm(x, g):
            return x * jax.lax.rsqrt(jnp.mean(x * x, -1, keepdims=True) + 1e-06) * g

        def rope(t, pos):
            hd = t.shape[-1]
            inv = 1.0 / ROPE_BASE ** (jnp.arange(0, hd, 2, dtype=jnp.float32) / hd)
            f = pos[:, None, :, None].astype(jnp.float32) * inv
            emb = jnp.concatenate([f, f], axis=-1)
            cos, sin = (jnp.cos(emb), jnp.sin(emb))
            rot = jnp.concatenate([-t[..., hd // 2:], t[..., :hd // 2]], axis=-1)
            return t * cos + rot * sin
        key = jax.random.key(seed)
        ks = jax.random.split(key, 9)
        scale = 0.02
        x = jax.random.normal(ks[0], (B, S, D), jnp.float32)
        causal = jnp.where(jnp.tril(jnp.ones((S, S), bool)), 0.0, -1000000000.0).astype(jnp.float32)
        attention_mask = jnp.broadcast_to(causal[None, None], (B, 1, S, S))
        position_ids = jnp.broadcast_to(jnp.arange(S, dtype=jnp.int32), (B, S))
        return {'x': x, 'attention_mask': attention_mask, 'position_ids': position_ids, 'router_w': jax.random.normal(ks[1], (D, 1), jnp.float32) * scale, 'router_b': jnp.zeros((1,), jnp.float32), 'wq': jax.random.normal(ks[2], (D, D), jnp.float32) * scale, 'wk': jax.random.normal(ks[3], (D, D), jnp.float32) * scale, 'wv': jax.random.normal(ks[4], (D, D), jnp.float32) * scale, 'wo': jax.random.normal(ks[5], (D, D), jnp.float32) * scale, 'w1': jax.random.normal(ks[6], (D, F), jnp.float32) * scale, 'w2': jax.random.normal(ks[7], (F, D), jnp.float32) * scale, 'ln1': jnp.ones((D,), jnp.float32), 'ln2': jnp.ones((D,), jnp.float32)}
    _L0_ffn_all = _L0_ffn_setup()
    _L0_ffn_in = {k: v for k, v in _L0_ffn_all.items() if k in ('attention_mask', 'position_ids', 'router_w', 'router_b', 'wq', 'wk', 'wv', 'wo', 'w1', 'w2', 'ln1', 'ln2')}
    del _L0_ffn_all
    return {'x': x, 'ctx_1024': ctx_1024, 'L0_attn_Wq': _L0_attn_in['Wq'], 'L0_attn_bq': _L0_attn_in['bq'], 'L0_attn_Wk': _L0_attn_in['Wk'], 'L0_attn_bk': _L0_attn_in['bk'], 'L0_attn_Wv': _L0_attn_in['Wv'], 'L0_attn_bv': _L0_attn_in['bv'], 'L0_attn_Wg': _L0_attn_in['Wg'], 'L0_attn_bg': _L0_attn_in['bg'], 'L0_attn_Wo': _L0_attn_in['Wo'], 'L0_attn_bo': _L0_attn_in['bo'], 'L0_xattn_Wq': _L0_xattn_in['Wq'], 'L0_xattn_bq': _L0_xattn_in['bq'], 'L0_xattn_Wk': _L0_xattn_in['Wk'], 'L0_xattn_bk': _L0_xattn_in['bk'], 'L0_xattn_Wv': _L0_xattn_in['Wv'], 'L0_xattn_bv': _L0_xattn_in['bv'], 'L0_xattn_Wo': _L0_xattn_in['Wo'], 'L0_xattn_bo': _L0_xattn_in['bo'], 'L0_ffn_attention_mask': _L0_ffn_in['attention_mask'], 'L0_ffn_position_ids': _L0_ffn_in['position_ids'], 'L0_ffn_router_w': _L0_ffn_in['router_w'], 'L0_ffn_router_b': _L0_ffn_in['router_b'], 'L0_ffn_wq': _L0_ffn_in['wq'], 'L0_ffn_wk': _L0_ffn_in['wk'], 'L0_ffn_wv': _L0_ffn_in['wv'], 'L0_ffn_wo': _L0_ffn_in['wo'], 'L0_ffn_w1': _L0_ffn_in['w1'], 'L0_ffn_w2': _L0_ffn_in['w2'], 'L0_ffn_ln1': _L0_ffn_in['ln1'], 'L0_ffn_ln2': _L0_ffn_in['ln2']}

def reference(x, ctx_1024, L0_attn_Wq, L0_attn_bq, L0_attn_Wk, L0_attn_bk, L0_attn_Wv, L0_attn_bv, L0_attn_Wg, L0_attn_bg, L0_attn_Wo, L0_attn_bo, L0_xattn_Wq, L0_xattn_bq, L0_xattn_Wk, L0_xattn_bk, L0_xattn_Wv, L0_xattn_bv, L0_xattn_Wo, L0_xattn_bo, L0_ffn_attention_mask, L0_ffn_position_ids, L0_ffn_router_w, L0_ffn_router_b, L0_ffn_wq, L0_ffn_wk, L0_ffn_wv, L0_ffn_wo, L0_ffn_w1, L0_ffn_w2, L0_ffn_ln1, L0_ffn_ln2):
    import jax
    import jax.numpy as jnp

    def _L0_attn_ref(hidden_state, Wq, bq, Wk, bk, Wv, bv, Wg, bg, Wo, bo):
        import jax, jax.numpy as jnp
        import numpy as np

        def _gla_forward(hidden_state, Wq, bq, Wk, bk, Wv, bv, Wg, bg, Wo, bo):
            q = hidden_state @ Wq + bq
            k = jax.nn.sigmoid(hidden_state @ Wk + bk)
            g = jax.nn.sigmoid(hidden_state @ Wg + bg)
            v = hidden_state @ Wv + bv
            B = hidden_state.shape[0]
            K = Wq.shape[1]
            V = Wv.shape[1]
            state0 = jnp.zeros((B, K, V), dtype=hidden_state.dtype)

            def step(state, inp):
                q_t, k_t, g_t, v_t = inp
                state = state * g_t[:, :, None] + k_t[:, :, None] * v_t[:, None, :]
                out_t = jnp.einsum('bkv,bk->bv', state, q_t)
                return (state, out_t)
            xs = (jnp.swapaxes(q, 0, 1), jnp.swapaxes(k, 0, 1), jnp.swapaxes(g, 0, 1), jnp.swapaxes(v, 0, 1))
            final_state, outs = jax.lax.scan(step, state0, xs)
            out = jnp.swapaxes(outs, 0, 1)
            out = out @ Wo + bo
            return (out, final_state)

        def _reference_tuple_inner(hidden_state, Wq, bq, Wk, bk, Wv, bv, Wg, bg, Wo, bo):
            return _gla_forward(hidden_state, Wq, bq, Wk, bk, Wv, bv, Wg, bg, Wo, bo)
        return _reference_tuple_inner(hidden_state, Wq, bq, Wk, bk, Wv, bv, Wg, bg, Wo, bo)[0]

    def _L0_xattn_ref(queries, keys, values, Wq, bq, Wk, bk, Wv, bv, Wo, bo):
        import jax, jax.numpy as jnp
        import numpy as np
        D_MODEL = 256
        N_HEADS = 16
        HEAD_DIM = D_MODEL // N_HEADS
        SCALE = HEAD_DIM ** (-0.5)
        B, L, _ = queries.shape
        S = keys.shape[1]
        q = (queries @ Wq + bq).reshape(B, L, N_HEADS, HEAD_DIM).transpose(0, 2, 1, 3)
        k = (keys @ Wk + bk).reshape(B, S, N_HEADS, HEAD_DIM).transpose(0, 2, 1, 3)
        v = (values @ Wv + bv).reshape(B, S, N_HEADS, HEAD_DIM).transpose(0, 2, 1, 3)
        scores = jnp.einsum('bhld,bhsd->bhls', q, k) * SCALE
        weights = jax.nn.softmax(scores, axis=-1)
        out = jnp.einsum('bhls,bhsd->bhld', weights, v)
        out = out.transpose(0, 2, 1, 3).reshape(B, L, D_MODEL)
        out = out @ Wo + bo
        return out

    def _L0_ffn_ref(x, attention_mask, position_ids, router_w, router_b, wq, wk, wv, wo, w1, w2, ln1, ln2):
        import jax, jax.numpy as jnp
        import numpy as np
        B, S, D, H, F = (4, 1024, 256, 16, 1024)
        CAP = 0.125
        ROPE_BASE = 10000.0

        def rmsnorm(x, g):
            return x * jax.lax.rsqrt(jnp.mean(x * x, -1, keepdims=True) + 1e-06) * g

        def rope(t, pos):
            hd = t.shape[-1]
            inv = 1.0 / ROPE_BASE ** (jnp.arange(0, hd, 2, dtype=jnp.float32) / hd)
            f = pos[:, None, :, None].astype(jnp.float32) * inv
            emb = jnp.concatenate([f, f], axis=-1)
            cos, sin = (jnp.cos(emb), jnp.sin(emb))
            rot = jnp.concatenate([-t[..., hd // 2:], t[..., :hd // 2]], axis=-1)
            return t * cos + rot * sin
        b, s, d = x.shape
        hd = d // H
        weights = (x @ router_w)[..., 0] + router_b[0]
        k = int(CAP * s)
        topv, topi = jax.lax.top_k(weights, k)
        thr = topv[:, -1]
        sel_mask = (weights > thr[:, None]).astype(x.dtype)
        kc = k - 1
        sel_idx = jnp.sort(topi[:, :kc], axis=1)
        bidx = jnp.arange(b)[:, None]
        x_sel = x[bidx, sel_idx]
        pos_sel = position_ids[bidx, sel_idx]
        w_sel = weights[bidx, sel_idx]
        m = attention_mask[:, 0]
        m_sel = m[bidx[:, :, None], sel_idx[:, :, None], sel_idx[:, None, :]]
        hn = rmsnorm(x_sel, ln1)

        def heads(t):
            return t.reshape(b, kc, H, hd).transpose(0, 2, 1, 3)
        q = rope(heads(hn @ wq), pos_sel)
        kk = rope(heads(hn @ wk), pos_sel)
        v = heads(hn @ wv)
        sc = jnp.einsum('bhqd,bhkd->bhqk', q, kk) / np.sqrt(hd).astype(np.float32)
        sc = sc + m_sel[:, None]
        a = jax.nn.softmax(sc, axis=-1)
        o = jnp.einsum('bhqk,bhkd->bhqd', a, v).transpose(0, 2, 1, 3).reshape(b, kc, d) @ wo
        x1 = x_sel + o
        x2 = x1 + jax.nn.gelu(rmsnorm(x1, ln2) @ w1) @ w2
        proc = x2 * w_sel[..., None]
        out = jnp.zeros_like(x).at[bidx, sel_idx].set(proc)
        return out + x * (1.0 - sel_mask)[..., None]
    x = x + _L0_attn_ref(_layernorm(x, axis=-1), L0_attn_Wq, L0_attn_bq, L0_attn_Wk, L0_attn_bk, L0_attn_Wv, L0_attn_bv, L0_attn_Wg, L0_attn_bg, L0_attn_Wo, L0_attn_bo)
    x = x + _L0_xattn_ref(_layernorm(x, axis=-1), ctx_1024, ctx_1024, L0_xattn_Wq, L0_xattn_bq, L0_xattn_Wk, L0_xattn_bk, L0_xattn_Wv, L0_xattn_bv, L0_xattn_Wo, L0_xattn_bo)
    x = x + _L0_ffn_ref(_layernorm(x, axis=-1), L0_ffn_attention_mask, L0_ffn_position_ids, L0_ffn_router_w, L0_ffn_router_b, L0_ffn_wq, L0_ffn_wk, L0_ffn_wv, L0_ffn_wo, L0_ffn_w1, L0_ffn_w2, L0_ffn_ln1, L0_ffn_ln2)
    return x

_drawn_inputs = setup_inputs


def setup_inputs(seed=0):
    import zlib

    import numpy as np

    out = dict(_drawn_inputs(seed))
    spreads = {'L0_xattn_bq': (0.0, 0.305),
     'L0_xattn_bk': (0.0, 0.8),
     'L0_xattn_bv': (0.0, 0.1),
     'L0_xattn_bo': (0.0, 0.1),
     'L0_ffn_ln1': (1.0, 0.6),
     'L0_ffn_ln2': (1.0, 0.6)}
    factors = {'L0_attn_bq': 8.0,
     'L0_attn_Wk': 3.568,
     'L0_attn_bk': 8.0,
     'L0_attn_bv': 4.767,
     'L0_attn_Wg': 5.358,
     'L0_attn_bg': 8.0,
     'L0_attn_bo': 2.866,
     'L0_ffn_wq': 8.0,
     'L0_ffn_wk': 8.0,
     'L0_ffn_wv': 8.0,
     'L0_ffn_wo': 8.0,
     'L0_ffn_w1': 5.407,
     'L0_ffn_w2': 5.271}
    for name, (base, spread) in spreads.items():
        noise = np.random.default_rng([zlib.crc32(name.encode()), seed]).standard_normal(out[name].shape)
        drawn = base * np.exp(spread * noise) if base else spread * noise
        out[name] = jnp.asarray(drawn.astype(out[name].dtype))
    for name, factor in factors.items():
        out[name] = (out[name] * factor).astype(out[name].dtype)
    return out
```

```python
from contextlib import ExitStack

import numpy as np
import concourse.bass as bass
from concourse import mybir

F32 = mybir.dt.float32
BF16 = mybir.dt.bfloat16
I32 = mybir.dt.int32
U32 = mybir.dt.uint32
ALU = mybir.AluOpType
ACT = mybir.ActivationFunctionType
AX = mybir.AxisListType

P = 128
D = 256
DC = D // P
KV = 64
LN_EPS = 1e-5


def need(eng, sem, value):
    if isinstance(value, int) and value <= 0:
        return
    eng.wait_ge(sem, value)


def run_units(eng, units, ahead, body):
    for u in range(2):
        body(u, u % 2, False)
    with eng.Fori(1, units // 2 - 1) as i:
        for parity in range(2):
            body(i * 2 + parity, parity, False)
    for u in range(units - 2, units):
        body(u, u % 2, u + ahead >= units)


def run_skewed(eng, units, lead, tail, body):
    known = lambda i: lambda k: 0 <= i + k < units
    first = 2
    end = units - tail - tail % 2
    for i in range(-lead, first):
        body(i, i % 2, known(i))
    with eng.Fori(first // 2, end // 2) as turn:
        for parity in range(2):
            body(turn * 2 + parity, parity, lambda k: True)
    for i in range(end, units + 1):
        body(i, i % 2, known(i))


def settle(eng, tally):
    eng.sem_inc(tally, 1)


class Chain:

    def __init__(self, eng, sem, base, value=0):
        self.eng, self.sem, self.base, self.n = eng, sem, base, value

    def step(self, instruction):
        instruction.then_inc(self.sem, 1)
        self.n += 1
        return self.n

    def after(self, n):
        self.eng.wait_ge(self.sem, self.base + n)

    def link(self, instruction):
        self.after(self.step(instruction))


def gla_phase(nc, units, hbm, x_all, ident):
    with ExitStack() as ctx:
        sb = lambda name, shape, dt=F32: ctx.enter_context(nc.sbuf_tensor(name, shape, dt))
        ps = lambda name, shape, dt=F32: ctx.enter_context(nc.psum_tensor(name, shape, dt))
        sem = lambda name: ctx.enter_context(nc.semaphore(name))

        w_qkg = sb("g_w_qkg", [P, 3, DC, KV])
        w_v = sb("g_w_v", [P, DC, KV])
        w_o = sb("g_w_o", [KV + 1, D])
        b_qkg = sb("g_b_qkg", [P, 3])
        nb_kg = sb("g_nb_kg", [P, 2])
        b_v = sb("g_b_v", [P, 2, KV])
        mask_far = sb("g_mask_far", [P, P])
        mask_near = sb("g_mask_near", [P, 5, P], I32)
        mhalf = sb("g_mhalf", [P, 2])
        stats = sb("g_stats", [P, 2, 6])
        mv = sb("g_mv", [P, 2, 2, 2])
        vare = sb("g_vare", [P, 2, 2])
        rstd = sb("g_rstd", [P, 2, 2])
        hn = sb("g_hn", [P, 2, 2, D])
        hT = sb("g_hT", [P, 2, DC, 2, P])
        ekg = sb("g_ekg", [P, 2, 2 * P])
        XW = 4 * P + 6 * 2 * P
        X = sb("g_X", [P, 2, XW])
        EB = [P // h for h in (1, 2, 4, 8, 16, 32)]
        blk = {h: sb(f"g_blk{h}", [P, 2, P // h]) for h in (2, 4, 8, 16, 32)}
        fac = {h: sb(f"g_fac{h}", [P, 2, 2 * (P // h)]) for h in (1, 2, 4, 8, 16, 32)}
        A = sb("g_A", [P, 2, 2, P])
        v = sb("g_v", [P, 2, 2, KV])
        oT = sb("g_oT", [KV + 1, 2, 2, P])

        psT = ps("g_psT", [P, 512])
        psP = ps("g_psP", [P, 512])
        psL = ps("g_psL", [P, 2, 2, 512])
        psO = ps("g_psO", [P, 512])
        psW = ps("g_psW", [P, 512])

        x_dma = [sem("g_x_even"), sem("g_x_odd")]
        w_dma = sem("g_w_dma")
        dve_tally = sem("g_dve_tally")
        pool_tally = sem("g_pool_tally")
        setup_v = sem("g_setup_v")
        setup_a = sem("g_setup_a")
        setup_p = sem("g_setup_p")
        vare_done = sem("g_vare_done")
        bn_done = sem("g_bn_done")
        exp_plus_one = sem("g_exp_plus_one")
        level_done = sem("g_level_done")
        mask_step = sem("g_mask_step")
        product_done = sem("g_product_done")
        qg_done = sem("g_qg_done")
        stats_done = sem("g_stats_done")
        rstd_done = sem("g_rstd_done")
        hn_done = sem("g_hn_done")
        hT_ps = sem("g_hT_ps")
        hT_done = sem("g_hT_done")
        proj_ps = sem("g_proj_ps")
        kg_exp = sem("g_kg_exp")
        q_done = sem("g_q_done")
        gates_done = sem("g_gates_done")
        blk_done = sem("g_blk_done")
        v_done = sem("g_v_done")
        X_done = sem("g_X_done")
        L_ps = sem("g_L_ps")
        A_done = sem("g_A_done")
        O_ps = sem("g_O_ps")
        oT_done = sem("g_oT_done")
        W_ps = sem("g_W_ps")
        x1_done = sem("g_x1_done")

        def load_consts(sp):
            for dst, src in (
                (w_qkg[:, 0], hbm["L0_attn_Wq"]), (w_qkg[:, 1], hbm["L0_attn_Wk"]),
                (w_qkg[:, 2], hbm["L0_attn_Wg"]), (w_v[:], hbm["L0_attn_Wv"]),
            ):
                sp.dma_start(dst, src.rearrange("(c p) n -> p c n", p=P)).then_inc(w_dma, 16)
            sp.dma_start(w_o[0:KV, :], hbm["L0_attn_Wo"]).then_inc(w_dma, 16)
            sp.dma_start(w_o[KV:KV + 1, :], hbm["L0_attn_bo"].rearrange("(a n) -> a n", a=1)).then_inc(w_dma, 16)
            sp.dma_start(b_qkg[:], hbm["attn_bias_cols"]).then_inc(w_dma, 16)
            for r in range(2):
                sp.dma_start(b_v[:, r, :], hbm["L0_attn_bv"].partition_broadcast(P)).then_inc(w_dma, 16)
            sp.dma_start(mask_far[:], hbm["mask_far"]).then_inc(w_dma, 16)
            sp.dma_start(mask_near[:], hbm["mask_near"]).then_inc(w_dma, 16)
            sp.dma_start(ident[:], hbm["ident"]).then_inc(w_dma, 16)
        NW = 12 * 16

        block = ctx.enter_context(nc.Block())

        @block.sync
        def _(sp):
            x_src = hbm["x"].rearrange("b t d -> t b d")

            def body(u, parity, last):
                need(sp, x_dma[parity], (u - parity) * 8)
                sp.dma_start(x_all[:, bass.ds(u * 2, 2), :], x_src[:, bass.ds(u * 2, 2), :]).then_inc(x_dma[parity], 16)
                if isinstance(u, int) and u == 0:
                    load_consts(sp)
            run_units(sp, units, 0, body)

        LEAD, TAIL = 4, 4

        @block.gpsimd
        def _(eng):
            eng.memset(mhalf[:], -0.5).then_inc(setup_p, 1)
            eng.wait_ge(setup_p, 1)
            eng.wait_ge(setup_v, 3)

            def rstd_of(u, parity):
                eng.wait_ge(stats_done, u + 1)
                need(eng, hn_done, u - 1)
                settle(eng, pool_tally)
                eng.tensor_scalar(vare[:, parity, :], mv[:, parity, :, 1], 1.0, LN_EPS, ALU.mult, ALU.add).then_inc(vare_done, 1)
                eng.wait_ge(vare_done, u + 1)
                eng.tensor_tensor(rstd[:, parity, :], vare[:, parity, :], mhalf[:], ALU.pow).then_inc(rstd_done, 1)

            def blocks_of(u, parity):
                eng.wait_ge(gates_done, u + 1)
                need(eng, X_done, u - 1)
                E = X[:, parity, 2 * P:3 * P]
                for k, h in enumerate((1, 2, 4, 8, 16, 32)):
                    nb = P // h
                    dst = fac[h][:, parity, 1:2 * nb - 1].rearrange("p (i r) -> p i r", i=2)[:, :, 0:nb - 1:2]
                    if h < 32:
                        E2 = blk[2 * h][:, parity, :]
                        eng.tensor_tensor(E2, E[:, 0:nb:2], E[:, 1:nb:2], ALU.mult).then_inc(product_done, 1)
                    settle(eng, pool_tally)
                    eng.tensor_scalar(dst, E.rearrange("p (j i) -> p i j", i=2), 1.0, 0.0, ALU.mult, ALU.add).then_inc(blk_done, 1)
                    if h < 32:
                        eng.wait_ge(product_done, u * 5 + k + 1)
                        E = E2

            def body(i, parity, on):
                if on(1):
                    blocks_of(i + 1, 1 - parity)
                if on(4):
                    rstd_of(i + 4, parity)
            run_skewed(eng, units, LEAD, TAIL, body)

        @block.scalar
        def _(eng):
            eng.wait_ge(w_dma, NW)
            eng.activation(nb_kg[:], b_qkg[:, 1:3], ACT.Copy, scale=-1.0).then_inc(setup_a, 1)
            eng.wait_ge(setup_a, 1)

            def gates_of(u, parity):
                eng.wait_ge(proj_ps, u + 1)
                need(eng, gates_done, u - 1)
                eng.activation(ekg[:, parity, 0:P], psP[:, P:2 * P], ACT.Exp, bias=nb_kg[:, 0:1], scale=-1.0)
                eng.activation(ekg[:, parity, P:2 * P], psP[:, 2 * P:3 * P], ACT.Exp, bias=nb_kg[:, 1:2], scale=-1.0).then_inc(kg_exp, 1)
                need(eng, L_ps, u - 1)
                eng.activation(X[:, parity, 3 * P:4 * P], psP[:, 0:P], ACT.Identity, bias=b_qkg[:, 0:1]).then_inc(q_done, 1)

            def hT_of(u, parity):
                eng.wait_ge(hT_ps, u + 1)
                need(eng, proj_ps, u - 1)
                eng.activation(hT[:, parity], psT[:].rearrange("p (c b t) -> p c b t", c=DC, b=2), ACT.Copy).then_inc(hT_done, 1)

            def outputs_of(u, parity):
                eng.wait_ge(O_ps, u + 1)
                need(eng, W_ps, u - 1)
                eng.activation(oT[0:KV, parity], psO[0:KV, 0:2 * P].rearrange("p (b t) -> p b t", b=2), ACT.Copy).then_inc(oT_done, 1)

            def body(i, parity, on):
                if on(2):
                    gates_of(i + 2, parity)
                if on(3):
                    hT_of(i + 3, 1 - parity)
                if on(0):
                    outputs_of(i, parity)
            run_skewed(eng, units, LEAD, TAIL, body)

        @block.vector
        def _(eng):
            for h in (1, 2, 4, 8, 16, 32):
                last = eng.memset(fac[h][:], 1.0)
                if h in (8, 32):
                    last.then_inc(setup_v, 1)
            eng.memset(oT[KV:KV + 1], 1.0).then_inc(setup_v, 1)
            eng.wait_ge(w_dma, NW)

            def v_of(u, parity):
                eng.wait_ge(q_done, u + 1)
                need(eng, O_ps, u - 1)
                eng.tensor_tensor(v[:, parity], psP[:, 3 * P:4 * P].rearrange("p (b n) -> p b n", b=2), b_v[:], ALU.add).then_inc(v_done, 1)

            def gate_sum_of(u, parity):
                eng.wait_ge(kg_exp, u + 1)
                eng.tensor_scalar(ekg[:, parity, :], ekg[:, parity, :], 1.0, None, ALU.add).then_inc(exp_plus_one, 1)

            def gates_of(u, parity):
                need(eng, L_ps, u - 1)
                need(eng, blk_done, 6 * (u - 1))
                eng.wait_ge(exp_plus_one, u + 1)
                eng.reciprocal(X[:, parity, P:3 * P], ekg[:, parity, :]).then_inc(gates_done, 1)

            def gated_query_of(u, parity):
                eng.wait_ge(gates_done, u + 1)
                eng.wait_ge(q_done, u + 1)
                eng.tensor_tensor(X[:, parity, 0:P], X[:, parity, 3 * P:4 * P], X[:, parity, 2 * P:3 * P], ALU.mult).then_inc(qg_done, 1)

            def level_of(u, parity, k):
                h = 1 << k
                nb = P // h
                src, dst = 4 * P + (k - 1) * 2 * P if k else 0, 4 * P + k * 2 * P
                eng.wait_ge(blk_done, u * 6 + k + 1)
                if k:
                    eng.wait_ge(level_done, u * 5 + k)
                else:
                    eng.wait_ge(qg_done, u + 1)
                lo, hi = (0, 2 * nb) if h < 32 else (nb // 2, nb + nb // 2)
                a = X[:, parity, src + lo * h:src + hi * h].rearrange("p (n h) -> p n h", h=h)
                o = X[:, parity, dst + lo * h:dst + hi * h].rearrange("p (n h) -> p n h", h=h)
                f = fac[h][:, parity, lo:hi].unsqueeze(2).broadcast_to([P, hi - lo, h])
                eng.tensor_tensor(o, a, f, ALU.mult).then_inc(level_done if k < 5 else X_done, 1)

            def stats_of(u, parity, load_parity):
                eng.wait_ge(x_dma[load_parity], (u - load_parity) * 8 + 16)
                need(eng, stats_done, u)
                settle(eng, dve_tally)
                for r in range(2):
                    last = eng.bn_stats(stats[:, r, :], x_all[:, u * 2 + r, :])
                last.then_inc(bn_done, 1)

            def mean_of(u, parity):
                eng.wait_ge(bn_done, u + 1)
                need(eng, hn_done, u - 1)
                settle(eng, dve_tally)
                for r in range(2):
                    last = eng.bn_aggr(mv[:, parity, r, :], stats[:, r, :])
                last.then_inc(stats_done, 1)

            def norm_of(u, parity):
                need(eng, hT_ps, u - 1)
                eng.wait_ge(stats_done, u + 1)
                eng.wait_ge(rstd_done, u + 1)
                for r in range(2):
                    last = eng.tensor_scalar(hn[:, parity, r, :], x_all[:, u * 2 + r, :], mv[:, parity, r, 0:1],
                                             rstd[:, parity, r:r + 1], ALU.subtract, ALU.mult)
                last.then_inc(hn_done, 1)

            def mask_of(u, parity, k):
                out = A[:, parity]
                if k == 0:
                    eng.wait_ge(L_ps, u + 1)
                    need(eng, O_ps, u - 1)
                    eng.tensor_tensor(out, psL[:, :, 0, 0:P], mask_far[:].unsqueeze(1).broadcast_to([P, 2, P]), ALU.mult).then_inc(mask_step, 1)
                    return
                tile = psL[:, :, 0, k * P:(k + 1) * P] if k < 4 else psL[:, :, 1, (k - 4) * P:(k - 3) * P]
                eng.wait_ge(mask_step, u * 5 + k)
                settle(eng, dve_tally)
                eng.copy_predicated(out, mask_near[:, k - 1, :].unsqueeze(1).broadcast_to([P, 2, P]), tile).then_inc(mask_step if k < 5 else A_done, 1)

            def residual_of(u):
                eng.wait_ge(W_ps, u + 1)
                eng.tensor_tensor(x_all[:, bass.ds(u * 2, 2), :], psW[:].rearrange("p (b d) -> p b d", b=2),
                                  x_all[:, bass.ds(u * 2, 2), :], ALU.add).then_inc(x1_done, 1)

            def body(i, parity, on):
                other = 1 - parity
                if on(1):
                    gate_sum_of(i + 1, other)
                    v_of(i + 1, other)
                    gates_of(i + 1, other)
                if on(4):
                    stats_of(i + 4, parity, parity)
                if on(1):
                    gated_query_of(i + 1, other)
                if on(4):
                    mean_of(i + 4, parity)
                if on(3):
                    norm_of(i + 3, other)
                for k in range(6):
                    if on(0):
                        mask_of(i, parity, k)
                    if on(1):
                        level_of(i + 1, other, k)
                if on(-1):
                    residual_of(i - 1)
            run_skewed(eng, units, LEAD, TAIL, body)

        @block.tensor
        def _(eng):
            eng.wait_ge(w_dma, NW)
            eng.wait_ge(setup_v, 3)

            def transposes(u, parity):
                eng.wait_ge(hn_done, u + 1)
                need(eng, hT_done, u)
                for ch in range(DC):
                    for r in range(2):
                        last = eng.transpose(psT[:, (ch * 2 + r) * P:(ch * 2 + r + 1) * P],
                                             hn[:, parity, r, ch * P:(ch + 1) * P], ident[:])
                last.then_inc(hT_ps, 1)

            def project(u, parity):
                eng.wait_ge(hT_done, u + 1)
                need(eng, kg_exp, u)
                need(eng, q_done, u)
                need(eng, v_done, u)
                for r in range(2):
                    for f in range(3):
                        for ch in range(DC):
                            eng.matmul(psP[r * KV:(r + 1) * KV, f * P:(f + 1) * P], w_qkg[:, f, ch, :],
                                       hT[:, parity, ch, r, :], start=ch == 0, stop=ch == DC - 1)
                for r in range(2):
                    for ch in range(DC):
                        last = eng.matmul(psP[:, 3 * P + r * KV:3 * P + (r + 1) * KV], hT[:, parity, ch, r, :],
                                          w_v[:, ch, :], start=ch == 0, stop=ch == DC - 1)
                last.then_inc(proj_ps, 1)

            def levels(u, parity):
                eng.wait_ge(X_done, u + 1)
                need(eng, A_done, u)
                far = 4 * P + 3 * 2 * P

                def pair(r, query, key, s, t, out):
                    rows = slice(r * KV, (r + 1) * KV)
                    return eng.matmul(out[s, t], X[rows, parity, key + s.start:key + s.stop],
                                      X[rows, parity, query + t.start:query + t.stop], start=True, stop=True)
                every = slice(0, P)
                for k, base in enumerate((far, 4 * P + 2 * 2 * P, 4 * P + 2 * P, 4 * P)):
                    for r in range(2):
                        pair(r, base, base + P, every, every, psL[:, r, 0, k * P:(k + 1) * P])
                for k, (query, key) in enumerate(((0, P), (3 * P, P))):
                    for r in range(2):
                        pair(r, query, key, every, every, psL[:, r, 1, k * P:(k + 1) * P])
                for r in range(2):
                    base = far + 2 * P
                    pair(r, base, base + P, slice(0, 32), slice(32, 64), psL[:, r, 0, 0:P])
                    pair(r, base, base + P, slice(64, 96), slice(96, 128), psL[:, r, 0, 0:P])
                    last = pair(r, base + 2 * P, base + 3 * P, slice(0, 64), slice(64, 128), psL[:, r, 0, 0:P])
                last.then_inc(L_ps, 1)

            def weighted(u, parity):
                eng.wait_ge(A_done, u + 1)
                eng.wait_ge(v_done, u + 1)
                need(eng, oT_done, u)
                for r in range(2):
                    last = eng.matmul(psO[0:KV, r * P:(r + 1) * P], v[:, parity, r, :], A[:, parity, r, :], start=True, stop=True)
                last.then_inc(O_ps, 1)

            def project_out(u, parity):
                eng.wait_ge(oT_done, u + 1)
                need(eng, x1_done, u)
                for r in range(2):
                    last = eng.matmul(psW[:, r * D:(r + 1) * D], oT[:, parity, r, :], w_o[:], start=True, stop=True)
                last.then_inc(W_ps, 1)

            def body(i, parity, on):
                if on(0):
                    levels(i, parity)
                if on(-1):
                    project_out(i - 1, 1 - parity)
                if on(2):
                    project(i + 2, parity)
                if on(3):
                    transposes(i + 3, 1 - parity)
                if on(0):
                    weighted(i, parity)
            run_skewed(eng, units, LEAD, TAIL, body)


HEADS = 16
HD = D // HEADS
VW = HD + 1


def xattn_phase(nc, units, hbm, x_all, ident, ln3_mv, ln3_dot):
    with ExitStack() as ctx:
        sb = lambda name, shape, dt=F32: ctx.enter_context(nc.sbuf_tensor(name, shape, dt))
        ps = lambda name, shape, dt=F32: ctx.enter_context(nc.psum_tensor(name, shape, dt))
        sem = lambda name: ctx.enter_context(nc.semaphore(name))

        w_q = sb("a_w_q", [P, DC, D])
        w_k = sb("a_w_k", [P, DC, D])
        w_v = sb("a_w_v", [P, DC, D])
        w_o = sb("a_w_o", [P, DC, D])
        b_cols = sb("a_b_cols", [P, 2, DC])
        odd_scale = sb("a_odd_scale", [P, 2])
        qb_cols = sb("a_qb_cols", [P, 2, DC])
        b_v = sb("a_b_v", [P, 2, D])
        b_o = sb("a_b_o", [P, 2, D])
        router = sb("a_router", [P, 2, D])
        ident_bf = sb("a_ident_bf", [P, P], BF16)
        mhalf = sb("a_mhalf", [P, 2])

        ctx_in = sb("a_ctx", [P, 2, 2, D])
        stats = sb("a_stats", [P, 2, 6])
        mv = sb("a_mv", [P, 2, 2])
        vare = sb("a_vare", [P, 2])
        rstd = sb("a_rstd", [P, 2])
        hn = sb("a_hn", [P, 2, D])
        hT = sb("a_hT", [P, DC, 2, P])
        cT = sb("a_cT", [P, DC, 2, P])
        qz = sb("a_qz", [P, 2, 2, DC, 2, P])
        kT = sb("a_kT", [P, 2, DC, 2, P])
        qz_bf = sb("a_qz_bf", [P, 2, 2, DC, 2, P], BF16)
        k_bf = sb("a_k_bf", [P, 2, DC, 2, P], BF16)
        vx = sb("a_vx", [P, 2, 2, HEADS, VW])
        nmax = sb("a_nmax", [P, 2, 4], BF16)
        pT = sb("a_pT", [P, 2, 4, P])
        rden = sb("a_rden", [P, HEADS])
        on = sb("a_on", [P, 2, HEADS, HD])
        oT = sb("a_oT", [P, 2, DC, P])
        stats3 = sb("a_stats3", [P, 2, 6])
        mv3 = sb("a_mv3", [P, 2, 2])
        prod = sb("a_prod", [P, 2, D])

        psA = ps("a_psA", [P, 512])
        psB = ps("a_psB", [P, 512])
        psC = ps("a_psC", [P, 512])
        psM = [ps(f"a_psM{i}", [P, 512]) for i in range(2)]
        psE = [ps(f"a_psE{i}", [P, 512]) for i in range(2)]
        psO = ps("a_psO", [P, 512])

        ctx_dma = [sem("a_ctx_even"), sem("a_ctx_odd")]
        w_dma = sem("a_w_dma")
        dve_tally = sem("a_dve_tally")
        pool_tally = sem("a_pool_tally")
        setup_v = sem("a_setup_v")
        dve = sem("a_dve")
        pool = sem("a_pool")
        stats_done = sem("a_stats_done")
        rstd_done = sem("a_rstd_done")
        hn_done = sem("a_hn_done")
        bo_done = sem("a_bo_done")
        hT_ps = sem("a_hT_ps")
        cT_ps = sem("a_cT_ps")
        hT_done = sem("a_hT_done")
        cT_done = sem("a_cT_done")
        q_ps = sem("a_q_ps")
        k_ps = sem("a_k_ps")
        v_ps = sem("a_v_ps")
        q_done = sem("a_q_done")
        k_done = sem("a_k_done")
        v_done = sem("a_v_done")
        qk_bf_done = sem("a_qk_bf_done")
        max_ps = sem("a_max_ps")
        nmax_done = sem("a_nmax_done")
        score_ps = sem("a_score_ps")
        p_done = sem("a_p_done")
        pv_ps = sem("a_pv_ps")
        on_done = sem("a_on_done")
        oT_ps = sem("a_oT_ps")
        oT_done = sem("a_oT_done")
        wo_ps = sem("a_wo_ps")
        x2_done = sem("a_x2_done")
        prod_done = sem("a_prod_done")
        dot_done = sem("a_dot_done")

        NW = 13 * 16
        block = ctx.enter_context(nc.Block())

        @block.sync
        def _(sp):
            for dst, name in ((w_q, "Wq"), (w_k, "Wk"), (w_v, "Wv"), (w_o, "Wo")):
                sp.dma_start(dst[:], hbm["L0_xattn_" + name].rearrange("(c p) n -> p c n", p=P)).then_inc(w_dma, 16)
            sp.dma_start(b_cols[:], hbm["xattn_bias_cols"]).then_inc(w_dma, 16)
            sp.dma_start(odd_scale[:], hbm["odd_scale"]).then_inc(w_dma, 16)
            sp.dma_start(mhalf[:], hbm["mhalf"]).then_inc(w_dma, 16)
            for r in range(2):
                sp.dma_start(b_v[:, r, :], hbm["L0_xattn_bv"].partition_broadcast(P)).then_inc(w_dma, 16)
                sp.dma_start(b_o[:, r, :], hbm["L0_xattn_bo"].partition_broadcast(P)).then_inc(w_dma, 16)
                sp.dma_start(router[:, r, :], hbm["router"].partition_broadcast(P)).then_inc(w_dma, 16)
            c_src = hbm["ctx_1024"].rearrange("b t d -> t b d")

            def body(u, parity, last):
                need(sp, cT_ps, u - 1)
                sp.dma_start(ctx_in[:, parity], c_src[:, bass.ds(u * 2, 2), :]).then_inc(ctx_dma[parity], 16)
            run_units(sp, units, 0, body)

        @block.gpsimd
        def _(eng):
            eng.wait_ge(w_dma, NW)
            c = Chain(eng, pool, 0)

            def rstd_of(u):
                eng.wait_ge(stats_done, u + 1)
                settle(eng, pool_tally)
                c.link(eng.tensor_scalar(vare[:], mv[:, :, 1], 1.0, LN_EPS, ALU.mult, ALU.add))
                eng.tensor_tensor(rstd[:], vare[:], mhalf[:], ALU.pow).then_inc(rstd_done, 1)

            def narrow(u, parity):
                eng.wait_ge(hn_done, u + 1)
                rows = x_all[:, bass.ds(u * 2, 2), :]
                eng.tensor_tensor(rows, rows, b_o[:], ALU.add).then_inc(bo_done, 1)
                need(eng, max_ps, 8 * (u - 1))
                eng.wait_ge(q_done, u + 1)
                settle(eng, pool_tally)
                eng.tensor_scalar(qz_bf[:, parity], qz[:, parity], 1.0, 0.0, ALU.mult, ALU.add)
                eng.wait_ge(k_done, u + 1)
                settle(eng, pool_tally)
                eng.tensor_scalar(k_bf[:, parity], kT[:, parity], 1.0, 0.0, ALU.mult, ALU.add).then_inc(qk_bf_done, 1)

            def route(u):
                eng.wait_ge(x2_done, 2 * u + 2)
                need(eng, dot_done, u)
                eng.tensor_tensor(prod[:], x_all[:, bass.ds(u * 2, 2), :], router[:], ALU.mult).then_inc(prod_done, 1)

            rstd_of(0)
            narrow(0, 0)

            def body(u, parity, last):
                c.base, c.n = u, 1
                if not last:
                    rstd_of(u + 1)
                if not (isinstance(u, int) and u == 0):
                    route(u - 1)
                if not last:
                    narrow(u + 1, 1 - parity)
            run_units(eng, units, 1, body)
            route(units - 1)

        @block.scalar
        def _(eng):
            eng.wait_ge(setup_v, 1)

            def turned(u):
                eng.wait_ge(hT_ps, u + 1)
                need(eng, q_ps, u)
                eng.activation(hT[:], psA[:].rearrange("p (c b t) -> p c b t", c=DC, b=2), ACT.Copy).then_inc(hT_done, 1)
                eng.wait_ge(cT_ps, u + 1)
                need(eng, v_ps, u)
                eng.activation(cT[:], psB[:].rearrange("p (c b t) -> p c b t", c=DC, b=2), ACT.Copy).then_inc(cT_done, 1)

            def queries(u, parity):
                eng.wait_ge(q_ps, u + 1)
                need(eng, score_ps, 8 * (u - 1))
                need(eng, qk_bf_done, u - 1)
                for odd in range(2):
                    for ch in range(DC):
                        last = eng.activation(qz[:, parity, odd, ch], psC[:, ch * 2 * P:(ch + 1) * 2 * P].rearrange("p (b t) -> p b t", b=2),
                                              ACT.Identity, bias=qb_cols[:, odd, ch:ch + 1], scale=odd_scale[:, odd:odd + 1])
                last.then_inc(q_done, 1)

            def keys(u, parity):
                eng.wait_ge(k_ps, u + 1)
                need(eng, score_ps, 8 * (u - 1))
                need(eng, qk_bf_done, u - 1)
                for ch in range(DC):
                    last = eng.activation(kT[:, parity, ch], psA[:, ch * 2 * P:(ch + 1) * 2 * P].rearrange("p (b t) -> p b t", b=2),
                                          ACT.Identity, bias=b_cols[:, 1, ch:ch + 1])
                last.then_inc(k_done, 1)

            def weights(u, j):
                eng.wait_ge(score_ps, u * 8 + j + 1)
                need(eng, pv_ps, u * 8 + j - 1)
                eng.activation(pT[:, j % 2], psE[j % 2][:].rearrange("p (k t) -> p k t", k=4), ACT.Exp).then_inc(p_done, 1)

            def out_turned(u, r):
                eng.wait_ge(oT_ps, u * 2 + r + 1)
                need(eng, wo_ps, u * 2 + r - 1)
                eng.activation(oT[:, r], psC[:, 0:2 * P].rearrange("p (c t) -> p c t", c=DC), ACT.Copy).then_inc(oT_done, 1)

            turned(0)
            queries(0, 0)
            keys(0, 0)

            def body(u, parity, last):
                first = isinstance(u, int) and u == 0
                for j in range(8):
                    weights(u, j)
                    if j == 1 and not first:
                        out_turned(u - 1, 1)
                    if j == 2 and not last:
                        turned(u + 1)
                    if j == 3 and not last:
                        queries(u + 1, 1 - parity)
                    if j == 4 and not last:
                        keys(u + 1, 1 - parity)
                    if j == 5:
                        out_turned(u, 0)
            run_units(eng, units, 1, body)
            out_turned(units - 1, 1)

        @block.vector
        def _(eng):
            eng.wait_ge(w_dma, NW)
            for odd in range(2):
                eng.tensor_scalar(qb_cols[:, odd, :], b_cols[:, 0, :], odd_scale[:, odd:odd + 1], None, ALU.mult)
            eng.tensor_copy(ident_bf[:], ident[:])
            eng.memset(vx[:], 1.0).then_inc(setup_v, 1)
            eng.wait_ge(setup_v, 1)
            c = Chain(eng, dve, 0)

            def norm_of(u):
                settle(eng, dve_tally)
                for r in range(2):
                    n = c.step(eng.bn_stats(stats[:, r, :], x_all[:, u * 2 + r, :]))
                c.after(n)
                settle(eng, dve_tally)
                for r in range(2):
                    last = eng.bn_aggr(mv[:, r, :], stats[:, r, :])
                last.then_inc(stats_done, 1)
                eng.wait_ge(stats_done, u + 1)
                need(eng, hT_ps, u)
                eng.wait_ge(rstd_done, u + 1)
                for r in range(2):
                    last = eng.tensor_scalar(hn[:, r, :], x_all[:, u * 2 + r, :], mv[:, r, 0:1],
                                             rstd[:, r:r + 1], ALU.subtract, ALU.mult)
                last.then_inc(hn_done, 1)

            def maxima(u, j):
                eng.wait_ge(max_ps, u * 8 + j + 1)
                need(eng, score_ps, u * 8 + j - 1)
                eng.tensor_reduce(nmax[:, j % 2, :], psM[j % 2][:].rearrange("p (k s) -> p k s", k=4), AX.X, ALU.max,
                                  negate=True).then_inc(nmax_done, 1)

            def values(u, parity):
                eng.wait_ge(v_ps, u + 1)
                need(eng, pv_ps, 8 * (u - 1))
                for r in range(2):
                    last = eng.tensor_tensor(vx[:, parity, r, :, 0:HD], psB[:, r * D:(r + 1) * D].rearrange("p (h i) -> p h i", h=HEADS),
                                             b_v[:, r, :].rearrange("p (h i) -> p h i", h=HEADS), ALU.add)
                last.then_inc(v_done, 1)

            def normalise(u, r):
                eng.wait_ge(pv_ps, u * 8 + 4 * r + 4)
                need(eng, oT_ps, u * 2 + r - 1)
                out = psO[:, 0:HEADS * VW].rearrange("p (h i) -> p h i", h=HEADS)
                c.link(eng.reciprocal(rden[:], out[:, :, HD]))
                eng.tensor_tensor(on[:, r], out[:, :, 0:HD], rden[:].unsqueeze(2).broadcast_to([P, HEADS, HD]), ALU.mult).then_inc(on_done, 1)

            def residual(u, r):
                eng.wait_ge(wo_ps, u * 2 + r + 1)
                eng.wait_ge(bo_done, u + 1)
                row = x_all[:, u * 2 + r, :]
                eng.tensor_tensor(row, psC[:, 2 * P:4 * P], row, ALU.add).then_inc(x2_done, 1)

            def look_ahead(u):
                eng.wait_ge(x2_done, u * 2 + 2)
                settle(eng, dve_tally)
                for r in range(2):
                    n = c.step(eng.bn_stats(stats3[:, r, :], x_all[:, u * 2 + r, :]))
                c.after(n)
                settle(eng, dve_tally)
                for r in range(2):
                    n = c.step(eng.bn_aggr(mv3[:, r, :], stats3[:, r, :]))
                c.after(n)
                c.link(eng.tensor_copy(ln3_mv[:, bass.ds(u * 2, 2), :], mv3[:]))
                eng.wait_ge(prod_done, u + 1)
                eng.tensor_reduce(ln3_dot[:, bass.ds(u * 2, 2)], prod[:], AX.X, ALU.add).then_inc(dot_done, 1)

            norm_of(0)
            values(0, 0)
            maxima(0, 0)
            counted = {}

            def body(u, parity, last):
                first = isinstance(u, int) and u == 0
                if not first:
                    c.base, c.n = (u - 1) * counted.get("turn", 0), counted["first"]
                start = c.n
                for j in range(8):
                    if j == 0 and not last:
                        norm_of(u + 1)
                    if j < 7:
                        maxima(u, j + 1)
                    elif not last:
                        maxima(u + 1, 0)
                    if j == 0 and not first:
                        normalise(u - 1, 1)
                    if j == 2 and not first:
                        residual(u - 1, 1)
                    if j == 3 and not first:
                        look_ahead(u - 1)
                    if j == 4:
                        normalise(u, 0)
                    if j == 5 and not last:
                        values(u + 1, 1 - parity)
                    if j == 6:
                        residual(u, 0)
                if first:
                    counted["first"] = c.n
                elif "turn" not in counted:
                    counted["turn"] = c.n - start
            run_units(eng, units, 1, body)
            normalise(units - 1, 1)
            residual(units - 1, 1)
            look_ahead(units - 1)

        @block.tensor
        def _(eng):
            eng.wait_ge(w_dma, NW)
            eng.wait_ge(setup_v, 1)

            def turn(u, parity):
                eng.wait_ge(hn_done, u + 1)
                need(eng, k_done, u)
                for ch in range(DC):
                    for r in range(2):
                        last = eng.transpose(psA[:, (ch * 2 + r) * P:(ch * 2 + r + 1) * P], hn[:, r, ch * P:(ch + 1) * P], ident[:])
                last.then_inc(hT_ps, 1)
                eng.wait_ge(ctx_dma[parity], (u - parity) * 8 + 16)
                need(eng, v_done, u)
                for ch in range(DC):
                    for r in range(2):
                        last = eng.transpose(psB[:, (ch * 2 + r) * P:(ch * 2 + r + 1) * P], ctx_in[:, parity, r, ch * P:(ch + 1) * P], ident[:])
                last.then_inc(cT_ps, 1)

            def features(out, w, src):
                for m in range(DC):
                    for ch in range(DC):
                        last = eng.matmul(out[:, m * 2 * P:(m + 1) * 2 * P], w[:, ch, m * P:(m + 1) * P], src[:, ch],
                                          start=ch == 0, stop=ch == DC - 1)
                return last

            def queries(u):
                eng.wait_ge(hT_done, u + 1)
                need(eng, x2_done, 2 * u - 2)
                features(psC, w_q, hT).then_inc(q_ps, 1)

            def keys(u):
                eng.wait_ge(cT_done, u + 1)
                eng.wait_ge(hT_done, u + 1)
                features(psA, w_k, cT).then_inc(k_ps, 1)

            def values(u):
                eng.wait_ge(cT_done, u + 1)
                for r in range(2):
                    for ch in range(DC):
                        last = eng.matmul(psB[:, r * D:(r + 1) * D], cT[:, ch, r, :], w_v[:, ch, :], start=ch == 0, stop=ch == DC - 1)
                last.then_inc(v_ps, 1)

            def rough_scores(u, parity, j):
                r, q = j // 4, j % 4
                rows = slice(32 * q, 32 * q + 32)
                eng.wait_ge(qk_bf_done, u + 1)
                need(eng, nmax_done, u * 8 + j - 1)
                for ch in range(DC):
                    for odd in range(2):
                        k = ch * 2 + odd
                        last = eng.matmul(psM[j % 2][:, k * P:(k + 1) * P], qz_bf[rows, parity, odd, ch, r, :], k_bf[rows, parity, ch, r, :],
                                          start=True, stop=True)
                last.then_inc(max_ps, 1)

            def scores(u, parity, j):
                r, q = j // 4, j % 4
                rows = slice(32 * q, 32 * q + 32)
                need(eng, p_done, u * 8 + j - 1)
                eng.wait_ge(nmax_done, u * 8 + j + 1)
                for k in range(4):
                    eng.matmul(psE[j % 2][:, k * P:(k + 1) * P], nmax[:, j % 2, k:k + 1].broadcast_to([P, P]), ident_bf[:],
                               start=k == 0, stop=False, skip_group_check=True)
                for ch in range(DC):
                    last = eng.matmul(psE[j % 2][:, ch * 2 * P:(ch + 1) * 2 * P], kT[rows, parity, ch, r, :], qz[rows, parity, :, ch, r, :],
                                      start=False, stop=True, skip_group_check=True)
                last.then_inc(score_ps, 1)

            def weigh(u, parity, j):
                r, q = j // 4, j % 4
                eng.wait_ge(p_done, u * 8 + j + 1)
                eng.wait_ge(v_done, u + 1)
                if q == 0:
                    need(eng, on_done, u * 2 + r)
                for ch in range(DC):
                    for odd in range(2):
                        h = 8 * ch + 2 * q + odd
                        last = eng.matmul(psO[:, h * VW:(h + 1) * VW], pT[:, j % 2, ch * 2 + odd, :], vx[:, parity, r, h, :], start=True, stop=True)
                last.then_inc(pv_ps, 1)

            def turn_out(u, r, next_unit):
                eng.wait_ge(on_done, u * 2 + r + 1)
                need(eng, x2_done, u * 2 + r)
                if next_unit:
                    eng.wait_ge(q_done, u + 2)
                o = on[:, r].rearrange("p h i -> p (h i)")
                for ch in range(DC):
                    last = eng.transpose(psC[:, ch * P:(ch + 1) * P], o[:, ch * P:(ch + 1) * P], ident[:])
                last.then_inc(oT_ps, 1)

            def project_out(u, r):
                eng.wait_ge(oT_done, u * 2 + r + 1)
                for ch in range(DC):
                    last = eng.matmul(psC[:, 2 * P:4 * P], oT[:, r, ch, :], w_o[:, ch, :], start=ch == 0, stop=ch == DC - 1)
                last.then_inc(wo_ps, 1)

            turn(0, 0)
            queries(0)
            keys(0)
            values(0)
            rough_scores(0, 0, 0)

            def body(u, parity, last):
                first = isinstance(u, int) and u == 0
                for j in range(8):
                    if j < 7:
                        rough_scores(u, parity, j + 1)
                    elif not last:
                        rough_scores(u + 1, 1 - parity, 0)
                    scores(u, parity, j)
                    if j >= 1:
                        weigh(u, parity, j - 1)
                    elif not first:
                        weigh(u - 1, 1 - parity, 7)
                    if j == 1 and not first:
                        turn_out(u - 1, 1, False)
                    if j == 2 and not first:
                        project_out(u - 1, 1)
                    if j == 2 and not last:
                        turn(u + 1, 1 - parity)
                    if j == 3 and not last:
                        queries(u + 1)
                    if j == 4 and not last:
                        keys(u + 1)
                    if j == 5:
                        turn_out(u, 0, not last)
                    if j == 5 and not last:
                        values(u + 1)
                    if j == 6:
                        project_out(u, 0)
            run_units(eng, units, 1, body)
            weigh(units - 1, (units - 1) % 2, 7)
            turn_out(units - 1, 1, False)
            project_out(units - 1, 1)


SLOTS = 16
ROWS_PER_TILE = P // SLOTS
FF = 1024
FC = FF // P
RMS_EPS = 1e-6
LOWEST = -3.0e38
MAGIC = 12582912.0
TWO_PI = (6.28125, 1.9350051879882812e-03, 3.019916050561733e-07)
PI = 3.1415925


def route_phase(nc, hbm, rows, out, ln3_mv, ln3_dot, ident, scratch_idx):
    tiles = rows // ROWS_PER_TILE
    with ExitStack() as ctx:
        sb = lambda name, shape, dt=F32: ctx.enter_context(nc.sbuf_tensor(name, shape, dt))
        ps = lambda name, shape, dt=F32: ctx.enter_context(nc.psum_tensor(name, shape, dt))
        sem = lambda name: ctx.enter_context(nc.semaphore(name))
        router = sb("r_router", [P, D])
        router_b = sb("r_router_b", [P, 1])
        mhalf = sb("r_mhalf", [P, rows])
        iota_p = sb("r_iota_p", [P, 1])
        own_slot = sb("r_own_slot", [P, ROWS_PER_TILE])
        pos_i = sb("r_pos_i", [P, 4], I32)
        pos_f = sb("r_pos_f", [P, 4])
        pos_own = sb("r_pos_own", [P, tiles, 4])
        inv_freq = sb("r_inv_freq", [P, HD // 2])
        rsum = sb("r_rsum", [P, 1])
        w_all = sb("r_w_all", [P, rows])
        wt = sb("r_wt", [P, P])
        wt2 = sb("r_wt2", [P, P])
        idx_u = sb("r_idx_u", [P, SLOTS], U32)
        idx_f = sb("r_idx_f", [P, SLOTS])
        top = sb("r_top", [P, SLOTS])
        keep = sb("r_keep", [P, P])
        idx_b = sb("r_idx_b", [P, rows * SLOTS])
        sel = sb("r_sel", [P, rows * SLOTS])
        idx_c = sb("r_idx_c", [P, tiles])
        pos_s = sb("r_pos_s", [P, tiles])
        turns = sb("r_turns", [P, tiles, HD // 2])
        over = sb("r_over", [P, tiles, HD // 2])
        ang = sb("r_ang", [P, 2, tiles, HD // 2])
        psW = ps("r_psW", [P, 512])
        psK = ps("r_psK", [P, 512])
        psP = ps("r_psP", [P, 512])
        w_dma = sem("r_w_dma")
        dve = sem("r_dve")
        var_done = sem("r_var_done")
        rstd_done = sem("r_rstd_done")
        w_done = sem("r_w_done")
        wt_ps = sem("r_wt_ps")
        top_done = sem("r_top_done")
        keep_ps = sem("r_keep_ps")
        scratch_out = sem("r_scratch_out")
        scratch_in = sem("r_scratch_in")
        sel_done = sem("r_sel_done")
        pos_ps = sem("r_pos_ps")
        ang_done = sem("r_ang_done")
        NW = 7 * 16
        block = ctx.enter_context(nc.Block())
        scratch_w = nc.dram_tensor("scratch_w", [rows * SLOTS], F32).ap()

        @block.sync
        def _(sp):
            sp.dma_start(router[:], hbm["router"].partition_broadcast(P)).then_inc(w_dma, 16)
            sp.dma_start(router_b[:], hbm["L0_ffn_router_b"].partition_broadcast(P)).then_inc(w_dma, 16)
            sp.dma_start(iota_p[:], hbm["iota_p"]).then_inc(w_dma, 16)
            sp.dma_start(own_slot[:], hbm["own_slot"]).then_inc(w_dma, 16)
            sp.dma_start(pos_i[:], hbm["positions"]).then_inc(w_dma, 16)
            sp.dma_start(pos_own[:], hbm["pos_own"]).then_inc(w_dma, 16)
            sp.dma_start(inv_freq[:], hbm["inv_freq"]).then_inc(w_dma, 16)
            sp.wait_ge(top_done, 1)
            sp.dma_start(scratch_idx.rearrange("(b r) -> b r", r=SLOTS), idx_f[:]).then_inc(scratch_out, 16)
            sp.dma_start(scratch_w.rearrange("(b r) -> b r", r=SLOTS), top[:]).then_inc(scratch_out, 16)
            sp.wait_ge(scratch_out, 32)
            sp.dma_start(idx_b[:], scratch_idx.partition_broadcast(P)).then_inc(scratch_in, 16)
            with nc.allow_non_contiguous_dma(reason="a slot on each partition"):
                sp.dma_start(idx_c[:], scratch_idx.rearrange("(i p) -> p i", p=P)).then_inc(scratch_in, 16)
                sp.dma_start(out["w_sel"][:], scratch_w.rearrange("(i p) -> p i", p=P)).then_inc(scratch_in, 16)

        @block.gpsimd
        def _(eng):
            eng.memset(mhalf[:], -0.5).then_inc(var_done, 1)
            eng.wait_ge(var_done, 2)
            eng.tensor_tensor(out["rstd"][:], out["rstd"][:], mhalf[:], ALU.pow).then_inc(rstd_done, 1)

        @block.tensor
        def _(eng):
            eng.wait_ge(w_done, 1)
            eng.transpose(psW[:, 0:P], w_all[:], ident[:]).then_inc(wt_ps, 1)
            eng.wait_ge(top_done, 2)
            eng.transpose(psK[:, 0:P], keep[:], ident[:]).then_inc(keep_ps, 1)
            eng.wait_ge(sel_done, 1)
            for i in range(tiles):
                last = eng.matmul(psP[:, i * 4:(i + 1) * 4], sel[:, i * P:(i + 1) * P], pos_f[:], start=True, stop=True)
            last.then_inc(pos_ps, 1)

        @block.scalar
        def _(eng):
            eng.wait_ge(ang_done, 1)
            eng.activation(out["sin_cos"][:], ang[:], ACT.Sin)

        @block.vector
        def _(eng):
            c = Chain(eng, dve, 0)
            mean, var = ln3_mv[:, :, 0], ln3_mv[:, :, 1]
            eng.tensor_scalar(out["rstd"][:], var, 1.0, LN_EPS, ALU.mult, ALU.add).then_inc(var_done, 1)
            eng.wait_ge(w_dma, NW)
            c.link(eng.tensor_reduce(rsum[:], router[:], AX.X, ALU.add))
            c.link(eng.tensor_scalar(w_all[:], mean, rsum[:, 0:1], None, ALU.mult))
            c.link(eng.tensor_tensor(w_all[:], ln3_dot[:], w_all[:], ALU.subtract))
            eng.wait_ge(rstd_done, 1)
            c.link(eng.tensor_tensor(w_all[:], w_all[:], out["rstd"][:], ALU.mult))
            eng.tensor_scalar(w_all[:], w_all[:], router_b[:, 0:1], None, ALU.add).then_inc(w_done, 1)
            c.link(eng.scalar_tensor_tensor(out["shift"][:], mean, -1.0, out["rstd"][:], ALU.mult, ALU.mult))
            eng.wait_ge(wt_ps, 1)
            c.link(eng.tensor_copy(wt[:], psW[:, 0:P]))
            c.link(eng.max(top[:, 0:8], wt[:]))
            c.link(eng.max_index(idx_u[:, 0:8], top[:, 0:8], wt[:]))
            c.link(eng.match_replace(wt2[:], top[:, 0:8], wt[:], LOWEST))
            c.link(eng.max(top[:, 8:16], wt2[:]))
            c.link(eng.max_index(idx_u[:, 8:16], top[:, 8:16], wt2[:]))
            c.link(eng.tensor_copy(idx_f[:], idx_u[:]))
            eng.memset(idx_f[:, SLOTS - 1:SLOTS], -1.0).then_inc(top_done, 1)
            eng.tensor_scalar(keep[:], wt[:], top[:, SLOTS - 1:SLOTS], None, ALU.is_le).then_inc(top_done, 1)
            c.link(eng.tensor_copy(pos_f[:], pos_i[:]))
            eng.wait_ge(keep_ps, 1)
            c.link(eng.tensor_tensor(out["end_scale"][:], psK[:, 0:rows], out["rstd"][:], ALU.mult))
            eng.tensor_tensor(out["end_shift"][:], psK[:, 0:rows], out["shift"][:], ALU.mult)
            c.link(eng.tensor_scalar(out["end_scale"][:], out["end_scale"][:], 1.0, None, ALU.add))
            eng.wait_ge(scratch_in, 48)
            eng.tensor_scalar(sel[:], idx_b[:], iota_p[:, 0:1], None, ALU.is_equal).then_inc(sel_done, 1)
            c.link(eng.tensor_scalar(idx_c[:], idx_c[:], 1.0, None, ALU.add))
            c.link(eng.tensor_tensor(out["idx_own"][:], idx_c[:].unsqueeze(2).broadcast_to([P, tiles, ROWS_PER_TILE]),
                                     own_slot[:].unsqueeze(1).broadcast_to([P, tiles, ROWS_PER_TILE]), ALU.mult))
            c.link(eng.tensor_scalar(out["idx_own"][:], out["idx_own"][:], -1.0, None, ALU.add))
            eng.wait_ge(pos_ps, 1)
            c.link(eng.tensor_tensor(pos_own[:], psP[:, 0:tiles * 4].rearrange("p (i b) -> p i b", b=4), pos_own[:], ALU.mult))
            c.link(eng.tensor_reduce(pos_s[:], pos_own[:], AX.X, ALU.add))
            half = [P, tiles, HD // 2]
            c.link(eng.tensor_tensor(ang[:, 0], pos_s[:].unsqueeze(2).broadcast_to(half), inv_freq[:].unsqueeze(1).broadcast_to(half), ALU.mult))
            c.link(eng.tensor_scalar(turns[:], ang[:, 0], 1.0 / (2.0 * np.pi), MAGIC, ALU.mult, ALU.add))
            c.link(eng.tensor_scalar(turns[:], turns[:], -MAGIC, None, ALU.add))
            for part in TWO_PI:
                c.link(eng.scalar_tensor_tensor(ang[:, 0], turns[:], -part, ang[:, 0], ALU.mult, ALU.add))
            c.link(eng.tensor_scalar(ang[:, 1], ang[:, 0], np.pi / 2, None, ALU.add))
            c.link(eng.tensor_scalar(over[:], ang[:, 1], PI, -2.0 * np.pi, ALU.is_gt, ALU.mult))
            c.link(eng.tensor_tensor(ang[:, 1], ang[:, 1], over[:], ALU.add))
            eng.tensor_scalar(ang[:], ang[:], PI, -PI, ALU.min, ALU.max).then_inc(ang_done, 1)


def ffn_phase(nc, hbm, rows, r_in, x_all, ident, scratch_idx, x_out):
    tiles = rows // ROWS_PER_TILE
    with ExitStack() as ctx:
        sb = lambda name, shape, dt=F32: ctx.enter_context(nc.sbuf_tensor(name, shape, dt))
        sem = lambda name: ctx.enter_context(nc.semaphore(name))
        W2 = 2
        w_q = sb("f_w_q", [P, DC, D])
        w_k = sb("f_w_k", [P, DC, D])
        w_v = sb("f_w_v", [P, DC, D])
        w_o = sb("f_w_o", [P, DC, D])
        w_1 = sb("f_w_1", [P, DC, FF])
        w_2 = sb("f_w_2", [P, FC, D])
        ln = sb("f_ln", [P, 2, D])
        mask = sb("f_mask", [P, 4, P])
        outside = sb("f_outside", [P, 32])
        odd_scale = sb("f_odd_scale", [P, 2])
        iota_p = sb("f_iota_p", [P, 1])
        iota_f = sb("f_iota_f", [P, P])
        mhalf = sb("f_mhalf", [P, 2])
        idx_b = sb("f_idx_b", [P, W2, P])
        sel = sb("f_sel", [P, W2, P])
        sel_g = sb("f_sel_g", [P, W2, ROWS_PER_TILE, P])
        big = sb("f_big", [P, W2, 16 * P])
        xs = sb("f_xs", [P, W2, D])
        hn = sb("f_hn", [P, W2, D])
        hT = sb("f_hT", [P, W2, DC, P])
        vt = sb("f_vt", [P, W2, D])
        qk = sb("f_qk", [P, W2, 2 * D])
        qz = sb("f_qz", [P, W2, 2, DC, P])
        kT = sb("f_kT", [P, W2, DC, P])
        m1 = sb("f_m1", [P, W2, P])
        mk = sb("f_mk", [P, W2, 32])
        ss = sb("f_ss", [P, W2, 2])
        rs = sb("f_rs", [P, W2, 2])
        mx = sb("f_mx", [P, W2, HEADS])
        den = sb("f_den", [P, W2, HEADS])
        ps = ctx.enter_context(nc.psum_tensor("f_ps", [P, W2, 4, 512], F32))

        names = ("idx_dma sel_v y_a gath_ps xs_a ss_v rs_p hn_v hT_ps hT_a qkv_ps rope_v vt_a m1_ps m1_a msk_ps mk_v qkT_ps "
                 "qk_a sc_ps sc_v ex_a zero_p pt_v pv_ps o_v oT_ps oT_a wo_ps x1_v ss2_v rs2_p hn2_v h2T_ps h2T_a w1_ps "
                 "ge_a scat_v w2_ps proc_v z_a scat_ps end_v out_dma").split()
        S = {n: sem("f_" + n) for n in names}
        w_dma = sem("f_w_dma")
        dve_tally = sem("f_dve_tally")
        pool_tally = sem("f_pool_tally")
        setup_v = sem("f_setup_v")
        dve = sem("f_dve")
        pool = sem("f_pool")
        out_dma = [S["out_dma"], sem("f_out_dma1")]
        idx_dma = [S["idx_dma"], sem("f_idx_dma1")]
        NW = 14 * 16
        block = ctx.enter_context(nc.Block())

        def turns(eng, body):
            body(0)
            with eng.Fori(1, tiles // W2) as i:
                body(i)

        def done(eng, name, i, w):
            eng.wait_ge(S[name], i * W2 + w + 1)

        def used(eng, name, i, w):
            need(eng, S[name], (i - 1) * W2 + w + 1)

        def bank(w, b, lo=0, hi=512):
            return ps[:, w, b, lo:hi]

        def normed(w):
            return big[:, w].rearrange("p (j d) -> p j d", d=D)

        def weights_t(w):
            return big[:, w].rearrange("p (h q) -> p h q", q=P)

        def hidden(w):
            return big[:, w, 0:8 * P].rearrange("p (f q) -> p f q", q=P)

        def sel_t(w):
            return big[:, w, 8 * P:16 * P].rearrange("p (j s) -> p j s", s=P)

        @block.sync
        def _(sp):
            for dst, name in ((w_q, "wq"), (w_k, "wk"), (w_v, "wv"), (w_1, "w1"), (w_2, "w2")):
                sp.dma_start(dst[:], hbm["L0_ffn_" + name].rearrange("(c p) n -> p c n", p=P)).then_inc(w_dma, 16)
            sp.dma_start(w_o[:], hbm["ffn_wo_by_head"].rearrange("(c p) n -> p c n", p=P)).then_inc(w_dma, 16)
            for k in range(2):
                sp.dma_start(ln[:, k, :], hbm[f"L0_ffn_ln{k + 1}"].partition_broadcast(P)).then_inc(w_dma, 16)
            sp.dma_start(mask[:], hbm["ffn_mask"]).then_inc(w_dma, 16)
            sp.dma_start(outside[:], hbm["outside"]).then_inc(w_dma, 16)
            sp.dma_start(odd_scale[:], hbm["odd_scale"]).then_inc(w_dma, 16)
            sp.dma_start(iota_p[:], hbm["iota_p"]).then_inc(w_dma, 16)
            sp.dma_start(iota_f[:], hbm["iota_f"]).then_inc(w_dma, 16)
            sp.dma_start(mhalf[:], hbm["mhalf"]).then_inc(w_dma, 16)

            def body(i):
                for w in range(W2):
                    used(sp, "sel_v", i, w)
                    sp.dma_start(idx_b[:, w, :], scratch_idx[bass.ds((i * W2 + w) * P, P)].partition_broadcast(P)).then_inc(idx_dma[w], 16)
                for w in range(W2):
                    done(sp, "end_v", i, w)
                    first_row = (i * W2 + w) * ROWS_PER_TILE
                    sp.dma_start(x_out.rearrange("b t d -> t b d")[:, bass.ds(first_row, ROWS_PER_TILE), :],
                                 x_all[:, bass.ds(first_row, ROWS_PER_TILE), :]).then_inc(out_dma[w], 16)
            turns(sp, body)
            for w in range(W2):
                sp.wait_ge(out_dma[w], 16 * (tiles // W2))

        @block.gpsimd
        def _(eng):
            eng.wait_ge(w_dma, NW)

            def body(i):
                c = Chain(eng, pool, i * 2 * W2)
                for w in range(W2):
                    done(eng, "ss_v", i, w)
                    used(eng, "hn_v", i, w)
                    settle(eng, pool_tally)
                    c.link(eng.tensor_scalar(rs[:, w, 0:1], ss[:, w, 0:1], 1.0 / D, RMS_EPS, ALU.mult, ALU.add))
                    eng.tensor_tensor(rs[:, w, 0:1], rs[:, w, 0:1], mhalf[:, 0:1], ALU.pow).then_inc(S["rs_p"], 1)
                for w in range(W2):
                    done(eng, "gath_ps", i, w)
                    settle(eng, pool_tally)
                    eng.memset(big[:, w], 0.0).then_inc(S["zero_p"], 1)
                for w in range(W2):
                    done(eng, "ss2_v", i, w)
                    settle(eng, pool_tally)
                    c.link(eng.tensor_scalar(rs[:, w, 1:2], ss[:, w, 1:2], 1.0 / D, RMS_EPS, ALU.mult, ALU.add))
                    eng.tensor_tensor(rs[:, w, 1:2], rs[:, w, 1:2], mhalf[:, 0:1], ALU.pow).then_inc(S["rs2_p"], 1)
            turns(eng, body)

        @block.scalar
        def _(eng):
            eng.wait_ge(w_dma, NW)

            def body(i):
                def copy(name, src_done, out, src):
                    for w in range(W2):
                        done(eng, src_done, i, w)
                        eng.activation(out(w), src(w), ACT.Copy).then_inc(S[name], 1)

                for w in range(W2):
                    used(eng, "scat_ps", i, w)
                    for j in range(ROWS_PER_TILE):
                        b = (i * W2 + w) * ROWS_PER_TILE + j
                        last = eng.activation(normed(w)[:, j, :], x_all[:, b, :], ACT.Identity,
                                              bias=r_in["shift"][:, bass.ds(b, 1)], scale=r_in["rstd"][:, bass.ds(b, 1)])
                    last.then_inc(S["y_a"], 1)
                copy("m1_a", "m1_ps", lambda w: m1[:, w, :], lambda w: bank(w, 3, 384, 512))
                copy("xs_a", "gath_ps", lambda w: xs[:, w, :], lambda w: bank(w, 0, 0, D))
                for w in range(W2):
                    done(eng, "y_a", i, w)
                    for j in range(ROWS_PER_TILE):
                        b = (i * W2 + w) * ROWS_PER_TILE + j
                        last = eng.activation(x_all[:, b, :], x_all[:, b, :], ACT.Identity,
                                              bias=r_in["end_shift"][:, bass.ds(b, 1)], scale=r_in["end_scale"][:, bass.ds(b, 1)])
                    last.then_inc(S["z_a"], 1)
                copy("hT_a", "hT_ps", lambda w: hT[:, w].rearrange("p c s -> p (c s)"), lambda w: bank(w, 1, 0, D))
                copy("vt_a", "qkv_ps", lambda w: vt[:, w, :], lambda w: bank(w, 3, 0, D))
                for w in range(W2):
                    done(eng, "qkT_ps", i, w)
                    eng.activation(kT[:, w].rearrange("p c s -> p (c s)"), bank(w, 1, D, 2 * D), ACT.Copy)
                    for odd in range(2):
                        last = eng.activation(qz[:, w, odd].rearrange("p c s -> p (c s)"), bank(w, 1, 0, D), ACT.Copy, scale=odd_scale[:, odd:odd + 1])
                    last.then_inc(S["qk_a"], 1)
                for w in range(W2):
                    done(eng, "sc_v", i, w)
                    eng.activation(qk[:, w, :], qk[:, w, :], ACT.Exp).then_inc(S["ex_a"], 1)
                copy("oT_a", "oT_ps", lambda w: hT[:, w].rearrange("p c s -> p (c s)"), lambda w: bank(w, 1, 0, D))
                copy("h2T_a", "h2T_ps", lambda w: hT[:, w].rearrange("p c s -> p (c s)"), lambda w: bank(w, 3, 0, D))
                for w in range(W2):
                    done(eng, "w1_ps", i, w)
                    eng.activation(hidden(w), ps[:, w, 0:2, :].rearrange("p b (f q) -> p (b f) q", q=P), ACT.Gelu_apprx_tanh).then_inc(S["ge_a"], 1)
            turns(eng, body)

        @block.vector
        def _(eng):
            eng.memset(sel_g[:], 0.0).then_inc(setup_v, 1)
            eng.wait_ge(w_dma, NW)
            eng.wait_ge(setup_v, 1)
            steps = 16

            def body(i):
                c = Chain(eng, dve, i * steps)
                tile = lambda w: i * W2 + w
                for w in range(W2):
                    eng.wait_ge(idx_dma[w], i * 16 + 16)
                    used(eng, "msk_ps", i, w)
                    used(eng, "gath_ps", i, w)
                    c.link(eng.tensor_scalar(sel[:, w, :], idx_b[:, w, :], iota_p[:, 0:1], None, ALU.is_equal))
                    diagonal = sel_g[:, w].rearrange("p j s -> p (j s)")
                    for j in range(ROWS_PER_TILE):
                        last = eng.tensor_copy(diagonal[:, j * (P + SLOTS):j * (P + SLOTS) + SLOTS], sel[:, w, j * SLOTS:(j + 1) * SLOTS])
                    last.then_inc(S["sel_v"], 1)
                for w in range(W2):
                    done(eng, "xs_a", i, w)
                    used(eng, "h2T_ps", i, w)
                    eng.tensor_tensor_reduce(hn[:, w, :], xs[:, w, :], xs[:, w, :], 1.0, 0.0, ALU.mult, ALU.add, ss[:, w, 0:1]).then_inc(S["ss_v"], 1)
                for w in range(W2):
                    done(eng, "ss_v", i, w)
                    done(eng, "rs_p", i, w)
                    eng.scalar_tensor_tensor(hn[:, w, :], xs[:, w, :], rs[:, w, 0:1], ln[:, 0, :], ALU.mult, ALU.mult).then_inc(S["hn_v"], 1)
                for w in range(W2):
                    done(eng, "msk_ps", i, w)
                    for q in range(4):
                        g = slice(32 * q, 32 * q + 32)
                        last = eng.tensor_tensor(mk[g, w, :], ps[g, w, 3, D + 32 * q:D + 32 * q + 32], outside[g, :], ALU.add)
                    last.then_inc(S["mk_v"], 1)
                for w in range(W2):
                    done(eng, "qkv_ps", i, w)
                    rot = qz[:, w].rearrange("p o c s -> p (o c s)")
                    table = [r_in["sin_cos"][:, k, bass.ds(tile(w), 1), :].broadcast_to([P, 4 * HEADS, HD // 2]) for k in range(2)]
                    t = bank(w, 2).rearrange("p (n i) -> p n i", i=HD // 2)
                    c.step(eng.tensor_tensor(rot.rearrange("p (n i) -> p n i", i=HD // 2), t, table[0], ALU.mult))
                    n2 = c.step(eng.tensor_tensor(qk[:, w, :].rearrange("p (n i) -> p n i", i=HD // 2), t, table[1], ALU.mult))
                    c.after(n2)
                    halves = qk[:, w, :].rearrange("p (n k i) -> p n k i", k=2, i=HD // 2)
                    others = rot.rearrange("p (n k i) -> p n k i", k=2, i=HD // 2)
                    eng.tensor_tensor(halves[:, :, 0, :], halves[:, :, 0, :], others[:, :, 1, :], ALU.subtract)
                    eng.tensor_tensor(halves[:, :, 1, :], halves[:, :, 1, :], others[:, :, 0, :], ALU.add).then_inc(S["rope_v"], 1)
                for w in range(W2):
                    done(eng, "sc_ps", i, w)
                    s = qk[:, w, :].rearrange("p (h k) -> p h k", k=32)
                    for q in range(4):
                        g = slice(32 * q, 32 * q + 32)
                        src = ps[g, w, :, :].rearrange("p b (h k) -> p (b h) k", k=P)[:, :, 32 * q:32 * q + 32]
                        n = c.step(eng.tensor_tensor(s[g], src, mk[g, w, :].unsqueeze(1).broadcast_to([32, HEADS, 32]), ALU.add)) if q == 3 else \
                            eng.tensor_tensor(s[g], src, mk[g, w, :].unsqueeze(1).broadcast_to([32, HEADS, 32]), ALU.add)
                    c.after(n)
                    c.link(eng.tensor_reduce(mx[:, w, :], s, AX.X, ALU.max))
                    eng.tensor_tensor(s, s, mx[:, w, :].unsqueeze(2).broadcast_to([P, HEADS, 32]), ALU.subtract).then_inc(S["sc_v"], 1)
                for w in range(W2):
                    done(eng, "ex_a", i, w)
                    done(eng, "zero_p", i, w)
                    s = qk[:, w, :].rearrange("p (h k) -> p h k", k=32)
                    used(eng, "o_v", i, w)
                    n = c.step(eng.tensor_reduce(den[:, w, :], s, AX.X, ALU.add))
                    for q in range(4):
                        g = slice(32 * q, 32 * q + 32)
                        last = eng.transpose(weights_t(w)[g, :, 32 * q:32 * q + 32], s[g])
                    last.then_inc(S["pt_v"], 1)
                    c.after(n)
                    c.link(eng.reciprocal(den[:, w, :], den[:, w, :]))
                for w in range(W2):
                    done(eng, "pv_ps", i, w)
                    eng.tensor_tensor(qz[:, w, 0].rearrange("p c s -> p (c s)").rearrange("p (h i) -> p h i", h=HEADS), bank(w, 0, 0, D).rearrange("p (h i) -> p h i", h=HEADS),
                                      den[:, w, :].unsqueeze(2).broadcast_to([P, HEADS, HD]), ALU.mult).then_inc(S["o_v"], 1)
                for w in range(W2):
                    done(eng, "pv_ps", i, w)
                    shape = [P, ROWS_PER_TILE, P]
                    eng.tensor_tensor(sel_t(w), iota_f[:].unsqueeze(1).broadcast_to(shape),
                                      r_in["idx_own"][:, bass.ds(tile(w), 1), :].rearrange("p a j -> p (a j)").unsqueeze(2).broadcast_to(shape), ALU.is_equal).then_inc(S["scat_v"], 1)
                for w in range(W2):
                    done(eng, "wo_ps", i, w)
                    eng.tensor_tensor(kT[:, w].rearrange("p c s -> p (c s)"), bank(w, 2, 0, D), xs[:, w, :], ALU.add).then_inc(S["x1_v"], 1)
                for w in range(W2):
                    done(eng, "x1_v", i, w)
                    x1 = kT[:, w].rearrange("p c s -> p (c s)")
                    eng.tensor_tensor_reduce(hn[:, w, :], x1, x1, 1.0, 0.0, ALU.mult, ALU.add, ss[:, w, 1:2]).then_inc(S["ss2_v"], 1)
                for w in range(W2):
                    done(eng, "ss2_v", i, w)
                    done(eng, "rs2_p", i, w)
                    eng.scalar_tensor_tensor(hn[:, w, :], kT[:, w].rearrange("p c s -> p (c s)"), rs[:, w, 1:2], ln[:, 1, :], ALU.mult, ALU.mult).then_inc(S["hn2_v"], 1)
                for w in range(W2):
                    done(eng, "w2_ps", i, w)
                    c.link(eng.tensor_tensor(xs[:, w, :], bank(w, 2, D, 2 * D), kT[:, w].rearrange("p c s -> p (c s)"), ALU.add))
                    eng.tensor_scalar(xs[:, w, :], xs[:, w, :], r_in["w_sel"][:, bass.ds(tile(w), 1)], None, ALU.mult).then_inc(S["proc_v"], 1)
                for w in range(W2):
                    done(eng, "scat_ps", i, w)
                    done(eng, "z_a", i, w)
                    first_row = tile(w) * ROWS_PER_TILE
                    x_rows = x_all[:, bass.ds(first_row, ROWS_PER_TILE), :].rearrange("p j d -> p (j d)")
                    eng.tensor_tensor(x_rows, ps[:, w].rearrange("p b n -> p (b n)"), x_rows, ALU.add).then_inc(S["end_v"], 1)
                assert c.n == steps, c.n
            turns(eng, body)

        @block.tensor
        def _(eng):
            eng.wait_ge(w_dma, NW)

            def body(i):
                first = isinstance(i, int)
                for w in range(W2):
                    done(eng, "sel_v", i, w)
                    used(eng, "end_v", i, w)
                    alone = 3 if first and w == 0 else 0
                    for b in range(alone):
                        eng.matmul(bank(w, 3, 384 + b * SLOTS, 384 + (b + 1) * SLOTS), mask[:, b, :], sel[:, w, b * SLOTS:(b + 1) * SLOTS], start=True, stop=True)
                    eng.matmul(bank(w, 3, 384 + alone * SLOTS, 512), mask[:, 3, :], sel[:, w, alone * SLOTS:P], start=True, stop=True).then_inc(S["m1_ps"], 1)
                for w in range(W2):
                    done(eng, "y_a", i, w)
                    for j in range(ROWS_PER_TILE):
                        last = eng.matmul(bank(w, 0, 0, D), sel_g[:, w, j, :], normed(w)[:, j, :], start=j == 0, stop=j == ROWS_PER_TILE - 1)
                    last.then_inc(S["gath_ps"], 1)
                for w in range(W2):
                    done(eng, "m1_a", i, w)
                    eng.matmul(bank(w, 3, D, D + P), m1[:, w, :], sel[:, w, :], start=True, stop=True).then_inc(S["msk_ps"], 1)
                for w in range(W2):
                    done(eng, "hn_v", i, w)
                    for ch in range(DC):
                        last = eng.transpose(bank(w, 1, ch * P, (ch + 1) * P), hn[:, w, ch * P:(ch + 1) * P], ident[:])
                    last.then_inc(S["hT_ps"], 1)
                for w in range(W2):
                    done(eng, "hT_a", i, w)
                    done(eng, "mk_v", i, w)
                    for wt, out in ((w_q, bank(w, 2, 0, D)), (w_k, bank(w, 2, D, 2 * D)), (w_v, bank(w, 3, 0, D))):
                        for ch in range(DC):
                            last = eng.matmul(out, hT[:, w, ch, :], wt[:, ch, :], start=ch == 0, stop=ch == DC - 1)
                    last.then_inc(S["qkv_ps"], 1)
                for w in range(W2):
                    done(eng, "rope_v", i, w)
                    for half in range(2):
                        for ch in range(DC):
                            k = half * 2 + ch
                            last = eng.transpose(bank(w, 1, k * P, (k + 1) * P), qk[:, w, k * P:(k + 1) * P], ident[:])
                    last.then_inc(S["qkT_ps"], 1)
                for w in range(W2):
                    done(eng, "qk_a", i, w)
                    done(eng, "vt_a", i, w)
                    for ch in range(DC):
                        for odd in range(2):
                            for q in range(4):
                                rows_q = slice(32 * q, 32 * q + 32)
                                k = ch * 2 + odd
                                last = eng.matmul(bank(w, q, k * P, (k + 1) * P), qz[rows_q, w, odd, ch, :], kT[rows_q, w, ch, :], start=True, stop=True)
                    last.then_inc(S["sc_ps"], 1)
                for w in range(W2):
                    done(eng, "pt_v", i, w)
                    for q in range(4):
                        for ch in range(DC):
                            for odd in range(2):
                                h, at = 8 * ch + 2 * q + odd, 4 * q + 2 * ch + odd
                                last = eng.matmul(bank(w, 0, at * HD, (at + 1) * HD), weights_t(w)[:, at, :], vt[:, w, h * HD:(h + 1) * HD], start=True, stop=True)
                    last.then_inc(S["pv_ps"], 1)
                for w in range(W2):
                    done(eng, "o_v", i, w)
                    o = qz[:, w, 0]
                    for ch in range(DC):
                        last = eng.transpose(bank(w, 1, ch * P, (ch + 1) * P), o[:, ch, :], ident[:])
                    last.then_inc(S["oT_ps"], 1)
                for w in range(W2):
                    done(eng, "oT_a", i, w)
                    for ch in range(DC):
                        last = eng.matmul(bank(w, 2, 0, D), hT[:, w, ch, :], w_o[:, ch, :], start=ch == 0, stop=ch == DC - 1)
                    last.then_inc(S["wo_ps"], 1)
                for w in range(W2):
                    done(eng, "hn2_v", i, w)
                    for ch in range(DC):
                        last = eng.transpose(bank(w, 3, ch * P, (ch + 1) * P), hn[:, w, ch * P:(ch + 1) * P], ident[:])
                    last.then_inc(S["h2T_ps"], 1)
                for w in range(W2):
                    done(eng, "h2T_a", i, w)
                    for f in range(FC):
                        for ch in range(DC):
                            last = eng.matmul(bank(w, f // 4, (f % 4) * P, (f % 4 + 1) * P), w_1[:, ch, f * P:(f + 1) * P], hT[:, w, ch, :],
                                              start=ch == 0, stop=ch == DC - 1)
                    last.then_inc(S["w1_ps"], 1)
                for w in range(W2):
                    done(eng, "ge_a", i, w)
                    for f in range(FC):
                        last = eng.matmul(bank(w, 2, D, 2 * D), hidden(w)[:, f, :], w_2[:, f, :], start=f == 0, stop=f == FC - 1)
                    last.then_inc(S["w2_ps"], 1)
                for w in range(W2):
                    done(eng, "proc_v", i, w)
                    done(eng, "scat_v", i, w)
                    for j in range(ROWS_PER_TILE):
                        last = eng.matmul(bank(w, j // 2, (j % 2) * D, (j % 2 + 1) * D), sel_t(w)[:, j, :], xs[:, w, :], start=True, stop=True)
                    last.then_inc(S["scat_ps"], 1)
            turns(eng, body)


def program(nc, hbm, x_out):
    rows = hbm["x"].shape[0]
    tiles = rows // ROWS_PER_TILE
    with ExitStack() as ctx:
        sb = lambda name, shape: ctx.enter_context(nc.sbuf_tensor(name, shape, F32))
        x_all = sb("x_all", [P, rows, D])
        ident = sb("ident", [P, P])
        ln3_mv = sb("ln3_mv", [P, rows, 2])
        ln3_dot = sb("ln3_dot", [P, rows])
        gla_phase(nc, rows // 2, hbm, x_all, ident)
        xattn_phase(nc, rows // 2, hbm, x_all, ident, ln3_mv, ln3_dot)
        routed = {
            "rstd": sb("rstd3", [P, rows]), "shift": sb("shift3", [P, rows]),
            "end_scale": sb("end_scale", [P, rows]), "end_shift": sb("end_shift", [P, rows]),
            "idx_own": sb("idx_own", [P, tiles, ROWS_PER_TILE]), "w_sel": sb("w_sel", [P, tiles]),
            "sin_cos": sb("sin_cos", [P, 2, tiles, HD // 2]),
        }
        scratch_idx = nc.dram_tensor("scratch_idx", [rows * SLOTS], F32).ap()
        route_phase(nc, hbm, rows, routed, ln3_mv, ln3_dot, ident, scratch_idx)
        ffn_phase(nc, hbm, rows, routed, x_all, ident, scratch_idx, x_out)


def shape_constants(rows):
    i = np.arange(P)
    split = np.zeros((P, P), np.int64)
    for k in range(7):
        split[((i[:, None] ^ i[None, :]) >> k) > 0] = 1 << k
    before = i[:, None] < i[None, :]
    near = [(split == h) & before for h in (8, 4, 2, 1)] + [split == 0]
    own = i[:, None] // SLOTS == np.arange(ROWS_PER_TILE)[None, :]
    pos_own = np.zeros((P, rows // ROWS_PER_TILE, 4), np.float32)
    pos_own[:, 1:, 3] = 1.0
    pos_own[i, 0, np.minimum(i // SLOTS, 3)] = 1.0
    k = np.arange(32)
    same = (k[None, :] // SLOTS == (i[:, None] // SLOTS) % 2) & (k[None, :] % SLOTS != SLOTS - 1)
    freq = (1.0 / np.float32(10000.0) ** (np.arange(0, HD, 2, dtype=np.float32) / np.float32(HD))).astype(np.float32)
    odd = (i // HD) % 2
    return {
        "ident": np.eye(P, dtype=np.float32),
        "mask_far": ((split >= 16) & before).astype(np.float32),
        "mask_near": np.ascontiguousarray(np.stack(near, 1).astype(np.int32)),
        "odd_scale": np.stack([(odd == 0) * HD ** -0.5, (odd == 1) * HD ** -0.5], 1).astype(np.float32),
        "mhalf": np.full((P, 2), -0.5, np.float32),
        "iota_p": i[:, None].astype(np.float32),
        "iota_f": np.ascontiguousarray(np.broadcast_to(i[None, :], (P, P)).astype(np.float32)),
        "own_slot": own.astype(np.float32),
        "pos_own": pos_own,
        "outside": np.where(same, 0.0, -1e30).astype(np.float32),
        "inv_freq": np.ascontiguousarray(np.broadcast_to(freq[None, :], (P, HD // 2))),
    }


def laid_out(inputs):
    a = {k: np.asarray(v) for k, v in inputs.items()}
    rows = a["x"].shape[0]
    names = ["x", "ctx_1024"] + [f"L0_attn_{n}" for n in ("Wq", "Wk", "Wg", "Wv", "Wo", "bv", "bo")]
    names += [f"L0_xattn_{n}" for n in ("Wq", "Wk", "Wv", "Wo", "bv", "bo")]
    names += [f"L0_ffn_{n}" for n in ("wq", "wk", "wv", "w1", "w2", "ln1", "ln2", "router_b")]
    out = {n: a[n] for n in names}
    out["router"] = a["L0_ffn_router_w"].reshape(D)
    out["attn_bias_cols"] = np.stack([np.tile(a[f"L0_attn_b{n}"], 2) for n in "qkg"], 1)
    out["xattn_bias_cols"] = np.stack([a[f"L0_xattn_b{n}"].reshape(DC, P).T for n in "qk"], 1)
    out["ffn_wo_by_head"] = a["L0_ffn_wo"].reshape(DC, 4, 2, HD, D).transpose(1, 0, 2, 3, 4).reshape(D, D)
    out["ffn_mask"] = a["L0_ffn_attention_mask"][:, 0, :P, :P].transpose(1, 0, 2)
    out["positions"] = a["L0_ffn_position_ids"][:, :P].T
    out.update(shape_constants(rows))
    return {k: np.ascontiguousarray(v) for k, v in out.items()}


def kernel(**inputs):
    import concourse.bacc as bacc
    from concourse.bass_utils import run_bass_kernel_spmd

    nc = bacc.Bacc("TRN2", target_bir_lowering=False, num_devices=1)
    arrays = laid_out(inputs)
    hbm = {k: nc.dram_tensor(f"in_{k}", a.shape, mybir.dt.from_np(a.dtype), kind="ExternalInput").ap() for k, a in arrays.items()}
    x_out = nc.dram_tensor("out_x", arrays["x"].shape, F32, kind="ExternalOutput").ap()
    program(nc, hbm, x_out)
    r = run_bass_kernel_spmd(nc, [{f"in_{k}": a for k, a in arrays.items()}], core_ids=[0])
    return r.results[0]["out_x"]
```

```python
from contextlib import ExitStack

import numpy as np
import concourse.bass as bass
from concourse import mybir

F32 = mybir.dt.float32
BF16 = mybir.dt.bfloat16
I32 = mybir.dt.int32
U32 = mybir.dt.uint32
ALU = mybir.AluOpType
ACT = mybir.ActivationFunctionType
AX = mybir.AxisListType

P = 128
D = 256
DC = D // P
KV = 64
LN_EPS = 1e-5


def need(eng, sem, value):
    if isinstance(value, int) and value <= 0:
        return
    eng.wait_ge(sem, value)


def run_units(eng, units, ahead, body):
    for u in range(2):
        body(u, u % 2, False)
    with eng.Fori(1, units // 2 - 1) as i:
        for parity in range(2):
            body(i * 2 + parity, parity, False)
    for u in range(units - 2, units):
        body(u, u % 2, u + ahead >= units)


def run_skewed(eng, units, lead, tail, body, drain=1):
    known = lambda i: lambda k: 0 <= i + k < units
    first = 2 * drain
    end = units - tail - tail % 2
    for i in range(-lead, first):
        body(i, i % 2, known(i))
    with eng.Fori(first // 2, end // 2) as turn:
        for parity in range(2):
            body(turn * 2 + parity, parity, lambda k: True)
    for i in range(end, units + drain):
        body(i, i % 2, known(i))


def settle(eng, tally):
    eng.sem_inc(tally, 1)


class Chain:

    def __init__(self, eng, sem, base, value=0):
        self.eng, self.sem, self.base, self.n = eng, sem, base, value

    def step(self, instruction):
        instruction.then_inc(self.sem, 1)
        self.n += 1
        return self.n

    def after(self, n):
        self.eng.wait_ge(self.sem, self.base + n)

    def link(self, instruction):
        self.after(self.step(instruction))


def gla_phase(nc, units, hbm, x_all, ident):
    with ExitStack() as ctx:
        sb = lambda name, shape, dt=F32: ctx.enter_context(nc.sbuf_tensor(name, shape, dt))
        ps = lambda name, shape, dt=F32: ctx.enter_context(nc.psum_tensor(name, shape, dt))
        sem = lambda name: ctx.enter_context(nc.semaphore(name))

        w_qkg = sb("g_w_qkg", [P, 3, DC, KV])
        w_v = sb("g_w_v", [P, DC, KV])
        w_o = sb("g_w_o", [KV + 1, D])
        b_qkg = sb("g_b_qkg", [P, 3])
        nb_kg = sb("g_nb_kg", [P, 2])
        b_v = sb("g_b_v", [P, 2, KV])
        mask_far = sb("g_mask_far", [P, P])
        mask_near = sb("g_mask_near", [P, 5, P], I32)
        mhalf = sb("g_mhalf", [P, 2])
        stats = sb("g_stats", [P, 2, 6])
        mv = sb("g_mv", [P, 2, 2, 2])
        vare = sb("g_vare", [P, 2, 2])
        rstd = sb("g_rstd", [P, 2, 2])
        hn = sb("g_hn", [P, 2, 2, D])
        hT = sb("g_hT", [P, 2, DC, 2, P])
        ekg = sb("g_ekg", [P, 2, 2 * P])
        XW = 4 * P + 6 * 2 * P
        X = sb("g_X", [P, 2, XW])
        EB = [P // h for h in (1, 2, 4, 8, 16, 32)]
        blk = {h: sb(f"g_blk{h}", [P, 2, P // h]) for h in (2, 4, 8, 16, 32)}
        fac = {h: sb(f"g_fac{h}", [P, 2, 2 * (P // h)]) for h in (1, 2, 4, 8, 16, 32)}
        A = sb("g_A", [P, 2, 2, P])
        v = sb("g_v", [P, 2, 2, KV])
        oT = sb("g_oT", [KV + 1, 2, 2, P])

        psT = ps("g_psT", [P, 512])
        psP = ps("g_psP", [P, 512])
        psL = ps("g_psL", [P, 2, 2, 512])
        psO = ps("g_psO", [P, 512])
        psW = ps("g_psW", [P, 512])

        x_dma = [sem("g_x_even"), sem("g_x_odd")]
        w_dma = sem("g_w_dma")
        dve_tally = sem("g_dve_tally")
        pool_tally = sem("g_pool_tally")
        setup_v = sem("g_setup_v")
        setup_a = sem("g_setup_a")
        setup_p = sem("g_setup_p")
        vare_done = sem("g_vare_done")
        bn_done = sem("g_bn_done")
        exp_plus_one = sem("g_exp_plus_one")
        level_done = sem("g_level_done")
        mask_step = sem("g_mask_step")
        product_done = sem("g_product_done")
        qg_done = sem("g_qg_done")
        stats_done = sem("g_stats_done")
        rstd_done = sem("g_rstd_done")
        hn_done = sem("g_hn_done")
        hT_ps = sem("g_hT_ps")
        hT_done = sem("g_hT_done")
        proj_ps = sem("g_proj_ps")
        kg_exp = sem("g_kg_exp")
        q_done = sem("g_q_done")
        gates_done = sem("g_gates_done")
        blk_done = sem("g_blk_done")
        v_done = sem("g_v_done")
        X_done = sem("g_X_done")
        L_ps = sem("g_L_ps")
        A_done = sem("g_A_done")
        O_ps = sem("g_O_ps")
        oT_done = sem("g_oT_done")
        W_ps = sem("g_W_ps")
        x1_done = sem("g_x1_done")

        def load_consts(sp):
            for dst, src in (
                (w_qkg[:, 0], hbm["L0_attn_Wq"]), (w_qkg[:, 1], hbm["L0_attn_Wk"]),
                (w_qkg[:, 2], hbm["L0_attn_Wg"]), (w_v[:], hbm["L0_attn_Wv"]),
            ):
                sp.dma_start(dst, src.rearrange("(c p) n -> p c n", p=P)).then_inc(w_dma, 16)
            sp.dma_start(w_o[0:KV, :], hbm["L0_attn_Wo"]).then_inc(w_dma, 16)
            sp.dma_start(w_o[KV:KV + 1, :], hbm["L0_attn_bo"].rearrange("(a n) -> a n", a=1)).then_inc(w_dma, 16)
            sp.dma_start(b_qkg[:], hbm["attn_bias_cols"]).then_inc(w_dma, 16)
            for r in range(2):
                sp.dma_start(b_v[:, r, :], hbm["L0_attn_bv"].partition_broadcast(P)).then_inc(w_dma, 16)
            sp.dma_start(mask_far[:], hbm["mask_far"]).then_inc(w_dma, 16)
            sp.dma_start(mask_near[:], hbm["mask_near"]).then_inc(w_dma, 16)
            sp.dma_start(ident[:], hbm["ident"]).then_inc(w_dma, 16)
        NW = 12 * 16

        block = ctx.enter_context(nc.Block())

        @block.sync
        def _(sp):
            x_src = hbm["x"].rearrange("b t d -> t b d")

            def body(u, parity, last):
                need(sp, x_dma[parity], (u - parity) * 8)
                sp.dma_start(x_all[:, bass.ds(u * 2, 2), :], x_src[:, bass.ds(u * 2, 2), :]).then_inc(x_dma[parity], 16)
                if isinstance(u, int) and u == 0:
                    load_consts(sp)
            run_units(sp, units, 0, body)

        LEAD, TAIL = 4, 4

        @block.gpsimd
        def _(eng):
            eng.memset(mhalf[:], -0.5).then_inc(setup_p, 1)
            eng.wait_ge(setup_p, 1)
            eng.wait_ge(setup_v, 3)

            def rstd_of(u, parity):
                eng.wait_ge(stats_done, u + 1)
                need(eng, hn_done, u - 1)
                settle(eng, pool_tally)
                eng.tensor_scalar(vare[:, parity, :], mv[:, parity, :, 1], 1.0, LN_EPS, ALU.mult, ALU.add).then_inc(vare_done, 1)
                eng.wait_ge(vare_done, u + 1)
                eng.tensor_tensor(rstd[:, parity, :], vare[:, parity, :], mhalf[:], ALU.pow).then_inc(rstd_done, 1)

            def blocks_of(u, parity):
                eng.wait_ge(gates_done, u + 1)
                need(eng, X_done, u - 1)
                E = X[:, parity, 2 * P:3 * P]
                for k, h in enumerate((1, 2, 4, 8, 16, 32)):
                    nb = P // h
                    dst = fac[h][:, parity, 1:2 * nb - 1].rearrange("p (i r) -> p i r", i=2)[:, :, 0:nb - 1:2]
                    if h < 32:
                        E2 = blk[2 * h][:, parity, :]
                        eng.tensor_tensor(E2, E[:, 0:nb:2], E[:, 1:nb:2], ALU.mult).then_inc(product_done, 1)
                    settle(eng, pool_tally)
                    eng.tensor_scalar(dst, E.rearrange("p (j i) -> p i j", i=2), 1.0, 0.0, ALU.mult, ALU.add).then_inc(blk_done, 1)
                    if h < 32:
                        eng.wait_ge(product_done, u * 5 + k + 1)
                        E = E2

            def body(i, parity, on):
                if on(1):
                    blocks_of(i + 1, 1 - parity)
                if on(4):
                    rstd_of(i + 4, parity)
            run_skewed(eng, units, LEAD, TAIL, body)

        @block.scalar
        def _(eng):
            eng.wait_ge(w_dma, NW)
            eng.activation(nb_kg[:], b_qkg[:, 1:3], ACT.Copy, scale=-1.0).then_inc(setup_a, 1)
            eng.wait_ge(setup_a, 1)

            def gates_of(u, parity):
                eng.wait_ge(proj_ps, u + 1)
                need(eng, gates_done, u - 1)
                eng.activation(ekg[:, parity, 0:P], psP[:, P:2 * P], ACT.Exp, bias=nb_kg[:, 0:1], scale=-1.0)
                eng.activation(ekg[:, parity, P:2 * P], psP[:, 2 * P:3 * P], ACT.Exp, bias=nb_kg[:, 1:2], scale=-1.0).then_inc(kg_exp, 1)
                need(eng, L_ps, u - 1)
                eng.activation(X[:, parity, 3 * P:4 * P], psP[:, 0:P], ACT.Identity, bias=b_qkg[:, 0:1]).then_inc(q_done, 1)

            def hT_of(u, parity):
                eng.wait_ge(hT_ps, u + 1)
                need(eng, proj_ps, u - 1)
                eng.activation(hT[:, parity], psT[:].rearrange("p (c b t) -> p c b t", c=DC, b=2), ACT.Copy).then_inc(hT_done, 1)

            def outputs_of(u, parity):
                eng.wait_ge(O_ps, u + 1)
                need(eng, W_ps, u - 1)
                eng.activation(oT[0:KV, parity], psO[0:KV, 0:2 * P].rearrange("p (b t) -> p b t", b=2), ACT.Copy).then_inc(oT_done, 1)

            def body(i, parity, on):
                if on(2):
                    gates_of(i + 2, parity)
                if on(3):
                    hT_of(i + 3, 1 - parity)
                if on(0):
                    outputs_of(i, parity)
            run_skewed(eng, units, LEAD, TAIL, body)

        @block.vector
        def _(eng):
            for h in (1, 2, 4, 8, 16, 32):
                last = eng.memset(fac[h][:], 1.0)
                if h in (8, 32):
                    last.then_inc(setup_v, 1)
            eng.memset(oT[KV:KV + 1], 1.0).then_inc(setup_v, 1)
            eng.wait_ge(w_dma, NW)

            def v_of(u, parity):
                eng.wait_ge(q_done, u + 1)
                need(eng, O_ps, u - 1)
                eng.tensor_tensor(v[:, parity], psP[:, 3 * P:4 * P].rearrange("p (b n) -> p b n", b=2), b_v[:], ALU.add).then_inc(v_done, 1)

            def gate_sum_of(u, parity):
                eng.wait_ge(kg_exp, u + 1)
                eng.tensor_scalar(ekg[:, parity, :], ekg[:, parity, :], 1.0, None, ALU.add).then_inc(exp_plus_one, 1)

            def gates_of(u, parity):
                need(eng, L_ps, u - 1)
                need(eng, blk_done, 6 * (u - 1))
                eng.wait_ge(exp_plus_one, u + 1)
                eng.reciprocal(X[:, parity, P:3 * P], ekg[:, parity, :]).then_inc(gates_done, 1)

            def gated_query_of(u, parity):
                eng.wait_ge(gates_done, u + 1)
                eng.wait_ge(q_done, u + 1)
                eng.tensor_tensor(X[:, parity, 0:P], X[:, parity, 3 * P:4 * P], X[:, parity, 2 * P:3 * P], ALU.mult).then_inc(qg_done, 1)

            def level_of(u, parity, k):
                h = 1 << k
                nb = P // h
                src, dst = 4 * P + (k - 1) * 2 * P if k else 0, 4 * P + k * 2 * P
                eng.wait_ge(blk_done, u * 6 + k + 1)
                if k:
                    eng.wait_ge(level_done, u * 5 + k)
                else:
                    eng.wait_ge(qg_done, u + 1)
                lo, hi = (0, 2 * nb) if h < 32 else (nb // 2, nb + nb // 2)
                a = X[:, parity, src + lo * h:src + hi * h].rearrange("p (n h) -> p n h", h=h)
                o = X[:, parity, dst + lo * h:dst + hi * h].rearrange("p (n h) -> p n h", h=h)
                f = fac[h][:, parity, lo:hi].unsqueeze(2).broadcast_to([P, hi - lo, h])
                eng.tensor_tensor(o, a, f, ALU.mult).then_inc(level_done if k < 5 else X_done, 1)

            def stats_of(u, parity, load_parity):
                eng.wait_ge(x_dma[load_parity], (u - load_parity) * 8 + 16)
                need(eng, stats_done, u)
                settle(eng, dve_tally)
                for r in range(2):
                    last = eng.bn_stats(stats[:, r, :], x_all[:, u * 2 + r, :])
                last.then_inc(bn_done, 1)

            def mean_of(u, parity):
                eng.wait_ge(bn_done, u + 1)
                need(eng, hn_done, u - 1)
                settle(eng, dve_tally)
                for r in range(2):
                    last = eng.bn_aggr(mv[:, parity, r, :], stats[:, r, :])
                last.then_inc(stats_done, 1)

            def norm_of(u, parity):
                need(eng, hT_ps, u - 1)
                eng.wait_ge(stats_done, u + 1)
                eng.wait_ge(rstd_done, u + 1)
                for r in range(2):
                    last = eng.tensor_scalar(hn[:, parity, r, :], x_all[:, u * 2 + r, :], mv[:, parity, r, 0:1],
                                             rstd[:, parity, r:r + 1], ALU.subtract, ALU.mult)
                last.then_inc(hn_done, 1)

            def mask_of(u, parity, k):
                out = A[:, parity]
                if k == 0:
                    eng.wait_ge(L_ps, u + 1)
                    need(eng, O_ps, u - 1)
                    eng.tensor_tensor(out, psL[:, :, 0, 0:P], mask_far[:].unsqueeze(1).broadcast_to([P, 2, P]), ALU.mult).then_inc(mask_step, 1)
                    return
                tile = psL[:, :, 0, k * P:(k + 1) * P] if k < 4 else psL[:, :, 1, (k - 4) * P:(k - 3) * P]
                eng.wait_ge(mask_step, u * 5 + k)
                settle(eng, dve_tally)
                eng.copy_predicated(out, mask_near[:, k - 1, :].unsqueeze(1).broadcast_to([P, 2, P]), tile).then_inc(mask_step if k < 5 else A_done, 1)

            def residual_of(u):
                eng.wait_ge(W_ps, u + 1)
                eng.tensor_tensor(x_all[:, bass.ds(u * 2, 2), :], psW[:].rearrange("p (b d) -> p b d", b=2),
                                  x_all[:, bass.ds(u * 2, 2), :], ALU.add).then_inc(x1_done, 1)

            def body(i, parity, on):
                other = 1 - parity
                if on(1):
                    gate_sum_of(i + 1, other)
                    v_of(i + 1, other)
                    gates_of(i + 1, other)
                if on(4):
                    stats_of(i + 4, parity, parity)
                if on(1):
                    gated_query_of(i + 1, other)
                if on(4):
                    mean_of(i + 4, parity)
                if on(3):
                    norm_of(i + 3, other)
                for k in range(6):
                    if on(0):
                        mask_of(i, parity, k)
                    if on(1):
                        level_of(i + 1, other, k)
                if on(-1):
                    residual_of(i - 1)
            run_skewed(eng, units, LEAD, TAIL, body)

        @block.tensor
        def _(eng):
            eng.wait_ge(w_dma, NW)
            eng.wait_ge(setup_v, 3)

            def transposes(u, parity):
                eng.wait_ge(hn_done, u + 1)
                need(eng, hT_done, u)
                for ch in range(DC):
                    for r in range(2):
                        last = eng.transpose(psT[:, (ch * 2 + r) * P:(ch * 2 + r + 1) * P],
                                             hn[:, parity, r, ch * P:(ch + 1) * P], ident[:])
                last.then_inc(hT_ps, 1)

            def project(u, parity):
                eng.wait_ge(hT_done, u + 1)
                need(eng, kg_exp, u)
                need(eng, q_done, u)
                need(eng, v_done, u)
                for r in range(2):
                    for f in range(3):
                        for ch in range(DC):
                            eng.matmul(psP[r * KV:(r + 1) * KV, f * P:(f + 1) * P], w_qkg[:, f, ch, :],
                                       hT[:, parity, ch, r, :], start=ch == 0, stop=ch == DC - 1)
                for r in range(2):
                    for ch in range(DC):
                        last = eng.matmul(psP[:, 3 * P + r * KV:3 * P + (r + 1) * KV], hT[:, parity, ch, r, :],
                                          w_v[:, ch, :], start=ch == 0, stop=ch == DC - 1)
                last.then_inc(proj_ps, 1)

            def levels(u, parity):
                eng.wait_ge(X_done, u + 1)
                need(eng, A_done, u)
                far = 4 * P + 3 * 2 * P

                def pair(r, query, key, s, t, out):
                    rows = slice(r * KV, (r + 1) * KV)
                    return eng.matmul(out[s, t], X[rows, parity, key + s.start:key + s.stop],
                                      X[rows, parity, query + t.start:query + t.stop], start=True, stop=True)
                every = slice(0, P)
                for k, base in enumerate((far, 4 * P + 2 * 2 * P, 4 * P + 2 * P, 4 * P)):
                    for r in range(2):
                        pair(r, base, base + P, every, every, psL[:, r, 0, k * P:(k + 1) * P])
                for k, (query, key) in enumerate(((0, P), (3 * P, P))):
                    for r in range(2):
                        pair(r, query, key, every, every, psL[:, r, 1, k * P:(k + 1) * P])
                for r in range(2):
                    base = far + 2 * P
                    pair(r, base, base + P, slice(0, 32), slice(32, 64), psL[:, r, 0, 0:P])
                    pair(r, base, base + P, slice(64, 96), slice(96, 128), psL[:, r, 0, 0:P])
                    last = pair(r, base + 2 * P, base + 3 * P, slice(0, 64), slice(64, 128), psL[:, r, 0, 0:P])
                last.then_inc(L_ps, 1)

            def weighted(u, parity):
                eng.wait_ge(A_done, u + 1)
                eng.wait_ge(v_done, u + 1)
                need(eng, oT_done, u)
                for r in range(2):
                    last = eng.matmul(psO[0:KV, r * P:(r + 1) * P], v[:, parity, r, :], A[:, parity, r, :], start=True, stop=True)
                last.then_inc(O_ps, 1)

            def project_out(u, parity):
                eng.wait_ge(oT_done, u + 1)
                need(eng, x1_done, u)
                for r in range(2):
                    last = eng.matmul(psW[:, r * D:(r + 1) * D], oT[:, parity, r, :], w_o[:], start=True, stop=True)
                last.then_inc(W_ps, 1)

            def body(i, parity, on):
                if on(0):
                    levels(i, parity)
                if on(-1):
                    project_out(i - 1, 1 - parity)
                if on(2):
                    project(i + 2, parity)
                if on(3):
                    transposes(i + 3, 1 - parity)
                if on(0):
                    weighted(i, parity)
            run_skewed(eng, units, LEAD, TAIL, body)


HEADS = 16
HD = D // HEADS
VW = HD + 1


def xattn_phase(nc, units, hbm, x_all, ident, ln3_mv, ln3_dot):
    with ExitStack() as ctx:
        sb = lambda name, shape, dt=F32: ctx.enter_context(nc.sbuf_tensor(name, shape, dt))
        ps = lambda name, shape, dt=F32: ctx.enter_context(nc.psum_tensor(name, shape, dt))
        sem = lambda name: ctx.enter_context(nc.semaphore(name))

        w_q = sb("a_w_q", [P, DC, D])
        w_k = sb("a_w_k", [P, DC, D])
        w_v = sb("a_w_v", [P, DC, D])
        w_o = sb("a_w_o", [P, DC, D])
        b_cols = sb("a_b_cols", [P, 2, DC])
        odd_scale = sb("a_odd_scale", [P, 2])
        qb_cols = sb("a_qb_cols", [P, 2, DC])
        b_v = sb("a_b_v", [P, 2, D])
        b_o = sb("a_b_o", [P, 2, D])
        router = sb("a_router", [P, 2, D])
        ident_bf = sb("a_ident_bf", [P, P], BF16)
        mhalf = sb("a_mhalf", [P, 2])

        ctx_in = sb("a_ctx", [P, 2, 2, D])
        stats = sb("a_stats", [P, 2, 6])
        mv = sb("a_mv", [P, 2, 2])
        vare = sb("a_vare", [P, 2])
        rstd = sb("a_rstd", [P, 2])
        hn = sb("a_hn", [P, 2, D])
        hT = sb("a_hT", [P, DC, 2, P])
        cT = sb("a_cT", [P, DC, 2, P])
        qz = sb("a_qz", [P, 2, 2, DC, 2, P])
        kT = sb("a_kT", [P, 2, DC, 2, P])
        qz_bf = sb("a_qz_bf", [P, 2, 2, DC, 2, P], BF16)
        k_bf = sb("a_k_bf", [P, 2, DC, 2, P], BF16)
        vz = sb("a_vz", [P, 2, 2, HEADS, 2 * HD])
        onez = sb("a_onez", [P, 2, 2 * HD])
        nmax = sb("a_nmax", [P, 2, 4], BF16)
        pT = sb("a_pT", [P, 2, 4, 4, P])
        rden = sb("a_rden", [P, 2, P])
        oT = sb("a_oT", [P, 2, DC, P])
        stats3 = sb("a_stats3", [P, 2, 6])
        mv3 = sb("a_mv3", [P, 2, 2])
        prod = sb("a_prod", [P, 2, D])

        psA = ps("a_psA", [P, 512])
        psB = ps("a_psB", [P, 512])
        psC = ps("a_psC", [P, 512])
        psM = [ps(f"a_psM{i}", [P, 512]) for i in range(2)]
        psE = [ps(f"a_psE{i}", [P, 512]) for i in range(2)]
        psO = ps("a_psO", [P, 512])

        ctx_dma = [sem("a_ctx_even"), sem("a_ctx_odd")]
        w_dma = sem("a_w_dma")
        dve_tally = sem("a_dve_tally")
        pool_tally = sem("a_pool_tally")
        setup_v = sem("a_setup_v")
        bn_done = sem("a_bn_done")
        bn3_done = sem("a_bn3_done")
        mean3_done = sem("a_mean3_done")
        kept_done = sem("a_kept_done")
        rden_done = sem("a_rden_done")
        vare_done = sem("a_vare_done")
        stats_done = sem("a_stats_done")
        rstd_done = sem("a_rstd_done")
        hn_done = sem("a_hn_done")
        bo_done = sem("a_bo_done")
        hT_ps = sem("a_hT_ps")
        cT_ps = sem("a_cT_ps")
        hT_done = sem("a_hT_done")
        cT_done = sem("a_cT_done")
        q_ps = sem("a_q_ps")
        k_ps = sem("a_k_ps")
        v_ps = sem("a_v_ps")
        q_done = sem("a_q_done")
        k_done = sem("a_k_done")
        v_done = sem("a_v_done")
        qk_bf_done = sem("a_qk_bf_done")
        max_ps = sem("a_max_ps")
        nmax_done = sem("a_nmax_done")
        score_ps = sem("a_score_ps")
        p_done = sem("a_p_done")
        pv_ps = sem("a_pv_ps")
        oT_done = sem("a_oT_done")
        wo_ps = sem("a_wo_ps")
        x2_done = sem("a_x2_done")
        prod_done = sem("a_prod_done")
        dot_done = sem("a_dot_done")

        NW = 13 * 16
        block = ctx.enter_context(nc.Block())

        @block.sync
        def _(sp):
            for dst, name in ((w_q, "Wq"), (w_k, "Wk"), (w_v, "Wv"), (w_o, "Wo")):
                sp.dma_start(dst[:], hbm["L0_xattn_" + name].rearrange("(c p) n -> p c n", p=P)).then_inc(w_dma, 16)
            sp.dma_start(b_cols[:], hbm["xattn_bias_cols"]).then_inc(w_dma, 16)
            sp.dma_start(odd_scale[:], hbm["odd_scale"]).then_inc(w_dma, 16)
            sp.dma_start(mhalf[:], hbm["mhalf"]).then_inc(w_dma, 16)
            for r in range(2):
                sp.dma_start(b_v[:, r, :], hbm["L0_xattn_bv"].partition_broadcast(P)).then_inc(w_dma, 16)
                sp.dma_start(b_o[:, r, :], hbm["L0_xattn_bo"].partition_broadcast(P)).then_inc(w_dma, 16)
                sp.dma_start(router[:, r, :], hbm["router"].partition_broadcast(P)).then_inc(w_dma, 16)
            c_src = hbm["ctx_1024"].rearrange("b t d -> t b d")

            def body(u, parity, last):
                need(sp, cT_ps, u - 1)
                sp.dma_start(ctx_in[:, parity], c_src[:, bass.ds(u * 2, 2), :]).then_inc(ctx_dma[parity], 16)
            run_units(sp, units, 0, body)

        LEAD, TAIL, DRAIN = 2, 2, 2

        @block.gpsimd
        def _(eng):
            eng.wait_ge(w_dma, NW)
            def rstd_of(u):
                eng.wait_ge(stats_done, u + 1)
                need(eng, hn_done, u)
                settle(eng, pool_tally)
                eng.tensor_scalar(vare[:], mv[:, :, 1], 1.0, LN_EPS, ALU.mult, ALU.add).then_inc(vare_done, 1)
                eng.wait_ge(vare_done, u + 1)
                eng.tensor_tensor(rstd[:], vare[:], mhalf[:], ALU.pow).then_inc(rstd_done, 1)

            def narrow(u, parity):
                need(eng, max_ps, 8 * (u - 1))
                eng.wait_ge(q_done, u + 1)
                settle(eng, pool_tally)
                eng.tensor_scalar(qz_bf[:, parity], qz[:, parity], 1.0, 0.0, ALU.mult, ALU.add)
                eng.wait_ge(k_done, u + 1)
                settle(eng, pool_tally)
                eng.tensor_scalar(k_bf[:, parity], kT[:, parity], 1.0, 0.0, ALU.mult, ALU.add).then_inc(qk_bf_done, 1)

            def bias_out(u):
                eng.wait_ge(hn_done, u + 1)
                rows = x_all[:, bass.ds(u * 2, 2), :]
                eng.tensor_tensor(rows, rows, b_o[:], ALU.add).then_inc(bo_done, 1)

            def route(u):
                eng.wait_ge(x2_done, 2 * u + 2)
                need(eng, dot_done, u)
                eng.tensor_tensor(prod[:], x_all[:, bass.ds(u * 2, 2), :], router[:], ALU.mult).then_inc(prod_done, 1)

            def body(i, parity, on):
                if on(-2):
                    route(i - 2)
                if on(1):
                    narrow(i + 1, 1 - parity)
                    bias_out(i + 1)
                if on(2):
                    rstd_of(i + 2)
            run_skewed(eng, units, LEAD, TAIL, body, DRAIN)

        @block.scalar
        def _(eng):
            eng.wait_ge(setup_v, 1)

            def rows_turned(u):
                eng.wait_ge(hT_ps, u + 1)
                need(eng, q_ps, u)
                eng.activation(hT[:], psA[:].rearrange("p (c b t) -> p c b t", c=DC, b=2), ACT.Copy).then_inc(hT_done, 1)

            def context_turned(u):
                eng.wait_ge(cT_ps, u + 1)
                need(eng, v_ps, u)
                eng.activation(cT[:], psB[:].rearrange("p (c b t) -> p c b t", c=DC, b=2), ACT.Copy).then_inc(cT_done, 1)

            def queries(u, parity):
                eng.wait_ge(q_ps, u + 1)
                need(eng, score_ps, 8 * (u - 1))
                need(eng, qk_bf_done, u - 1)
                for odd in range(2):
                    for ch in range(DC):
                        last = eng.activation(qz[:, parity, odd, ch], psC[:, ch * 2 * P:(ch + 1) * 2 * P].rearrange("p (b t) -> p b t", b=2),
                                              ACT.Identity, bias=qb_cols[:, odd, ch:ch + 1], scale=odd_scale[:, odd:odd + 1])
                last.then_inc(q_done, 1)

            def keys(u, parity):
                eng.wait_ge(k_ps, u + 1)
                need(eng, score_ps, 8 * (u - 1))
                need(eng, qk_bf_done, u - 1)
                for ch in range(DC):
                    last = eng.activation(kT[:, parity, ch], psA[:, ch * 2 * P:(ch + 1) * 2 * P].rearrange("p (b t) -> p b t", b=2),
                                          ACT.Identity, bias=b_cols[:, 1, ch:ch + 1])
                last.then_inc(k_done, 1)

            def weights(u, j):
                eng.wait_ge(score_ps, u * 8 + j + 1)
                need(eng, pv_ps, (u - 1) * 2 + j // 4 + 1)
                eng.activation(pT[:, j // 4, j % 4], psE[j % 2][:].rearrange("p (k t) -> p k t", k=4), ACT.Exp).then_inc(p_done, 1)

            def body(i, parity, on):
                for j in range(8):
                    if on(0):
                        weights(i, j)
                    if j == 1 and on(1):
                        context_turned(i + 1)
                        rows_turned(i + 1)
                    if j == 2 and on(1):
                        keys(i + 1, 1 - parity)
                    if j == 3 and on(1):
                        queries(i + 1, 1 - parity)
            run_skewed(eng, units, LEAD, TAIL, body, DRAIN)

        @block.vector
        def _(eng):
            eng.wait_ge(w_dma, NW)
            for odd in range(2):
                eng.tensor_scalar(qb_cols[:, odd, :], b_cols[:, 0, :], odd_scale[:, odd:odd + 1], None, ALU.mult)
            eng.tensor_copy(ident_bf[:], ident[:])
            eng.memset(vz[:], 0.0)
            for odd in range(2):
                eng.memset(onez[:, odd, odd * HD:(odd + 1) * HD], 1.0)
                last = eng.memset(onez[:, odd, (1 - odd) * HD:(2 - odd) * HD], 0.0)
            last.then_inc(setup_v, 1)
            eng.wait_ge(setup_v, 1)

            def stats_of(u):
                need(eng, stats_done, u)
                for r in range(2):
                    last = eng.bn_stats(stats[:, r, :], x_all[:, u * 2 + r, :])
                last.then_inc(bn_done, 1)

            def mean_of(u):
                eng.wait_ge(bn_done, u + 1)
                need(eng, hn_done, u)
                settle(eng, dve_tally)
                for r in range(2):
                    last = eng.bn_aggr(mv[:, r, :], stats[:, r, :])
                last.then_inc(stats_done, 1)

            def norm_of(u):
                eng.wait_ge(stats_done, u + 1)
                need(eng, hT_ps, u)
                eng.wait_ge(rstd_done, u + 1)
                for r in range(2):
                    last = eng.tensor_scalar(hn[:, r, :], x_all[:, u * 2 + r, :], mv[:, r, 0:1],
                                             rstd[:, r:r + 1], ALU.subtract, ALU.mult)
                last.then_inc(hn_done, 1)

            def maxima(u, j):
                eng.wait_ge(max_ps, u * 8 + j + 1)
                need(eng, score_ps, u * 8 + j - 1)
                eng.tensor_reduce(nmax[:, j % 2, :], psM[j % 2][:].rearrange("p (k s) -> p k s", k=4), AX.X, ALU.max,
                                  negate=True).then_inc(nmax_done, 1)

            def values(u, parity):
                eng.wait_ge(v_ps, u + 1)
                need(eng, pv_ps, 2 * (u - 1))
                for r in range(2):
                    for odd in range(2):
                        heads = vz[:, parity, r].rearrange("p (n k) m -> p n k m", k=2)[:, :, odd, odd * HD:(odd + 1) * HD]
                        own = lambda t: t.rearrange("p (n k i) -> p n k i", k=2, i=HD)[:, :, odd, :]
                        last = eng.tensor_tensor(heads, own(psB[:, r * D:(r + 1) * D]), own(b_v[:, r, :]), ALU.add)
                last.then_inc(v_done, 1)

            def normalise(u, r, ch):
                eng.wait_ge(pv_ps, u * 2 + r + 1)
                need(eng, oT_done, (u * 2 + r - 1) * 2 + ch + 1)
                eng.reciprocal(rden[:, ch, :], psO[:, (2 + ch) * P:(3 + ch) * P]).then_inc(rden_done, 1)
                need(eng, wo_ps, u * 2 + r - 1)
                eng.wait_ge(rden_done, (u * 2 + r) * 2 + ch + 1)
                eng.tensor_tensor(oT[:, r, ch, :], psO[:, ch * P:(ch + 1) * P], rden[:, ch, :], ALU.mult).then_inc(oT_done, 1)

            def residual(u, r):
                eng.wait_ge(wo_ps, u * 2 + r + 1)
                eng.wait_ge(bo_done, u + 1)
                row = x_all[:, u * 2 + r, :]
                eng.tensor_tensor(row, psC[:, 2 * P:4 * P], row, ALU.add).then_inc(x2_done, 1)

            def stats3_of(u):
                eng.wait_ge(x2_done, u * 2 + 2)
                need(eng, mean3_done, u)
                settle(eng, dve_tally)
                for r in range(2):
                    last = eng.bn_stats(stats3[:, r, :], x_all[:, u * 2 + r, :])
                last.then_inc(bn3_done, 1)

            def mean3_of(u):
                eng.wait_ge(bn3_done, u + 1)
                need(eng, kept_done, u)
                settle(eng, dve_tally)
                for r in range(2):
                    last = eng.bn_aggr(mv3[:, r, :], stats3[:, r, :])
                last.then_inc(mean3_done, 1)

            def keep_of(u):
                eng.wait_ge(mean3_done, u + 1)
                eng.tensor_copy(ln3_mv[:, bass.ds(u * 2, 2), :], mv3[:]).then_inc(kept_done, 1)

            def dot_of(u):
                eng.wait_ge(prod_done, u + 1)
                eng.tensor_reduce(ln3_dot[:, bass.ds(u * 2, 2)], prod[:], AX.X, ALU.add).then_inc(dot_done, 1)

            def body(i, parity, on):
                for j in range(8):
                    if j < 7 and on(0):
                        maxima(i, j + 1)
                    if j == 7 and on(1):
                        maxima(i + 1, 0)
                    if j == 0 and on(1):
                        norm_of(i + 1)
                    if j == 1 and on(-1):
                        residual(i - 1, 0)
                    if j in (2, 3) and on(-1):
                        normalise(i - 1, 1, j - 2)
                    if j == 4:
                        if on(2):
                            stats_of(i + 2)
                        if on(-2):
                            stats3_of(i - 2)
                    if j == 5:
                        if on(2):
                            mean_of(i + 2)
                        if on(-2):
                            mean3_of(i - 2)
                    if j == 6:
                        if on(-2):
                            keep_of(i - 2)
                            dot_of(i - 2)
                        if on(-1):
                            residual(i - 1, 1)
                    if j in (6, 7) and on(0):
                        normalise(i, 0, j - 6)
                    if j == 7 and on(1):
                        values(i + 1, 1 - parity)
            run_skewed(eng, units, LEAD, TAIL, body, DRAIN)

        @block.tensor
        def _(eng):
            eng.wait_ge(w_dma, NW)
            eng.wait_ge(setup_v, 1)

            def turn_rows(u):
                eng.wait_ge(hn_done, u + 1)
                need(eng, k_done, u)
                for ch in range(DC):
                    for r in range(2):
                        last = eng.transpose(psA[:, (ch * 2 + r) * P:(ch * 2 + r + 1) * P], hn[:, r, ch * P:(ch + 1) * P], ident[:])
                last.then_inc(hT_ps, 1)

            def turn_context(u, parity):
                eng.wait_ge(ctx_dma[parity], (u - parity) * 8 + 16)
                need(eng, v_done, u)
                for ch in range(DC):
                    for r in range(2):
                        last = eng.transpose(psB[:, (ch * 2 + r) * P:(ch * 2 + r + 1) * P], ctx_in[:, parity, r, ch * P:(ch + 1) * P], ident[:])
                last.then_inc(cT_ps, 1)

            def features(out, w, src):
                for m in range(DC):
                    for ch in range(DC):
                        last = eng.matmul(out[:, m * 2 * P:(m + 1) * 2 * P], w[:, ch, m * P:(m + 1) * P], src[:, ch],
                                          start=ch == 0, stop=ch == DC - 1)
                return last

            def queries(u):
                eng.wait_ge(hT_done, u + 1)
                need(eng, x2_done, 2 * (u - 2) + 1)
                features(psC, w_q, hT).then_inc(q_ps, 1)

            def keys(u):
                eng.wait_ge(cT_done, u + 1)
                eng.wait_ge(hT_done, u + 1)
                features(psA, w_k, cT).then_inc(k_ps, 1)

            def values(u, r):
                eng.wait_ge(cT_done, u + 1)
                for ch in range(DC):
                    last = eng.matmul(psB[:, r * D:(r + 1) * D], cT[:, ch, r, :], w_v[:, ch, :], start=ch == 0, stop=ch == DC - 1)
                if r == 1:
                    last.then_inc(v_ps, 1)

            def rough_scores(u, parity, j):
                r, q = j // 4, j % 4
                rows = slice(32 * q, 32 * q + 32)
                eng.wait_ge(qk_bf_done, u + 1)
                need(eng, nmax_done, u * 8 + j - 1)
                for ch in range(DC):
                    for odd in range(2):
                        k = ch * 2 + odd
                        last = eng.matmul(psM[j % 2][:, k * P:(k + 1) * P], qz_bf[rows, parity, odd, ch, r, :], k_bf[rows, parity, ch, r, :],
                                          start=True, stop=True)
                last.then_inc(max_ps, 1)

            def scores(u, parity, j):
                r, q = j // 4, j % 4
                rows = slice(32 * q, 32 * q + 32)
                need(eng, p_done, u * 8 + j - 1)
                eng.wait_ge(nmax_done, u * 8 + j + 1)
                for k in range(4):
                    eng.matmul(psE[j % 2][:, k * P:(k + 1) * P], nmax[:, j % 2, k:k + 1].broadcast_to([P, P]), ident_bf[:],
                               start=k == 0, stop=False, skip_group_check=True)
                for ch in range(DC):
                    last = eng.matmul(psE[j % 2][:, ch * 2 * P:(ch + 1) * 2 * P], kT[rows, parity, ch, r, :], qz[rows, parity, :, ch, r, :],
                                      start=False, stop=True, skip_group_check=True)
                last.then_inc(score_ps, 1)

            def weigh(u, parity, r, ch):
                eng.wait_ge(p_done, u * 8 + r * 4 + 4)
                eng.wait_ge(v_done, u + 1)
                need(eng, oT_done, (u * 2 + r) * 2)
                for den in range(2):
                    for odd in range(2):
                        for q in range(4):
                            weight = onez[:, odd, :] if den else vz[:, parity, r, 8 * ch + 2 * q + odd, :]
                            last = eng.matmul(psO[32 * q:32 * q + 32, (2 * den + ch) * P:(2 * den + ch + 1) * P], weight,
                                              pT[:, r, q, 2 * ch + odd, :], start=odd == 0, stop=odd == 1, skip_group_check=True,
                                              tile_position=(0, 32 * q))
                if ch == 1:
                    last.then_inc(pv_ps, 1)

            def project_out(u, r, next_queries):
                eng.wait_ge(oT_done, (u * 2 + r) * 2 + 2)
                need(eng, x2_done, u * 2 + r)
                if next_queries is not None:
                    eng.wait_ge(q_done, next_queries)
                for ch in range(DC):
                    last = eng.matmul(psC[:, 2 * P:4 * P], oT[:, r, ch, :], w_o[:, ch, :], start=ch == 0, stop=ch == DC - 1)
                last.then_inc(wo_ps, 1)

            def body(i, parity, on):
                other = 1 - parity
                for j in range(8):
                    if j < 7 and on(0):
                        rough_scores(i, parity, j + 1)
                    if j == 7 and on(1):
                        rough_scores(i + 1, other, 0)
                    if on(0):
                        scores(i, parity, j)
                    if j in (0, 1) and on(-1):
                        weigh(i - 1, other, 1, j)
                    if j in (4, 5) and on(0):
                        weigh(i, parity, 0, j - 4)
                    if j == 0 and on(-1):
                        project_out(i - 1, 0, i + 1 if on(0) else None)
                    if j == 1 and on(1):
                        turn_context(i + 1, other)
                        turn_rows(i + 1)
                    if j == 2 and on(1):
                        keys(i + 1)
                    if j == 3 and on(1):
                        queries(i + 1)
                    if j == 5 and on(-1):
                        project_out(i - 1, 1, i + 2 if on(1) else None)
                    if j in (6, 7) and on(1):
                        values(i + 1, j - 6)
            run_skewed(eng, units, LEAD, TAIL, body, DRAIN)


SLOTS = 16
ROWS_PER_TILE = P // SLOTS
FF = 1024
FC = FF // P
RMS_EPS = 1e-6
LOWEST = -3.0e38
MAGIC = 12582912.0
TWO_PI = (6.28125, 1.9350051879882812e-03, 3.019916050561733e-07)
PI = 3.1415925


def route_phase(nc, hbm, rows, out, ln3_mv, ln3_dot, ident, scratch_idx):
    tiles = rows // ROWS_PER_TILE
    with ExitStack() as ctx:
        sb = lambda name, shape, dt=F32: ctx.enter_context(nc.sbuf_tensor(name, shape, dt))
        ps = lambda name, shape, dt=F32: ctx.enter_context(nc.psum_tensor(name, shape, dt))
        sem = lambda name: ctx.enter_context(nc.semaphore(name))
        router = sb("r_router", [P, D])
        router_b = sb("r_router_b", [P, 1])
        mhalf = sb("r_mhalf", [P, rows])
        iota_p = sb("r_iota_p", [P, 1])
        own_slot = sb("r_own_slot", [P, ROWS_PER_TILE])
        pos_i = sb("r_pos_i", [P, 4], I32)
        pos_f = sb("r_pos_f", [P, 4])
        pos_own = sb("r_pos_own", [P, tiles, 4])
        inv_freq = sb("r_inv_freq", [P, HD // 2])
        rsum = sb("r_rsum", [P, 1])
        w_all = sb("r_w_all", [P, rows])
        wt = sb("r_wt", [P, P])
        wt2 = sb("r_wt2", [P, P])
        idx_u = sb("r_idx_u", [P, SLOTS], U32)
        idx_f = sb("r_idx_f", [P, SLOTS])
        top = sb("r_top", [P, SLOTS])
        keep = sb("r_keep", [P, P])
        idx_b = sb("r_idx_b", [P, rows * SLOTS])
        sel = sb("r_sel", [P, rows * SLOTS])
        idx_c = sb("r_idx_c", [P, tiles])
        pos_s = sb("r_pos_s", [P, tiles])
        turns = sb("r_turns", [P, tiles, HD // 2])
        over = sb("r_over", [P, tiles, HD // 2])
        ang = sb("r_ang", [P, 2, tiles, HD // 2])
        psW = ps("r_psW", [P, 512])
        psK = ps("r_psK", [P, 512])
        psP = ps("r_psP", [P, 512])
        w_dma = sem("r_w_dma")
        dve = sem("r_dve")
        var_done = sem("r_var_done")
        rstd_done = sem("r_rstd_done")
        w_done = sem("r_w_done")
        wt_ps = sem("r_wt_ps")
        top_done = sem("r_top_done")
        keep_ps = sem("r_keep_ps")
        scratch_out = sem("r_scratch_out")
        scratch_in = sem("r_scratch_in")
        sel_done = sem("r_sel_done")
        pos_ps = sem("r_pos_ps")
        ang_done = sem("r_ang_done")
        NW = 7 * 16
        block = ctx.enter_context(nc.Block())
        scratch_w = nc.dram_tensor("scratch_w", [rows * SLOTS], F32).ap()

        @block.sync
        def _(sp):
            sp.dma_start(router[:], hbm["router"].partition_broadcast(P)).then_inc(w_dma, 16)
            sp.dma_start(router_b[:], hbm["L0_ffn_router_b"].partition_broadcast(P)).then_inc(w_dma, 16)
            sp.dma_start(iota_p[:], hbm["iota_p"]).then_inc(w_dma, 16)
            sp.dma_start(own_slot[:], hbm["own_slot"]).then_inc(w_dma, 16)
            sp.dma_start(pos_i[:], hbm["positions"]).then_inc(w_dma, 16)
            sp.dma_start(pos_own[:], hbm["pos_own"]).then_inc(w_dma, 16)
            sp.dma_start(inv_freq[:], hbm["inv_freq"]).then_inc(w_dma, 16)
            sp.wait_ge(top_done, 1)
            sp.dma_start(scratch_idx.rearrange("(b r) -> b r", r=SLOTS), idx_f[:]).then_inc(scratch_out, 16)
            sp.dma_start(scratch_w.rearrange("(b r) -> b r", r=SLOTS), top[:]).then_inc(scratch_out, 16)
            sp.wait_ge(scratch_out, 32)
            sp.dma_start(idx_b[:], scratch_idx.partition_broadcast(P)).then_inc(scratch_in, 16)
            with nc.allow_non_contiguous_dma(reason="a slot on each partition"):
                sp.dma_start(idx_c[:], scratch_idx.rearrange("(i p) -> p i", p=P)).then_inc(scratch_in, 16)
                sp.dma_start(out["w_sel"][:], scratch_w.rearrange("(i p) -> p i", p=P)).then_inc(scratch_in, 16)

        @block.gpsimd
        def _(eng):
            eng.memset(mhalf[:], -0.5).then_inc(var_done, 1)
            eng.wait_ge(var_done, 2)
            eng.tensor_tensor(out["rstd"][:], out["rstd"][:], mhalf[:], ALU.pow).then_inc(rstd_done, 1)

        @block.tensor
        def _(eng):
            eng.wait_ge(w_done, 1)
            eng.transpose(psW[:, 0:P], w_all[:], ident[:]).then_inc(wt_ps, 1)
            eng.wait_ge(top_done, 2)
            eng.transpose(psK[:, 0:P], keep[:], ident[:]).then_inc(keep_ps, 1)
            eng.wait_ge(sel_done, 1)
            for i in range(tiles):
                last = eng.matmul(psP[:, i * 4:(i + 1) * 4], sel[:, i * P:(i + 1) * P], pos_f[:], start=True, stop=True)
            last.then_inc(pos_ps, 1)

        @block.scalar
        def _(eng):
            eng.wait_ge(ang_done, 1)
            eng.activation(out["sin_cos"][:], ang[:], ACT.Sin)

        @block.vector
        def _(eng):
            c = Chain(eng, dve, 0)
            mean, var = ln3_mv[:, :, 0], ln3_mv[:, :, 1]
            eng.tensor_scalar(out["rstd"][:], var, 1.0, LN_EPS, ALU.mult, ALU.add).then_inc(var_done, 1)
            eng.wait_ge(w_dma, NW)
            c.link(eng.tensor_reduce(rsum[:], router[:], AX.X, ALU.add))
            c.link(eng.tensor_scalar(w_all[:], mean, rsum[:, 0:1], None, ALU.mult))
            c.link(eng.tensor_tensor(w_all[:], ln3_dot[:], w_all[:], ALU.subtract))
            eng.wait_ge(rstd_done, 1)
            c.link(eng.tensor_tensor(w_all[:], w_all[:], out["rstd"][:], ALU.mult))
            eng.tensor_scalar(w_all[:], w_all[:], router_b[:, 0:1], None, ALU.add).then_inc(w_done, 1)
            c.link(eng.scalar_tensor_tensor(out["shift"][:], mean, -1.0, out["rstd"][:], ALU.mult, ALU.mult))
            eng.wait_ge(wt_ps, 1)
            c.link(eng.tensor_copy(wt[:], psW[:, 0:P]))
            c.link(eng.max(top[:, 0:8], wt[:]))
            c.link(eng.max_index(idx_u[:, 0:8], top[:, 0:8], wt[:]))
            c.link(eng.match_replace(wt2[:], top[:, 0:8], wt[:], LOWEST))
            c.link(eng.max(top[:, 8:16], wt2[:]))
            c.link(eng.max_index(idx_u[:, 8:16], top[:, 8:16], wt2[:]))
            c.link(eng.tensor_copy(idx_f[:], idx_u[:]))
            eng.memset(idx_f[:, SLOTS - 1:SLOTS], -1.0).then_inc(top_done, 1)
            eng.tensor_scalar(keep[:], wt[:], top[:, SLOTS - 1:SLOTS], None, ALU.is_le).then_inc(top_done, 1)
            c.link(eng.tensor_copy(pos_f[:], pos_i[:]))
            eng.wait_ge(keep_ps, 1)
            c.link(eng.tensor_tensor(out["end_scale"][:], psK[:, 0:rows], out["rstd"][:], ALU.mult))
            eng.tensor_tensor(out["end_shift"][:], psK[:, 0:rows], out["shift"][:], ALU.mult)
            c.link(eng.tensor_scalar(out["end_scale"][:], out["end_scale"][:], 1.0, None, ALU.add))
            eng.wait_ge(scratch_in, 48)
            eng.tensor_scalar(sel[:], idx_b[:], iota_p[:, 0:1], None, ALU.is_equal).then_inc(sel_done, 1)
            c.link(eng.tensor_scalar(idx_c[:], idx_c[:], 1.0, None, ALU.add))
            c.link(eng.tensor_tensor(out["idx_own"][:], idx_c[:].unsqueeze(2).broadcast_to([P, tiles, ROWS_PER_TILE]),
                                     own_slot[:].unsqueeze(1).broadcast_to([P, tiles, ROWS_PER_TILE]), ALU.mult))
            c.link(eng.tensor_scalar(out["idx_own"][:], out["idx_own"][:], -1.0, None, ALU.add))
            eng.wait_ge(pos_ps, 1)
            c.link(eng.tensor_tensor(pos_own[:], psP[:, 0:tiles * 4].rearrange("p (i b) -> p i b", b=4), pos_own[:], ALU.mult))
            c.link(eng.tensor_reduce(pos_s[:], pos_own[:], AX.X, ALU.add))
            half = [P, tiles, HD // 2]
            c.link(eng.tensor_tensor(ang[:, 0], pos_s[:].unsqueeze(2).broadcast_to(half), inv_freq[:].unsqueeze(1).broadcast_to(half), ALU.mult))
            c.link(eng.tensor_scalar(turns[:], ang[:, 0], 1.0 / (2.0 * np.pi), MAGIC, ALU.mult, ALU.add))
            c.link(eng.tensor_scalar(turns[:], turns[:], -MAGIC, None, ALU.add))
            for part in TWO_PI:
                c.link(eng.scalar_tensor_tensor(ang[:, 0], turns[:], -part, ang[:, 0], ALU.mult, ALU.add))
            c.link(eng.tensor_scalar(ang[:, 1], ang[:, 0], np.pi / 2, None, ALU.add))
            c.link(eng.tensor_scalar(over[:], ang[:, 1], PI, -2.0 * np.pi, ALU.is_gt, ALU.mult))
            c.link(eng.tensor_tensor(ang[:, 1], ang[:, 1], over[:], ALU.add))
            eng.tensor_scalar(ang[:], ang[:], PI, -PI, ALU.min, ALU.max).then_inc(ang_done, 1)


def ffn_phase(nc, hbm, rows, r_in, x_all, ident, scratch_idx, x_out):
    tiles = rows // ROWS_PER_TILE
    with ExitStack() as ctx:
        sb = lambda name, shape, dt=F32: ctx.enter_context(nc.sbuf_tensor(name, shape, dt))
        sem = lambda name: ctx.enter_context(nc.semaphore(name))
        W2 = 2
        w_q = sb("f_w_q", [P, DC, D])
        w_k = sb("f_w_k", [P, DC, D])
        w_v = sb("f_w_v", [P, DC, D])
        w_o = sb("f_w_o", [P, DC, D])
        w_1 = sb("f_w_1", [P, DC, FF])
        w_2 = sb("f_w_2", [P, FC, D])
        ln = sb("f_ln", [P, 2, D])
        mask = sb("f_mask", [P, 4, P])
        outside = sb("f_outside", [P, 32])
        odd_scale = sb("f_odd_scale", [P, 2])
        iota_p = sb("f_iota_p", [P, 1])
        iota_f = sb("f_iota_f", [P, P])
        mhalf = sb("f_mhalf", [P, 2])
        idx_b = sb("f_idx_b", [P, W2, P])
        sel = sb("f_sel", [P, W2, P])
        sel_g = sb("f_sel_g", [P, W2, ROWS_PER_TILE, P])
        big = sb("f_big", [P, W2, 16 * P])
        xs = sb("f_xs", [P, W2, D])
        hn = sb("f_hn", [P, W2, D])
        hT = sb("f_hT", [P, W2, DC, P])
        vt = sb("f_vt", [P, W2, D])
        qk = sb("f_qk", [P, W2, 2 * D])
        qz = sb("f_qz", [P, W2, 2, DC, P])
        kT = sb("f_kT", [P, W2, DC, P])
        m1 = sb("f_m1", [P, W2, P])
        mk = sb("f_mk", [P, W2, 32])
        ss = sb("f_ss", [P, W2, 2])
        rs = sb("f_rs", [P, W2, 2])
        mx = sb("f_mx", [P, W2, HEADS])
        den = sb("f_den", [P, W2, HEADS])
        ps = ctx.enter_context(nc.psum_tensor("f_ps", [P, W2, 4, 512], F32))

        names = ("idx_dma sel_v y_a gath_ps xs_a ss_v rs_p hn_v hT_ps hT_a qkv_ps rope_v vt_a m1_ps m1_a msk_ps mk_v qkT_ps "
                 "qk_a sc_ps sc_v ex_a zero_p pt_v pv_ps o_v oT_ps oT_a wo_ps x1_v ss2_v rs2_p hn2_v h2T_ps h2T_a w1_ps "
                 "ge_a scat_v w2_ps proc_v z_a scat_ps end_v out_dma").split()
        S = {n: sem("f_" + n) for n in names}
        w_dma = sem("f_w_dma")
        dve_tally = sem("f_dve_tally")
        pool_tally = sem("f_pool_tally")
        setup_v = sem("f_setup_v")
        dve = sem("f_dve")
        pool = sem("f_pool")
        out_dma = [S["out_dma"], sem("f_out_dma1")]
        idx_dma = [S["idx_dma"], sem("f_idx_dma1")]
        NW = 14 * 16
        block = ctx.enter_context(nc.Block())

        def turns(eng, body):
            body(0)
            with eng.Fori(1, tiles // W2) as i:
                body(i)

        def done(eng, name, i, w):
            eng.wait_ge(S[name], i * W2 + w + 1)

        def used(eng, name, i, w):
            need(eng, S[name], (i - 1) * W2 + w + 1)

        def bank(w, b, lo=0, hi=512):
            return ps[:, w, b, lo:hi]

        def normed(w):
            return big[:, w].rearrange("p (j d) -> p j d", d=D)

        def weights_t(w):
            return big[:, w].rearrange("p (h q) -> p h q", q=P)

        def hidden(w):
            return big[:, w, 0:8 * P].rearrange("p (f q) -> p f q", q=P)

        def sel_t(w):
            return big[:, w, 8 * P:16 * P].rearrange("p (j s) -> p j s", s=P)

        @block.sync
        def _(sp):
            for dst, name in ((w_q, "wq"), (w_k, "wk"), (w_v, "wv"), (w_1, "w1"), (w_2, "w2")):
                sp.dma_start(dst[:], hbm["L0_ffn_" + name].rearrange("(c p) n -> p c n", p=P)).then_inc(w_dma, 16)
            sp.dma_start(w_o[:], hbm["ffn_wo_by_head"].rearrange("(c p) n -> p c n", p=P)).then_inc(w_dma, 16)
            for k in range(2):
                sp.dma_start(ln[:, k, :], hbm[f"L0_ffn_ln{k + 1}"].partition_broadcast(P)).then_inc(w_dma, 16)
            sp.dma_start(mask[:], hbm["ffn_mask"]).then_inc(w_dma, 16)
            sp.dma_start(outside[:], hbm["outside"]).then_inc(w_dma, 16)
            sp.dma_start(odd_scale[:], hbm["odd_scale"]).then_inc(w_dma, 16)
            sp.dma_start(iota_p[:], hbm["iota_p"]).then_inc(w_dma, 16)
            sp.dma_start(iota_f[:], hbm["iota_f"]).then_inc(w_dma, 16)
            sp.dma_start(mhalf[:], hbm["mhalf"]).then_inc(w_dma, 16)

            def body(i):
                for w in range(W2):
                    used(sp, "sel_v", i, w)
                    sp.dma_start(idx_b[:, w, :], scratch_idx[bass.ds((i * W2 + w) * P, P)].partition_broadcast(P)).then_inc(idx_dma[w], 16)
                for w in range(W2):
                    done(sp, "end_v", i, w)
                    first_row = (i * W2 + w) * ROWS_PER_TILE
                    sp.dma_start(x_out.rearrange("b t d -> t b d")[:, bass.ds(first_row, ROWS_PER_TILE), :],
                                 x_all[:, bass.ds(first_row, ROWS_PER_TILE), :]).then_inc(out_dma[w], 16)
            turns(sp, body)
            for w in range(W2):
                sp.wait_ge(out_dma[w], 16 * (tiles // W2))

        @block.gpsimd
        def _(eng):
            eng.wait_ge(w_dma, NW)

            def body(i):
                c = Chain(eng, pool, i * 2 * W2)
                for w in range(W2):
                    done(eng, "ss_v", i, w)
                    used(eng, "hn_v", i, w)
                    settle(eng, pool_tally)
                    c.link(eng.tensor_scalar(rs[:, w, 0:1], ss[:, w, 0:1], 1.0 / D, RMS_EPS, ALU.mult, ALU.add))
                    eng.tensor_tensor(rs[:, w, 0:1], rs[:, w, 0:1], mhalf[:, 0:1], ALU.pow).then_inc(S["rs_p"], 1)
                for w in range(W2):
                    done(eng, "gath_ps", i, w)
                    settle(eng, pool_tally)
                    eng.memset(big[:, w], 0.0).then_inc(S["zero_p"], 1)
                for w in range(W2):
                    done(eng, "ss2_v", i, w)
                    settle(eng, pool_tally)
                    c.link(eng.tensor_scalar(rs[:, w, 1:2], ss[:, w, 1:2], 1.0 / D, RMS_EPS, ALU.mult, ALU.add))
                    eng.tensor_tensor(rs[:, w, 1:2], rs[:, w, 1:2], mhalf[:, 0:1], ALU.pow).then_inc(S["rs2_p"], 1)
            turns(eng, body)

        @block.scalar
        def _(eng):
            eng.wait_ge(w_dma, NW)

            def body(i):
                def copy(name, src_done, out, src):
                    for w in range(W2):
                        done(eng, src_done, i, w)
                        eng.activation(out(w), src(w), ACT.Copy).then_inc(S[name], 1)

                for w in range(W2):
                    used(eng, "scat_ps", i, w)
                    for j in range(ROWS_PER_TILE):
                        b = (i * W2 + w) * ROWS_PER_TILE + j
                        last = eng.activation(normed(w)[:, j, :], x_all[:, b, :], ACT.Identity,
                                              bias=r_in["shift"][:, bass.ds(b, 1)], scale=r_in["rstd"][:, bass.ds(b, 1)])
                    last.then_inc(S["y_a"], 1)
                copy("m1_a", "m1_ps", lambda w: m1[:, w, :], lambda w: bank(w, 3, 384, 512))
                copy("xs_a", "gath_ps", lambda w: xs[:, w, :], lambda w: bank(w, 0, 0, D))
                for w in range(W2):
                    done(eng, "y_a", i, w)
                    for j in range(ROWS_PER_TILE):
                        b = (i * W2 + w) * ROWS_PER_TILE + j
                        last = eng.activation(x_all[:, b, :], x_all[:, b, :], ACT.Identity,
                                              bias=r_in["end_shift"][:, bass.ds(b, 1)], scale=r_in["end_scale"][:, bass.ds(b, 1)])
                    last.then_inc(S["z_a"], 1)
                copy("hT_a", "hT_ps", lambda w: hT[:, w].rearrange("p c s -> p (c s)"), lambda w: bank(w, 1, 0, D))
                copy("vt_a", "qkv_ps", lambda w: vt[:, w, :], lambda w: bank(w, 3, 0, D))
                for w in range(W2):
                    done(eng, "qkT_ps", i, w)
                    eng.activation(kT[:, w].rearrange("p c s -> p (c s)"), bank(w, 1, D, 2 * D), ACT.Copy)
                    for odd in range(2):
                        last = eng.activation(qz[:, w, odd].rearrange("p c s -> p (c s)"), bank(w, 1, 0, D), ACT.Copy, scale=odd_scale[:, odd:odd + 1])
                    last.then_inc(S["qk_a"], 1)
                for w in range(W2):
                    done(eng, "sc_v", i, w)
                    eng.activation(qk[:, w, :], qk[:, w, :], ACT.Exp).then_inc(S["ex_a"], 1)
                copy("oT_a", "oT_ps", lambda w: hT[:, w].rearrange("p c s -> p (c s)"), lambda w: bank(w, 1, 0, D))
                copy("h2T_a", "h2T_ps", lambda w: hT[:, w].rearrange("p c s -> p (c s)"), lambda w: bank(w, 3, 0, D))
                for w in range(W2):
                    done(eng, "w1_ps", i, w)
                    eng.activation(hidden(w), ps[:, w, 0:2, :].rearrange("p b (f q) -> p (b f) q", q=P), ACT.Gelu_apprx_tanh).then_inc(S["ge_a"], 1)
            turns(eng, body)

        @block.vector
        def _(eng):
            eng.memset(sel_g[:], 0.0).then_inc(setup_v, 1)
            eng.wait_ge(w_dma, NW)
            eng.wait_ge(setup_v, 1)
            steps = 16

            def body(i):
                c = Chain(eng, dve, i * steps)
                tile = lambda w: i * W2 + w
                for w in range(W2):
                    eng.wait_ge(idx_dma[w], i * 16 + 16)
                    used(eng, "msk_ps", i, w)
                    used(eng, "gath_ps", i, w)
                    c.link(eng.tensor_scalar(sel[:, w, :], idx_b[:, w, :], iota_p[:, 0:1], None, ALU.is_equal))
                    diagonal = sel_g[:, w].rearrange("p j s -> p (j s)")
                    for j in range(ROWS_PER_TILE):
                        last = eng.tensor_copy(diagonal[:, j * (P + SLOTS):j * (P + SLOTS) + SLOTS], sel[:, w, j * SLOTS:(j + 1) * SLOTS])
                    last.then_inc(S["sel_v"], 1)
                for w in range(W2):
                    done(eng, "xs_a", i, w)
                    used(eng, "h2T_ps", i, w)
                    eng.tensor_tensor_reduce(hn[:, w, :], xs[:, w, :], xs[:, w, :], 1.0, 0.0, ALU.mult, ALU.add, ss[:, w, 0:1]).then_inc(S["ss_v"], 1)
                for w in range(W2):
                    done(eng, "ss_v", i, w)
                    done(eng, "rs_p", i, w)
                    eng.scalar_tensor_tensor(hn[:, w, :], xs[:, w, :], rs[:, w, 0:1], ln[:, 0, :], ALU.mult, ALU.mult).then_inc(S["hn_v"], 1)
                for w in range(W2):
                    done(eng, "msk_ps", i, w)
                    for q in range(4):
                        g = slice(32 * q, 32 * q + 32)
                        last = eng.tensor_tensor(mk[g, w, :], ps[g, w, 3, D + 32 * q:D + 32 * q + 32], outside[g, :], ALU.add)
                    last.then_inc(S["mk_v"], 1)
                for w in range(W2):
                    done(eng, "qkv_ps", i, w)
                    rot = qz[:, w].rearrange("p o c s -> p (o c s)")
                    table = [r_in["sin_cos"][:, k, bass.ds(tile(w), 1), :].broadcast_to([P, 4 * HEADS, HD // 2]) for k in range(2)]
                    t = bank(w, 2).rearrange("p (n i) -> p n i", i=HD // 2)
                    c.step(eng.tensor_tensor(rot.rearrange("p (n i) -> p n i", i=HD // 2), t, table[0], ALU.mult))
                    n2 = c.step(eng.tensor_tensor(qk[:, w, :].rearrange("p (n i) -> p n i", i=HD // 2), t, table[1], ALU.mult))
                    c.after(n2)
                    halves = qk[:, w, :].rearrange("p (n k i) -> p n k i", k=2, i=HD // 2)
                    others = rot.rearrange("p (n k i) -> p n k i", k=2, i=HD // 2)
                    eng.tensor_tensor(halves[:, :, 0, :], halves[:, :, 0, :], others[:, :, 1, :], ALU.subtract)
                    eng.tensor_tensor(halves[:, :, 1, :], halves[:, :, 1, :], others[:, :, 0, :], ALU.add).then_inc(S["rope_v"], 1)
                for w in range(W2):
                    done(eng, "sc_ps", i, w)
                    s = qk[:, w, :].rearrange("p (h k) -> p h k", k=32)
                    for q in range(4):
                        g = slice(32 * q, 32 * q + 32)
                        src = ps[g, w, :, :].rearrange("p b (h k) -> p (b h) k", k=P)[:, :, 32 * q:32 * q + 32]
                        n = c.step(eng.tensor_tensor(s[g], src, mk[g, w, :].unsqueeze(1).broadcast_to([32, HEADS, 32]), ALU.add)) if q == 3 else \
                            eng.tensor_tensor(s[g], src, mk[g, w, :].unsqueeze(1).broadcast_to([32, HEADS, 32]), ALU.add)
                    c.after(n)
                    c.link(eng.tensor_reduce(mx[:, w, :], s, AX.X, ALU.max))
                    eng.tensor_tensor(s, s, mx[:, w, :].unsqueeze(2).broadcast_to([P, HEADS, 32]), ALU.subtract).then_inc(S["sc_v"], 1)
                for w in range(W2):
                    done(eng, "ex_a", i, w)
                    done(eng, "zero_p", i, w)
                    s = qk[:, w, :].rearrange("p (h k) -> p h k", k=32)
                    used(eng, "o_v", i, w)
                    n = c.step(eng.tensor_reduce(den[:, w, :], s, AX.X, ALU.add))
                    for q in range(4):
                        g = slice(32 * q, 32 * q + 32)
                        last = eng.transpose(weights_t(w)[g, :, 32 * q:32 * q + 32], s[g])
                    last.then_inc(S["pt_v"], 1)
                    c.after(n)
                    c.link(eng.reciprocal(den[:, w, :], den[:, w, :]))
                for w in range(W2):
                    done(eng, "pv_ps", i, w)
                    eng.tensor_tensor(qz[:, w, 0].rearrange("p c s -> p (c s)").rearrange("p (h i) -> p h i", h=HEADS), bank(w, 0, 0, D).rearrange("p (h i) -> p h i", h=HEADS),
                                      den[:, w, :].unsqueeze(2).broadcast_to([P, HEADS, HD]), ALU.mult).then_inc(S["o_v"], 1)
                for w in range(W2):
                    done(eng, "pv_ps", i, w)
                    shape = [P, ROWS_PER_TILE, P]
                    eng.tensor_tensor(sel_t(w), iota_f[:].unsqueeze(1).broadcast_to(shape),
                                      r_in["idx_own"][:, bass.ds(tile(w), 1), :].rearrange("p a j -> p (a j)").unsqueeze(2).broadcast_to(shape), ALU.is_equal).then_inc(S["scat_v"], 1)
                for w in range(W2):
                    done(eng, "wo_ps", i, w)
                    eng.tensor_tensor(kT[:, w].rearrange("p c s -> p (c s)"), bank(w, 2, 0, D), xs[:, w, :], ALU.add).then_inc(S["x1_v"], 1)
                for w in range(W2):
                    done(eng, "x1_v", i, w)
                    x1 = kT[:, w].rearrange("p c s -> p (c s)")
                    eng.tensor_tensor_reduce(hn[:, w, :], x1, x1, 1.0, 0.0, ALU.mult, ALU.add, ss[:, w, 1:2]).then_inc(S["ss2_v"], 1)
                for w in range(W2):
                    done(eng, "ss2_v", i, w)
                    done(eng, "rs2_p", i, w)
                    eng.scalar_tensor_tensor(hn[:, w, :], kT[:, w].rearrange("p c s -> p (c s)"), rs[:, w, 1:2], ln[:, 1, :], ALU.mult, ALU.mult).then_inc(S["hn2_v"], 1)
                for w in range(W2):
                    done(eng, "w2_ps", i, w)
                    c.link(eng.tensor_tensor(xs[:, w, :], bank(w, 2, D, 2 * D), kT[:, w].rearrange("p c s -> p (c s)"), ALU.add))
                    eng.tensor_scalar(xs[:, w, :], xs[:, w, :], r_in["w_sel"][:, bass.ds(tile(w), 1)], None, ALU.mult).then_inc(S["proc_v"], 1)
                for w in range(W2):
                    done(eng, "scat_ps", i, w)
                    done(eng, "z_a", i, w)
                    first_row = tile(w) * ROWS_PER_TILE
                    x_rows = x_all[:, bass.ds(first_row, ROWS_PER_TILE), :].rearrange("p j d -> p (j d)")
                    eng.tensor_tensor(x_rows, ps[:, w].rearrange("p b n -> p (b n)"), x_rows, ALU.add).then_inc(S["end_v"], 1)
                assert c.n == steps, c.n
            turns(eng, body)

        @block.tensor
        def _(eng):
            eng.wait_ge(w_dma, NW)

            def body(i):
                first = isinstance(i, int)
                for w in range(W2):
                    done(eng, "sel_v", i, w)
                    used(eng, "end_v", i, w)
                    alone = 3 if first and w == 0 else 0
                    for b in range(alone):
                        eng.matmul(bank(w, 3, 384 + b * SLOTS, 384 + (b + 1) * SLOTS), mask[:, b, :], sel[:, w, b * SLOTS:(b + 1) * SLOTS], start=True, stop=True)
                    eng.matmul(bank(w, 3, 384 + alone * SLOTS, 512), mask[:, 3, :], sel[:, w, alone * SLOTS:P], start=True, stop=True).then_inc(S["m1_ps"], 1)
                for w in range(W2):
                    done(eng, "y_a", i, w)
                    for j in range(ROWS_PER_TILE):
                        last = eng.matmul(bank(w, 0, 0, D), sel_g[:, w, j, :], normed(w)[:, j, :], start=j == 0, stop=j == ROWS_PER_TILE - 1)
                    last.then_inc(S["gath_ps"], 1)
                for w in range(W2):
                    done(eng, "m1_a", i, w)
                    eng.matmul(bank(w, 3, D, D + P), m1[:, w, :], sel[:, w, :], start=True, stop=True).then_inc(S["msk_ps"], 1)
                for w in range(W2):
                    done(eng, "hn_v", i, w)
                    for ch in range(DC):
                        last = eng.transpose(bank(w, 1, ch * P, (ch + 1) * P), hn[:, w, ch * P:(ch + 1) * P], ident[:])
                    last.then_inc(S["hT_ps"], 1)
                for w in range(W2):
                    done(eng, "hT_a", i, w)
                    done(eng, "mk_v", i, w)
                    for wt, out in ((w_q, bank(w, 2, 0, D)), (w_k, bank(w, 2, D, 2 * D)), (w_v, bank(w, 3, 0, D))):
                        for ch in range(DC):
                            last = eng.matmul(out, hT[:, w, ch, :], wt[:, ch, :], start=ch == 0, stop=ch == DC - 1)
                    last.then_inc(S["qkv_ps"], 1)
                for w in range(W2):
                    done(eng, "rope_v", i, w)
                    for half in range(2):
                        for ch in range(DC):
                            k = half * 2 + ch
                            last = eng.transpose(bank(w, 1, k * P, (k + 1) * P), qk[:, w, k * P:(k + 1) * P], ident[:])
                    last.then_inc(S["qkT_ps"], 1)
                for w in range(W2):
                    done(eng, "qk_a", i, w)
                    done(eng, "vt_a", i, w)
                    for ch in range(DC):
                        for odd in range(2):
                            for q in range(4):
                                rows_q = slice(32 * q, 32 * q + 32)
                                k = ch * 2 + odd
                                last = eng.matmul(bank(w, q, k * P, (k + 1) * P), qz[rows_q, w, odd, ch, :], kT[rows_q, w, ch, :], start=True, stop=True)
                    last.then_inc(S["sc_ps"], 1)
                for w in range(W2):
                    done(eng, "pt_v", i, w)
                    for q in range(4):
                        for ch in range(DC):
                            for odd in range(2):
                                h, at = 8 * ch + 2 * q + odd, 4 * q + 2 * ch + odd
                                last = eng.matmul(bank(w, 0, at * HD, (at + 1) * HD), weights_t(w)[:, at, :], vt[:, w, h * HD:(h + 1) * HD], start=True, stop=True)
                    last.then_inc(S["pv_ps"], 1)
                for w in range(W2):
                    done(eng, "o_v", i, w)
                    o = qz[:, w, 0]
                    for ch in range(DC):
                        last = eng.transpose(bank(w, 1, ch * P, (ch + 1) * P), o[:, ch, :], ident[:])
                    last.then_inc(S["oT_ps"], 1)
                for w in range(W2):
                    done(eng, "oT_a", i, w)
                    for ch in range(DC):
                        last = eng.matmul(bank(w, 2, 0, D), hT[:, w, ch, :], w_o[:, ch, :], start=ch == 0, stop=ch == DC - 1)
                    last.then_inc(S["wo_ps"], 1)
                for w in range(W2):
                    done(eng, "hn2_v", i, w)
                    for ch in range(DC):
                        last = eng.transpose(bank(w, 3, ch * P, (ch + 1) * P), hn[:, w, ch * P:(ch + 1) * P], ident[:])
                    last.then_inc(S["h2T_ps"], 1)
                for w in range(W2):
                    done(eng, "h2T_a", i, w)
                    for f in range(FC):
                        for ch in range(DC):
                            last = eng.matmul(bank(w, f // 4, (f % 4) * P, (f % 4 + 1) * P), w_1[:, ch, f * P:(f + 1) * P], hT[:, w, ch, :],
                                              start=ch == 0, stop=ch == DC - 1)
                    last.then_inc(S["w1_ps"], 1)
                for w in range(W2):
                    done(eng, "ge_a", i, w)
                    for f in range(FC):
                        last = eng.matmul(bank(w, 2, D, 2 * D), hidden(w)[:, f, :], w_2[:, f, :], start=f == 0, stop=f == FC - 1)
                    last.then_inc(S["w2_ps"], 1)
                for w in range(W2):
                    done(eng, "proc_v", i, w)
                    done(eng, "scat_v", i, w)
                    for j in range(ROWS_PER_TILE):
                        last = eng.matmul(bank(w, j // 2, (j % 2) * D, (j % 2 + 1) * D), sel_t(w)[:, j, :], xs[:, w, :], start=True, stop=True)
                    last.then_inc(S["scat_ps"], 1)
            turns(eng, body)


def program(nc, hbm, x_out):
    rows = hbm["x"].shape[0]
    tiles = rows // ROWS_PER_TILE
    with ExitStack() as ctx:
        sb = lambda name, shape: ctx.enter_context(nc.sbuf_tensor(name, shape, F32))
        x_all = sb("x_all", [P, rows, D])
        ident = sb("ident", [P, P])
        ln3_mv = sb("ln3_mv", [P, rows, 2])
        ln3_dot = sb("ln3_dot", [P, rows])
        gla_phase(nc, rows // 2, hbm, x_all, ident)
        xattn_phase(nc, rows // 2, hbm, x_all, ident, ln3_mv, ln3_dot)
        routed = {
            "rstd": sb("rstd3", [P, rows]), "shift": sb("shift3", [P, rows]),
            "end_scale": sb("end_scale", [P, rows]), "end_shift": sb("end_shift", [P, rows]),
            "idx_own": sb("idx_own", [P, tiles, ROWS_PER_TILE]), "w_sel": sb("w_sel", [P, tiles]),
            "sin_cos": sb("sin_cos", [P, 2, tiles, HD // 2]),
        }
        scratch_idx = nc.dram_tensor("scratch_idx", [rows * SLOTS], F32).ap()
        route_phase(nc, hbm, rows, routed, ln3_mv, ln3_dot, ident, scratch_idx)
        ffn_phase(nc, hbm, rows, routed, x_all, ident, scratch_idx, x_out)


def shape_constants(rows):
    i = np.arange(P)
    split = np.zeros((P, P), np.int64)
    for k in range(7):
        split[((i[:, None] ^ i[None, :]) >> k) > 0] = 1 << k
    before = i[:, None] < i[None, :]
    near = [(split == h) & before for h in (8, 4, 2, 1)] + [split == 0]
    own = i[:, None] // SLOTS == np.arange(ROWS_PER_TILE)[None, :]
    pos_own = np.zeros((P, rows // ROWS_PER_TILE, 4), np.float32)
    pos_own[:, 1:, 3] = 1.0
    pos_own[i, 0, np.minimum(i // SLOTS, 3)] = 1.0
    k = np.arange(32)
    same = (k[None, :] // SLOTS == (i[:, None] // SLOTS) % 2) & (k[None, :] % SLOTS != SLOTS - 1)
    freq = (1.0 / np.float32(10000.0) ** (np.arange(0, HD, 2, dtype=np.float32) / np.float32(HD))).astype(np.float32)
    odd = (i // HD) % 2
    return {
        "ident": np.eye(P, dtype=np.float32),
        "mask_far": ((split >= 16) & before).astype(np.float32),
        "mask_near": np.ascontiguousarray(np.stack(near, 1).astype(np.int32)),
        "odd_scale": np.stack([(odd == 0) * HD ** -0.5, (odd == 1) * HD ** -0.5], 1).astype(np.float32),
        "mhalf": np.full((P, 2), -0.5, np.float32),
        "iota_p": i[:, None].astype(np.float32),
        "iota_f": np.ascontiguousarray(np.broadcast_to(i[None, :], (P, P)).astype(np.float32)),
        "own_slot": own.astype(np.float32),
        "pos_own": pos_own,
        "outside": np.where(same, 0.0, -1e30).astype(np.float32),
        "inv_freq": np.ascontiguousarray(np.broadcast_to(freq[None, :], (P, HD // 2))),
    }


def laid_out(inputs):
    a = {k: np.asarray(v) for k, v in inputs.items()}
    rows = a["x"].shape[0]
    names = ["x", "ctx_1024"] + [f"L0_attn_{n}" for n in ("Wq", "Wk", "Wg", "Wv", "Wo", "bv", "bo")]
    names += [f"L0_xattn_{n}" for n in ("Wq", "Wk", "Wv", "Wo", "bv", "bo")]
    names += [f"L0_ffn_{n}" for n in ("wq", "wk", "wv", "w1", "w2", "ln1", "ln2", "router_b")]
    out = {n: a[n] for n in names}
    out["router"] = a["L0_ffn_router_w"].reshape(D)
    out["attn_bias_cols"] = np.stack([np.tile(a[f"L0_attn_b{n}"], 2) for n in "qkg"], 1)
    out["xattn_bias_cols"] = np.stack([a[f"L0_xattn_b{n}"].reshape(DC, P).T for n in "qk"], 1)
    out["ffn_wo_by_head"] = a["L0_ffn_wo"].reshape(DC, 4, 2, HD, D).transpose(1, 0, 2, 3, 4).reshape(D, D)
    out["ffn_mask"] = a["L0_ffn_attention_mask"][:, 0, :P, :P].transpose(1, 0, 2)
    out["positions"] = a["L0_ffn_position_ids"][:, :P].T
    out.update(shape_constants(rows))
    return {k: np.ascontiguousarray(v) for k, v in out.items()}


def kernel(**inputs):
    import concourse.bacc as bacc
    from concourse.bass_utils import run_bass_kernel_spmd

    nc = bacc.Bacc("TRN2", target_bir_lowering=False, num_devices=1)
    arrays = laid_out(inputs)
    hbm = {k: nc.dram_tensor(f"in_{k}", a.shape, mybir.dt.from_np(a.dtype), kind="ExternalInput").ap() for k, a in arrays.items()}
    x_out = nc.dram_tensor("out_x", arrays["x"].shape, F32, kind="ExternalOutput").ap()
    program(nc, hbm, x_out)
    r = run_bass_kernel_spmd(nc, [{f"in_{k}": a for k, a in arrays.items()}], core_ids=[0])
    return r.results[0]["out_x"]
```

```python
from contextlib import ExitStack

import numpy as np
import concourse.bass as bass
from concourse import mybir

F32 = mybir.dt.float32
BF16 = mybir.dt.bfloat16
I32 = mybir.dt.int32
U32 = mybir.dt.uint32
ALU = mybir.AluOpType
ACT = mybir.ActivationFunctionType
AX = mybir.AxisListType

P = 128
D = 256
DC = D // P
KV = 64
LN_EPS = 1e-5


def need(eng, sem, value):
    if isinstance(value, int) and value <= 0:
        return
    eng.wait_ge(sem, value)


def run_units(eng, units, ahead, body):
    for u in range(2):
        body(u, u % 2, False)
    with eng.Fori(1, units // 2 - 1) as i:
        for parity in range(2):
            body(i * 2 + parity, parity, False)
    for u in range(units - 2, units):
        body(u, u % 2, u + ahead >= units)


def run_skewed(eng, units, lead, tail, body, drain=1):
    known = lambda i: lambda k: 0 <= i + k < units
    first = 2 * drain
    end = units - tail - tail % 2
    for i in range(-lead, first):
        body(i, i % 2, known(i))
    with eng.Fori(first // 2, end // 2) as turn:
        for parity in range(2):
            body(turn * 2 + parity, parity, lambda k: True)
    for i in range(end, units + drain):
        body(i, i % 2, known(i))


def settle(eng, tally):
    eng.sem_inc(tally, 1)


class Chain:

    def __init__(self, eng, sem, base, value=0):
        self.eng, self.sem, self.base, self.n = eng, sem, base, value

    def step(self, instruction):
        instruction.then_inc(self.sem, 1)
        self.n += 1
        return self.n

    def after(self, n):
        self.eng.wait_ge(self.sem, self.base + n)

    def link(self, instruction):
        self.after(self.step(instruction))


def gla_phase(nc, units, hbm, x_all, ident, load_after):
    with ExitStack() as ctx:
        sb = lambda name, shape, dt=F32: ctx.enter_context(nc.sbuf_tensor(name, shape, dt))
        ps = lambda name, shape, dt=F32: ctx.enter_context(nc.psum_tensor(name, shape, dt))
        sem = lambda name: ctx.enter_context(nc.semaphore(name))

        w_qkg = sb("g_w_qkg", [P, 3, DC, KV])
        w_v = sb("g_w_v", [P, DC, KV])
        w_o = sb("g_w_o", [KV + 1, D])
        b_qkg = sb("g_b_qkg", [P, 3])
        nb_kg = sb("g_nb_kg", [P, 2])
        b_v = sb("g_b_v", [P, 2, KV])
        mask_far = sb("g_mask_far", [P, P])
        mask_near = sb("g_mask_near", [P, 5, P], I32)
        mhalf = sb("g_mhalf", [P, 2])
        stats = sb("g_stats", [P, 2, 6])
        mv = sb("g_mv", [P, 2, 2, 2])
        vare = sb("g_vare", [P, 2, 2])
        rstd = sb("g_rstd", [P, 2, 2])
        minus = sb("g_minus", [P, 2])
        neg_mean = sb("g_neg_mean", [P, 2, 2])
        shift = sb("g_shift", [P, 2, 2])
        hn = sb("g_hn", [P, 2, 2, D])
        hT = sb("g_hT", [P, 2, DC, 2, P])
        ekg = sb("g_ekg", [P, 2, 2 * P])
        XW = 4 * P + 6 * 2 * P
        X = sb("g_X", [P, 2, XW])
        EB = [P // h for h in (1, 2, 4, 8, 16, 32)]
        blk = {h: sb(f"g_blk{h}", [P, 2, P // h]) for h in (2, 4, 8, 16, 32)}
        fac = {h: sb(f"g_fac{h}", [P, 2, 2 * (P // h)]) for h in (1, 2, 4, 8, 16, 32)}
        A = sb("g_A", [P, 2, 2, P])
        v = sb("g_v", [P, 2, 2, KV])
        oT = sb("g_oT", [KV + 1, 2, 2, P])

        psT = ps("g_psT", [P, 512])
        psP = ps("g_psP", [P, 512])
        psL = ps("g_psL", [P, 2, 2, 512])
        psO = ps("g_psO", [P, 512])
        psW = ps("g_psW", [P, 512])

        x_dma = [sem("g_x_even"), sem("g_x_odd")]
        w_dma = sem("g_w_dma")
        ident_dma = sem("g_ident_dma")
        dve_tally = sem("g_dve_tally")
        pool_tally = sem("g_pool_tally")
        setup_v = sem("g_setup_v")
        setup_a = sem("g_setup_a")
        setup_p = sem("g_setup_p")
        vare_done = sem("g_vare_done")
        pow_done = sem("g_pow_done")
        bn_done = sem("g_bn_done")
        exp_plus_one = sem("g_exp_plus_one")
        level_done = sem("g_level_done")
        mask_step = sem("g_mask_step")
        product_done = sem("g_product_done")
        qg_done = sem("g_qg_done")
        stats_done = sem("g_stats_done")
        rstd_done = sem("g_rstd_done")
        hn_done = sem("g_hn_done")
        hT_ps = sem("g_hT_ps")
        hT_done = sem("g_hT_done")
        proj_ps = sem("g_proj_ps")
        kg_exp = sem("g_kg_exp")
        q_done = sem("g_q_done")
        gates_done = sem("g_gates_done")
        blk_done = sem("g_blk_done")
        v_done = sem("g_v_done")
        X_done = sem("g_X_done")
        L_ps = sem("g_L_ps")
        A_done = sem("g_A_done")
        O_ps = sem("g_O_ps")
        oT_done = sem("g_oT_done")
        W_ps = sem("g_W_ps")
        x1_done = sem("g_x1_done")

        def load_consts(sp):
            sp.dma_start(ident[:], hbm["ident"]).then_inc(ident_dma, 16)
            for dst, src in (
                (w_qkg[:, 0], hbm["L0_attn_Wq"]), (w_qkg[:, 1], hbm["L0_attn_Wk"]),
                (w_qkg[:, 2], hbm["L0_attn_Wg"]), (w_v[:], hbm["L0_attn_Wv"]),
            ):
                sp.dma_start(dst, src.rearrange("(c p) n -> p c n", p=P)).then_inc(w_dma, 16)
            sp.dma_start(w_o[0:KV, :], hbm["L0_attn_Wo"]).then_inc(w_dma, 16)
            sp.dma_start(w_o[KV:KV + 1, :], hbm["L0_attn_bo"].rearrange("(a n) -> a n", a=1)).then_inc(w_dma, 16)
            sp.dma_start(b_qkg[:], hbm["attn_bias_cols"]).then_inc(w_dma, 16)
            for r in range(2):
                sp.dma_start(b_v[:, r, :], hbm["L0_attn_bv"].partition_broadcast(P)).then_inc(w_dma, 16)
            sp.dma_start(mask_far[:], hbm["mask_far"]).then_inc(w_dma, 16)
            sp.dma_start(mask_near[:], hbm["mask_near"]).then_inc(w_dma, 16)
        NW = 11 * 16

        block = ctx.enter_context(nc.Block())

        @block.sync
        def _(sp):
            x_src = hbm["x"].rearrange("b t d -> t b d")

            def body(u, parity, last):
                need(sp, x_dma[parity], (u - parity) * 8)
                sp.dma_start(x_all[:, bass.ds(u * 2, 2), :], x_src[:, bass.ds(u * 2, 2), :]).then_inc(x_dma[parity], 16)
                if isinstance(u, int) and u == 0:
                    load_consts(sp)
            run_units(sp, units, 0, body)
            load_after(sp)

        LEAD, TAIL = 4, 4

        @block.gpsimd
        def _(eng):
            eng.memset(minus[:], -1.0)
            eng.memset(mhalf[:], -0.5).then_inc(setup_p, 1)
            eng.wait_ge(setup_p, 1)
            eng.wait_ge(setup_v, 3)

            def rstd_of(u, parity):
                eng.wait_ge(stats_done, u + 1)
                need(eng, hn_done, u - 1)
                settle(eng, pool_tally)
                eng.tensor_scalar(vare[:, parity, :], mv[:, parity, :, 1], 1.0, LN_EPS, ALU.mult, ALU.add).then_inc(vare_done, 1)
                eng.tensor_tensor(neg_mean[:, parity, :], mv[:, parity, :, 0], minus[:], ALU.mult)
                eng.wait_ge(vare_done, u + 1)
                eng.tensor_tensor(rstd[:, parity, :], vare[:, parity, :], mhalf[:], ALU.pow).then_inc(pow_done, 1)
                eng.wait_ge(pow_done, u + 1)
                eng.tensor_tensor(shift[:, parity, :], neg_mean[:, parity, :], rstd[:, parity, :], ALU.mult).then_inc(rstd_done, 1)

            def blocks_of(u, parity):
                eng.wait_ge(gates_done, u + 1)
                need(eng, X_done, u - 1)
                E = X[:, parity, 2 * P:3 * P]
                for k, h in enumerate((1, 2, 4, 8, 16, 32)):
                    nb = P // h
                    dst = fac[h][:, parity, 1:2 * nb - 1].rearrange("p (i r) -> p i r", i=2)[:, :, 0:nb - 1:2]
                    if h < 32:
                        E2 = blk[2 * h][:, parity, :]
                        eng.tensor_tensor(E2, E[:, 0:nb:2], E[:, 1:nb:2], ALU.mult).then_inc(product_done, 1)
                    settle(eng, pool_tally)
                    eng.tensor_scalar(dst, E.rearrange("p (j i) -> p i j", i=2), 1.0, 0.0, ALU.mult, ALU.add).then_inc(blk_done, 1)
                    if h < 32:
                        eng.wait_ge(product_done, u * 5 + k + 1)
                        E = E2

            def body(i, parity, on):
                if on(1):
                    blocks_of(i + 1, 1 - parity)
                if on(4):
                    rstd_of(i + 4, parity)
            run_skewed(eng, units, LEAD, TAIL, body)

        @block.scalar
        def _(eng):

            def norm_of(u, parity):
                need(eng, hT_ps, u - 1)
                eng.wait_ge(rstd_done, u + 1)
                for r in range(2):
                    last = eng.activation(hn[:, parity, r, :], x_all[:, u * 2 + r, :], ACT.Identity,
                                          bias=shift[:, parity, r:r + 1], scale=rstd[:, parity, r:r + 1])
                last.then_inc(hn_done, 1)

            def gates_of(u, parity):
                eng.wait_ge(proj_ps, u + 1)
                need(eng, gates_done, u - 1)
                eng.activation(ekg[:, parity, 0:P], psP[:, P:2 * P], ACT.Exp, bias=nb_kg[:, 0:1], scale=-1.0)
                eng.activation(ekg[:, parity, P:2 * P], psP[:, 2 * P:3 * P], ACT.Exp, bias=nb_kg[:, 1:2], scale=-1.0).then_inc(kg_exp, 1)
                need(eng, L_ps, u - 1)
                eng.activation(X[:, parity, 3 * P:4 * P], psP[:, 0:P], ACT.Identity, bias=b_qkg[:, 0:1]).then_inc(q_done, 1)
                eng.wait_ge(kg_exp, u + 1)
                eng.activation(ekg[:, parity], ekg[:, parity], ACT.Copy, bias=1.0).then_inc(exp_plus_one, 1)

            def hT_of(u, parity):
                eng.wait_ge(hT_ps, u + 1)
                need(eng, proj_ps, u - 1)
                eng.activation(hT[:, parity], psT[:].rearrange("p (c b t) -> p c b t", c=DC, b=2), ACT.Copy).then_inc(hT_done, 1)

            def outputs_of(u, parity):
                eng.wait_ge(O_ps, u + 1)
                need(eng, W_ps, u - 1)
                eng.activation(oT[0:KV, parity], psO[0:KV, 0:2 * P].rearrange("p (b t) -> p b t", b=2), ACT.Copy).then_inc(oT_done, 1)

            def body(i, parity, on):
                if on(3):
                    norm_of(i + 3, 1 - parity)
                if isinstance(i, int) and i == -2:
                    eng.wait_ge(w_dma, NW)
                    eng.activation(nb_kg[:], b_qkg[:, 1:3], ACT.Copy, scale=-1.0).then_inc(setup_a, 1)
                    eng.wait_ge(setup_a, 1)
                if on(2):
                    gates_of(i + 2, parity)
                if on(3):
                    hT_of(i + 3, 1 - parity)
                if on(0):
                    outputs_of(i, parity)
            run_skewed(eng, units, LEAD, TAIL, body)

        @block.vector
        def _(eng):
            for h in (1, 2, 4, 8, 16, 32):
                last = eng.memset(fac[h][:], 1.0)
                if h in (8, 32):
                    last.then_inc(setup_v, 1)
            eng.memset(oT[KV:KV + 1], 1.0).then_inc(setup_v, 1)

            def v_of(u, parity):
                eng.wait_ge(q_done, u + 1)
                need(eng, O_ps, u - 1)
                eng.tensor_tensor(v[:, parity], psP[:, 3 * P:4 * P].rearrange("p (b n) -> p b n", b=2), b_v[:], ALU.add).then_inc(v_done, 1)

            def gates_of(u, parity):
                need(eng, L_ps, u - 1)
                need(eng, blk_done, 6 * (u - 1))
                eng.wait_ge(exp_plus_one, u + 1)
                eng.reciprocal(X[:, parity, P:3 * P], ekg[:, parity, :]).then_inc(gates_done, 1)

            def gated_query_of(u, parity):
                eng.wait_ge(gates_done, u + 1)
                eng.wait_ge(q_done, u + 1)
                eng.tensor_tensor(X[:, parity, 0:P], X[:, parity, 3 * P:4 * P], X[:, parity, 2 * P:3 * P], ALU.mult).then_inc(qg_done, 1)

            def level_of(u, parity, k):
                h = 1 << k
                nb = P // h
                src, dst = 4 * P + (k - 1) * 2 * P if k else 0, 4 * P + k * 2 * P
                eng.wait_ge(blk_done, u * 6 + k + 1)
                if k:
                    eng.wait_ge(level_done, u * 5 + k)
                else:
                    eng.wait_ge(qg_done, u + 1)
                lo, hi = (0, 2 * nb) if h < 32 else (nb // 2, nb + nb // 2)
                a = X[:, parity, src + lo * h:src + hi * h].rearrange("p (n h) -> p n h", h=h)
                o = X[:, parity, dst + lo * h:dst + hi * h].rearrange("p (n h) -> p n h", h=h)
                f = fac[h][:, parity, lo:hi].unsqueeze(2).broadcast_to([P, hi - lo, h])
                eng.tensor_tensor(o, a, f, ALU.mult).then_inc(level_done if k < 5 else X_done, 1)

            def stats_of(u, parity, load_parity):
                eng.wait_ge(x_dma[load_parity], (u - load_parity) * 8 + 16)
                need(eng, stats_done, u)
                settle(eng, dve_tally)
                for r in range(2):
                    last = eng.bn_stats(stats[:, r, :], x_all[:, u * 2 + r, :])
                last.then_inc(bn_done, 1)

            def mean_of(u, parity):
                eng.wait_ge(bn_done, u + 1)
                need(eng, hn_done, u - 1)
                settle(eng, dve_tally)
                for r in range(2):
                    last = eng.bn_aggr(mv[:, parity, r, :], stats[:, r, :])
                last.then_inc(stats_done, 1)

            def mask_of(u, parity, k):
                out = A[:, parity]
                if k == 0:
                    eng.wait_ge(L_ps, u + 1)
                    need(eng, O_ps, u - 1)
                    eng.tensor_tensor(out, psL[:, :, 0, 0:P], mask_far[:].unsqueeze(1).broadcast_to([P, 2, P]), ALU.mult).then_inc(mask_step, 1)
                    return
                tile = psL[:, :, 0, k * P:(k + 1) * P] if k < 4 else psL[:, :, 1, (k - 4) * P:(k - 3) * P]
                eng.wait_ge(mask_step, u * 5 + k)
                settle(eng, dve_tally)
                eng.copy_predicated(out, mask_near[:, k - 1, :].unsqueeze(1).broadcast_to([P, 2, P]), tile).then_inc(mask_step if k < 5 else A_done, 1)

            def residual_of(u):
                eng.wait_ge(W_ps, u + 1)
                eng.tensor_tensor(x_all[:, bass.ds(u * 2, 2), :], psW[:].rearrange("p (b d) -> p b d", b=2),
                                  x_all[:, bass.ds(u * 2, 2), :], ALU.add).then_inc(x1_done, 1)

            def body(i, parity, on):
                other = 1 - parity
                if isinstance(i, int) and i == -1:
                    eng.wait_ge(w_dma, NW)
                if on(1):
                    v_of(i + 1, other)
                    gates_of(i + 1, other)
                if on(4):
                    stats_of(i + 4, parity, parity)
                if on(1):
                    gated_query_of(i + 1, other)
                if on(4):
                    mean_of(i + 4, parity)
                for k in range(6):
                    if on(0):
                        mask_of(i, parity, k)
                    if on(1):
                        level_of(i + 1, other, k)
                if on(-1):
                    residual_of(i - 1)
            run_skewed(eng, units, LEAD, TAIL, body)

        @block.tensor
        def _(eng):
            eng.wait_ge(ident_dma, 16)
            eng.wait_ge(setup_v, 3)

            def transposes(u, parity):
                eng.wait_ge(hn_done, u + 1)
                need(eng, hT_done, u)
                for ch in range(DC):
                    for r in range(2):
                        last = eng.transpose(psT[:, (ch * 2 + r) * P:(ch * 2 + r + 1) * P],
                                             hn[:, parity, r, ch * P:(ch + 1) * P], ident[:])
                last.then_inc(hT_ps, 1)

            def project(u, parity):
                eng.wait_ge(hT_done, u + 1)
                need(eng, kg_exp, u)
                need(eng, q_done, u)
                need(eng, v_done, u)
                for r in range(2):
                    for f in range(3):
                        for ch in range(DC):
                            eng.matmul(psP[r * KV:(r + 1) * KV, f * P:(f + 1) * P], w_qkg[:, f, ch, :],
                                       hT[:, parity, ch, r, :], start=ch == 0, stop=ch == DC - 1)
                for r in range(2):
                    for ch in range(DC):
                        last = eng.matmul(psP[:, 3 * P + r * KV:3 * P + (r + 1) * KV], hT[:, parity, ch, r, :],
                                          w_v[:, ch, :], start=ch == 0, stop=ch == DC - 1)
                last.then_inc(proj_ps, 1)

            def levels(u, parity):
                eng.wait_ge(X_done, u + 1)
                need(eng, A_done, u)
                far = 4 * P + 3 * 2 * P

                def pair(r, query, key, s, t, out):
                    rows = slice(r * KV, (r + 1) * KV)
                    return eng.matmul(out[s, t], X[rows, parity, key + s.start:key + s.stop],
                                      X[rows, parity, query + t.start:query + t.stop], start=True, stop=True)
                every = slice(0, P)
                for k, base in enumerate((far, 4 * P + 2 * 2 * P, 4 * P + 2 * P, 4 * P)):
                    for r in range(2):
                        pair(r, base, base + P, every, every, psL[:, r, 0, k * P:(k + 1) * P])
                for k, (query, key) in enumerate(((0, P), (3 * P, P))):
                    for r in range(2):
                        pair(r, query, key, every, every, psL[:, r, 1, k * P:(k + 1) * P])
                for r in range(2):
                    base = far + 2 * P
                    pair(r, base, base + P, slice(0, 32), slice(32, 64), psL[:, r, 0, 0:P])
                    pair(r, base, base + P, slice(64, 96), slice(96, 128), psL[:, r, 0, 0:P])
                    last = pair(r, base + 2 * P, base + 3 * P, slice(0, 64), slice(64, 128), psL[:, r, 0, 0:P])
                last.then_inc(L_ps, 1)

            def weighted(u, parity):
                eng.wait_ge(A_done, u + 1)
                eng.wait_ge(v_done, u + 1)
                need(eng, oT_done, u)
                for r in range(2):
                    last = eng.matmul(psO[0:KV, r * P:(r + 1) * P], v[:, parity, r, :], A[:, parity, r, :], start=True, stop=True)
                last.then_inc(O_ps, 1)

            def project_out(u, parity):
                eng.wait_ge(oT_done, u + 1)
                need(eng, x1_done, u)
                for r in range(2):
                    last = eng.matmul(psW[:, r * D:(r + 1) * D], oT[:, parity, r, :], w_o[:], start=True, stop=True)
                last.then_inc(W_ps, 1)

            def body(i, parity, on):
                if on(0):
                    levels(i, parity)
                if on(-1):
                    project_out(i - 1, 1 - parity)
                if isinstance(i, int) and i == -2:
                    eng.wait_ge(w_dma, NW)
                if on(2):
                    project(i + 2, parity)
                if on(3):
                    transposes(i + 3, 1 - parity)
                if on(0):
                    weighted(i, parity)
            run_skewed(eng, units, LEAD, TAIL, body)


HEADS = 16
HD = D // HEADS


def xattn_weights(nc, ctx, hbm):
    W = {name: ctx.enter_context(nc.sbuf_tensor("a_" + name, shape, F32)) for name, shape in (
        ("w_q", [P, DC, D]), ("w_k", [P, DC, D]), ("w_v", [P, DC, D]), ("w_o", [P, DC, D]),
        ("b_cols", [P, 2, DC]),
        ("odd_scale", [P, 2]),
        ("half_rows", [P, 2]),
        ("mhalf", [P, 2]), ("b_v", [P, D]), ("b_o", [P, D]), ("router", [P, D]))}
    W["dma"] = ctx.enter_context(nc.semaphore("a_w_dma"))
    W["count"] = 11 * 16

    def load(sp):
        for n, name in (("w_q", "Wq"), ("w_k", "Wk"), ("w_v", "Wv"), ("w_o", "Wo")):
            sp.dma_start(W[n][:], hbm["L0_xattn_" + name].rearrange("(c p) n -> p c n", p=P)).then_inc(W["dma"], 16)
        for n, name in (("b_cols", "xattn_bias_cols"), ("odd_scale", "odd_scale"), ("half_rows", "half_rows"), ("mhalf", "mhalf")):
            sp.dma_start(W[n][:], hbm[name]).then_inc(W["dma"], 16)
        for n, name in (("b_v", "L0_xattn_bv"), ("b_o", "L0_xattn_bo"), ("router", "router")):
            sp.dma_start(W[n][:], hbm[name].partition_broadcast(P)).then_inc(W["dma"], 16)
    return W, load


def xattn_phase(nc, units, hbm, W, x_all, ident, ln3_mean, ln3_rstd, ln3_dot, loads_after):
    with ExitStack() as ctx:
        sb = lambda name, shape, dt=F32: ctx.enter_context(nc.sbuf_tensor(name, shape, dt))
        ps = lambda name, shape, dt=F32: ctx.enter_context(nc.psum_tensor(name, shape, dt))
        sem = lambda name: ctx.enter_context(nc.semaphore(name))

        w_q, w_k, w_v, w_o, b_cols, odd_scale, half_rows, mhalf, b_v, b_o, router = (
            W[n] for n in ("w_q", "w_k", "w_v", "w_o", "b_cols", "odd_scale", "half_rows", "mhalf", "b_v", "b_o", "router"))
        w_dma, NW = W["dma"], W["count"]
        qb_cols = sb("a_qb_cols", [P, 2, DC])
        ident_bf = sb("a_ident_bf", [P, P], BF16)

        ctx_in = sb("a_ctx", [P, 2, 2, D])
        stats = sb("a_stats", [P, 2, 6])
        mv = sb("a_mv", [P, 2, 2])
        vare = sb("a_vare", [P, 2])
        rstd = sb("a_rstd", [P, 2])
        hn = sb("a_hn", [P, 2, D])
        hT = sb("a_hT", [P, DC, 2, P])
        cT = sb("a_cT", [P, DC, 2, P])
        qz = sb("a_qz", [P, 2, 2, DC, 2, P])
        kT = sb("a_kT", [P, 2, DC, 2, P])
        qz_bf = sb("a_qz_bf", [P, 2, 2, DC, 2, P], BF16)
        k_bf = sb("a_k_bf", [P, 2, DC, 2, P], BF16)
        v1 = sb("a_v1", [P, 2, 2, HEADS, 2 * HD])
        nmax = sb("a_nmax", [P, 2, 4], BF16)
        pT = sb("a_pT", [P, 2, 4, 4, P])
        parts = sb("a_parts", [P, 2, 2, 2 * P])
        rden = sb("a_rden", [P, 2, P])
        oT = sb("a_oT", [P, 2, DC, P])
        stats3 = sb("a_stats3", [P, 2, 6])
        mv3 = sb("a_mv3", [P, 2, 2])
        vare3 = sb("a_vare3", [P, 2])
        prod = sb("a_prod", [P, 2, D])

        psA = ps("a_psA", [P, 512])
        psB = ps("a_psB", [P, 512])
        psC = ps("a_psC", [P, 512])
        psM = [ps(f"a_psM{i}", [P, 512]) for i in range(2)]
        psE = [ps(f"a_psE{i}", [P, 512]) for i in range(2)]
        psO = ps("a_psO", [P, 512])

        ctx_dma = [sem("a_ctx_even"), sem("a_ctx_odd")]
        dve_tally = sem("a_dve_tally")
        pool_tally = sem("a_pool_tally")
        setup_v = sem("a_setup_v")
        bn_done = sem("a_bn_done")
        bn3_done = sem("a_bn3_done")
        mean3_done = sem("a_mean3_done")
        kept_done = sem("a_kept_done")
        rden_done = sem("a_rden_done")
        parts_done = sem("a_parts_done")
        joined = sem("a_joined")
        swapped = sem("a_swapped")
        vare_done = sem("a_vare_done")
        vare3_done = sem("a_vare3_done")
        rstd3_done = sem("a_rstd3_done")
        stats_done = sem("a_stats_done")
        rstd_done = sem("a_rstd_done")
        hn_done = sem("a_hn_done")
        bo_done = sem("a_bo_done")
        hT_ps = sem("a_hT_ps")
        cT_ps = sem("a_cT_ps")
        hT_done = sem("a_hT_done")
        cT_done = sem("a_cT_done")
        q_ps = sem("a_q_ps")
        k_ps = sem("a_k_ps")
        v_ps = sem("a_v_ps")
        q_done = sem("a_q_done")
        k_done = sem("a_k_done")
        v_done = sem("a_v_done")
        qk_bf_done = sem("a_qk_bf_done")
        max_ps = sem("a_max_ps")
        nmax_done = sem("a_nmax_done")
        score_ps = sem("a_score_ps")
        p_done = sem("a_p_done")
        pv_ps = sem("a_pv_ps")
        oT_done = sem("a_oT_done")
        wo_ps = sem("a_wo_ps")
        x2_done = sem("a_x2_done")
        prod_done = sem("a_prod_done")
        dot_done = sem("a_dot_done")

        block = ctx.enter_context(nc.Block())

        @block.sync
        def _(sp):
            c_src = hbm["ctx_1024"].rearrange("b t d -> t b d")

            def body(u, parity, last):
                need(sp, cT_ps, u - 1)
                sp.dma_start(ctx_in[:, parity], c_src[:, bass.ds(u * 2, 2), :]).then_inc(ctx_dma[parity], 16)
            run_units(sp, units, 0, body)
            for load in loads_after:
                load(sp)

        LEAD, TAIL, DRAIN = 2, 2, 2

        @block.gpsimd
        def _(eng):
            eng.wait_ge(w_dma, NW)
            def rstd_of(u):
                eng.wait_ge(stats_done, u + 1)
                need(eng, hn_done, u)
                settle(eng, pool_tally)
                eng.tensor_scalar(vare[:], mv[:, :, 1], 1.0, LN_EPS, ALU.mult, ALU.add).then_inc(vare_done, 1)
                eng.wait_ge(vare_done, u + 1)
                eng.tensor_tensor(rstd[:], vare[:], mhalf[:], ALU.pow).then_inc(rstd_done, 1)

            def narrow(u, parity):
                need(eng, max_ps, 8 * (u - 1))
                eng.wait_ge(k_done, u + 1)
                settle(eng, pool_tally)
                eng.tensor_scalar(k_bf[:, parity], kT[:, parity], 1.0, 0.0, ALU.mult, ALU.add)
                eng.wait_ge(q_done, u + 1)
                settle(eng, pool_tally)
                eng.tensor_scalar(qz_bf[:, parity], qz[:, parity], 1.0, 0.0, ALU.mult, ALU.add).then_inc(qk_bf_done, 1)

            def bias_out(u):
                eng.wait_ge(hn_done, u + 1)
                rows = x_all[:, bass.ds(u * 2, 2), :]
                eng.tensor_tensor(rows, rows, b_o[:].unsqueeze(1).broadcast_to([P, 2, D]), ALU.add).then_inc(bo_done, 1)

            def join(u, r):
                eng.wait_ge(parts_done, u * 2 + r + 1)
                eng.tensor_tensor(parts[:, 0], parts[:, 0], parts[:, 1], ALU.add).then_inc(joined, 1)

            def rstd3_of(u):
                eng.wait_ge(mean3_done, u + 1)
                need(eng, rstd3_done, u)
                settle(eng, pool_tally)
                eng.tensor_scalar(vare3[:], mv3[:, :, 1], 1.0, LN_EPS, ALU.mult, ALU.add).then_inc(vare3_done, 1)
                eng.wait_ge(vare3_done, u + 1)
                eng.tensor_tensor(ln3_rstd[:, bass.ds(u * 2, 2)], vare3[:], mhalf[:], ALU.pow).then_inc(rstd3_done, 1)

            def route(u):
                eng.wait_ge(x2_done, 2 * u + 2)
                need(eng, dot_done, u)
                eng.tensor_tensor(prod[:], x_all[:, bass.ds(u * 2, 2), :],
                                  router[:].unsqueeze(1).broadcast_to([P, 2, D]), ALU.mult).then_inc(prod_done, 1)

            def body(i, parity, on):
                if on(-2):
                    route(i - 2)
                if on(-1):
                    join(i - 1, 1)
                if on(1):
                    narrow(i + 1, 1 - parity)
                    bias_out(i + 1)
                if on(0):
                    join(i, 0)
                if on(2):
                    rstd_of(i + 2)
                if on(-2):
                    rstd3_of(i - 2)
            run_skewed(eng, units, LEAD, TAIL, body, DRAIN)

        @block.scalar
        def _(eng):
            eng.wait_ge(setup_v, 1)

            def rows_turned(u):
                eng.wait_ge(hT_ps, u + 1)
                need(eng, q_ps, u)
                eng.activation(hT[:], psA[:].rearrange("p (c b t) -> p c b t", c=DC, b=2), ACT.Copy).then_inc(hT_done, 1)

            def context_turned(u):
                eng.wait_ge(cT_ps, u + 1)
                need(eng, v_ps, u)
                eng.activation(cT[:], psB[:].rearrange("p (c b t) -> p c b t", c=DC, b=2), ACT.Copy).then_inc(cT_done, 1)

            def queries(u, parity):
                eng.wait_ge(q_ps, u + 1)
                need(eng, score_ps, 8 * (u - 1))
                need(eng, qk_bf_done, u - 1)
                for odd in range(2):
                    for ch in range(DC):
                        last = eng.activation(qz[:, parity, odd, ch], psA[:, ch * 2 * P:(ch + 1) * 2 * P].rearrange("p (b t) -> p b t", b=2),
                                              ACT.Identity, bias=qb_cols[:, odd, ch:ch + 1], scale=odd_scale[:, odd:odd + 1])
                last.then_inc(q_done, 1)

            def keys(u, parity):
                eng.wait_ge(k_ps, u + 1)
                need(eng, score_ps, 8 * (u - 1))
                need(eng, qk_bf_done, u - 1)
                for ch in range(DC):
                    last = eng.activation(kT[:, parity, ch], psA[:, ch * 2 * P:(ch + 1) * 2 * P].rearrange("p (b t) -> p b t", b=2),
                                          ACT.Identity, bias=b_cols[:, 1, ch:ch + 1])
                last.then_inc(k_done, 1)

            def weights(u, j):
                eng.wait_ge(score_ps, u * 8 + j + 1)
                need(eng, pv_ps, (u - 1) * 2 + j // 4 + 1)
                eng.activation(pT[:, j // 4, j % 4], psE[j % 2][:].rearrange("p (k t) -> p k t", k=4), ACT.Exp).then_inc(p_done, 1)

            def parts_of(u, r):
                row = u * 2 + r
                eng.wait_ge(pv_ps, row + 1)
                need(eng, oT_done, row * 2)
                for odd in range(2):
                    for what in range(2):
                        half = odd ^ what
                        last = eng.activation(parts[:, odd, what], psO[:, odd * 2 * P:(odd + 1) * 2 * P], ACT.Copy, scale=half_rows[:, half:half + 1])
                last.then_inc(parts_done, 1)

            def body(i, parity, on):
                for j in range(8):
                    if on(0):
                        weights(i, j)
                    if j == 0 and on(1):
                        context_turned(i + 1)
                    if j == 1 and on(1):
                        rows_turned(i + 1)
                    if j == 1 and on(-1):
                        parts_of(i - 1, 1)
                    if j == 5 and on(0):
                        parts_of(i, 0)
                    if j == 2 and on(1):
                        keys(i + 1, 1 - parity)
                    if j == 4 and on(1):
                        queries(i + 1, 1 - parity)
            run_skewed(eng, units, LEAD, TAIL, body, DRAIN)

        @block.vector
        def _(eng):
            eng.wait_ge(w_dma, NW)
            for odd in range(2):
                eng.tensor_scalar(qb_cols[:, odd, :], b_cols[:, 0, :], odd_scale[:, odd:odd + 1], None, ALU.mult)
            eng.tensor_copy(ident_bf[:], ident[:])
            eng.memset(v1[:], 1.0).then_inc(setup_v, 1)
            eng.wait_ge(setup_v, 1)

            def stats_of(u):
                need(eng, stats_done, u)
                for r in range(2):
                    last = eng.bn_stats(stats[:, r, :], x_all[:, u * 2 + r, :])
                last.then_inc(bn_done, 1)

            def mean_of(u):
                eng.wait_ge(bn_done, u + 1)
                need(eng, hn_done, u)
                settle(eng, dve_tally)
                for r in range(2):
                    last = eng.bn_aggr(mv[:, r, :], stats[:, r, :])
                last.then_inc(stats_done, 1)

            def norm_of(u):
                eng.wait_ge(stats_done, u + 1)
                need(eng, hT_ps, u)
                eng.wait_ge(rstd_done, u + 1)
                for r in range(2):
                    last = eng.tensor_scalar(hn[:, r, :], x_all[:, u * 2 + r, :], mv[:, r, 0:1],
                                             rstd[:, r:r + 1], ALU.subtract, ALU.mult)
                last.then_inc(hn_done, 1)

            def maxima(u, j):
                eng.wait_ge(max_ps, u * 8 + j + 1)
                need(eng, score_ps, u * 8 + j - 1)
                eng.tensor_reduce(nmax[:, j % 2, :], psM[j % 2][:].rearrange("p (k s) -> p k s", k=4), AX.X, ALU.max,
                                  negate=True).then_inc(nmax_done, 1)

            def values(u, parity):
                eng.wait_ge(v_ps, u + 1)
                need(eng, pv_ps, 2 * (u - 1))
                for r in range(2):
                    for odd in range(2):
                        heads = v1[:, parity, r].rearrange("p (n k) m -> p n k m", k=2)[:, :, odd, odd * HD:(odd + 1) * HD]
                        own = lambda t: t.rearrange("p (n k i) -> p n k i", k=2, i=HD)[:, :, odd, :]
                        last = eng.tensor_tensor(heads, own(psB[:, r * D:(r + 1) * D]), own(b_v[:]), ALU.add)
                last.then_inc(v_done, 1)

            def normalise(u, r, ch):
                row = u * 2 + r
                eng.wait_ge(joined, row + 1)
                need(eng, oT_done, (row - 1) * 2 + ch + 1)
                eng.reciprocal(rden[:, ch, :], parts[:, 0, 1, ch * P:(ch + 1) * P]).then_inc(rden_done, 1)
                eng.wait_ge(rden_done, row * 2 + ch + 1)
                settle(eng, dve_tally)
                eng.stream_shuffle(rden[:, ch, :], rden[:, ch, :], [(i + HD) % 32 for i in range(32)]).then_inc(swapped, 1)
                need(eng, wo_ps, row - 1)
                eng.wait_ge(swapped, row * 2 + ch + 1)
                eng.tensor_tensor(oT[:, r, ch, :], parts[:, 0, 0, ch * P:(ch + 1) * P], rden[:, ch, :], ALU.mult).then_inc(oT_done, 1)

            def residual(u, r):
                eng.wait_ge(wo_ps, u * 2 + r + 1)
                eng.wait_ge(bo_done, u + 1)
                row = x_all[:, u * 2 + r, :]
                eng.tensor_tensor(row, psC[:, r * D:(r + 1) * D], row, ALU.add).then_inc(x2_done, 1)

            def stats3_of(u):
                eng.wait_ge(x2_done, u * 2 + 2)
                need(eng, mean3_done, u)
                settle(eng, dve_tally)
                for r in range(2):
                    last = eng.bn_stats(stats3[:, r, :], x_all[:, u * 2 + r, :])
                last.then_inc(bn3_done, 1)

            def mean3_of(u):
                eng.wait_ge(bn3_done, u + 1)
                need(eng, kept_done, u)
                need(eng, vare3_done, u)
                settle(eng, dve_tally)
                for r in range(2):
                    last = eng.bn_aggr(mv3[:, r, :], stats3[:, r, :])
                last.then_inc(mean3_done, 1)

            def keep_of(u):
                eng.wait_ge(mean3_done, u + 1)
                eng.tensor_copy(ln3_mean[:, bass.ds(u * 2, 2)], mv3[:, :, 0]).then_inc(kept_done, 1)

            def dot_of(u):
                eng.wait_ge(prod_done, u + 1)
                eng.tensor_reduce(ln3_dot[:, bass.ds(u * 2, 2)], prod[:], AX.X, ALU.add).then_inc(dot_done, 1)

            def body(i, parity, on):
                for j in range(8):
                    if j < 7 and on(0):
                        maxima(i, j + 1)
                    if j == 7 and on(1):
                        maxima(i + 1, 0)
                    if j == 0:
                        if on(1):
                            norm_of(i + 1)
                    if j in (0, 1) and on(-1):
                        normalise(i - 1, 0, j)
                    if j == 1 and on(-2):
                        residual(i - 2, 1)
                    if j == 2 and on(-2):
                        stats3_of(i - 2)
                    if j in (3, 4) and on(-1):
                        normalise(i - 1, 1, j - 3)
                    if j == 4 and on(-1):
                        residual(i - 1, 0)
                    if j == 5:
                        if on(-2):
                            mean3_of(i - 2)
                        if on(2):
                            stats_of(i + 2)
                    if j == 6:
                        if on(-2):
                            keep_of(i - 2)
                            dot_of(i - 2)
                        if on(2):
                            mean_of(i + 2)
                    if j == 7 and on(1):
                        values(i + 1, 1 - parity)
            run_skewed(eng, units, LEAD, TAIL, body, DRAIN)

        @block.tensor
        def _(eng):
            eng.wait_ge(w_dma, NW)
            eng.wait_ge(setup_v, 1)

            def turn_rows(u):
                eng.wait_ge(hn_done, u + 1)
                need(eng, q_done, u)
                for ch in range(DC):
                    for r in range(2):
                        last = eng.transpose(psA[:, (ch * 2 + r) * P:(ch * 2 + r + 1) * P], hn[:, r, ch * P:(ch + 1) * P], ident[:])
                last.then_inc(hT_ps, 1)

            def turn_context(u, parity):
                eng.wait_ge(ctx_dma[parity], (u - parity) * 8 + 16)
                need(eng, v_done, u)
                for ch in range(DC):
                    for r in range(2):
                        last = eng.transpose(psB[:, (ch * 2 + r) * P:(ch * 2 + r + 1) * P], ctx_in[:, parity, r, ch * P:(ch + 1) * P], ident[:])
                last.then_inc(cT_ps, 1)

            def features(out, w, src):
                for m in range(DC):
                    for ch in range(DC):
                        last = eng.matmul(out[:, m * 2 * P:(m + 1) * 2 * P], w[:, ch, m * P:(m + 1) * P], src[:, ch],
                                          start=ch == 0, stop=ch == DC - 1)
                return last

            def queries(u):
                eng.wait_ge(hT_done, u + 1)
                eng.wait_ge(k_done, u + 1)
                features(psA, w_q, hT).then_inc(q_ps, 1)

            def keys(u):
                eng.wait_ge(cT_done, u + 1)
                eng.wait_ge(hT_done, u + 1)
                features(psA, w_k, cT).then_inc(k_ps, 1)

            def values(u, r):
                eng.wait_ge(cT_done, u + 1)
                for ch in range(DC):
                    last = eng.matmul(psB[:, r * D:(r + 1) * D], cT[:, ch, r, :], w_v[:, ch, :], start=ch == 0, stop=ch == DC - 1)
                if r == 1:
                    last.then_inc(v_ps, 1)

            def rough_scores(u, parity, j):
                r, q = j // 4, j % 4
                rows = slice(32 * q, 32 * q + 32)
                eng.wait_ge(qk_bf_done, u + 1)
                need(eng, nmax_done, u * 8 + j - 1)
                for ch in range(DC):
                    for odd in range(2):
                        k = ch * 2 + odd
                        last = eng.matmul(psM[j % 2][:, k * P:(k + 1) * P], qz_bf[rows, parity, odd, ch, r, :], k_bf[rows, parity, ch, r, :],
                                          start=True, stop=True)
                last.then_inc(max_ps, 1)

            def scores(u, parity, j):
                r, q = j // 4, j % 4
                rows = slice(32 * q, 32 * q + 32)
                need(eng, p_done, u * 8 + j - 1)
                eng.wait_ge(nmax_done, u * 8 + j + 1)
                for k in range(4):
                    eng.matmul(psE[j % 2][:, k * P:(k + 1) * P], nmax[:, j % 2, k:k + 1].broadcast_to([P, P]), ident_bf[:],
                               start=k == 0, stop=False, skip_group_check=True)
                for ch in range(DC):
                    last = eng.matmul(psE[j % 2][:, ch * 2 * P:(ch + 1) * 2 * P], kT[rows, parity, ch, r, :], qz[rows, parity, :, ch, r, :],
                                      start=False, stop=True, skip_group_check=True)
                last.then_inc(score_ps, 1)

            def weigh(u, parity, r, ch):
                eng.wait_ge(p_done, u * 8 + r * 4 + 4)
                eng.wait_ge(v_done, u + 1)
                need(eng, parts_done, u * 2 + r)
                for odd in range(2):
                    for q in range(4):
                        last = eng.matmul(psO[32 * q:32 * q + 32, (2 * odd + ch) * P:(2 * odd + ch + 1) * P],
                                          v1[:, parity, r, 8 * ch + 2 * q + odd, :], pT[:, r, q, 2 * ch + odd, :],
                                          start=True, stop=True, tile_position=(0, 32 * q))
                if ch == 1:
                    last.then_inc(pv_ps, 1)

            def project_out(u, r):
                eng.wait_ge(oT_done, (u * 2 + r) * 2 + 2)
                need(eng, x2_done, u * 2 + r)
                for ch in range(DC):
                    last = eng.matmul(psC[:, r * D:(r + 1) * D], oT[:, r, ch, :], w_o[:, ch, :], start=ch == 0, stop=ch == DC - 1)
                last.then_inc(wo_ps, 1)

            def body(i, parity, on):
                other = 1 - parity
                for j in range(8):
                    if j < 7 and on(0):
                        rough_scores(i, parity, j + 1)
                    if j == 7 and on(1):
                        rough_scores(i + 1, other, 0)
                    if on(0):
                        scores(i, parity, j)
                    if j == 0 and on(1):
                        turn_context(i + 1, other)
                    if j == 1 and on(1):
                        turn_rows(i + 1)
                    if j in (0, 1) and on(-1):
                        weigh(i - 1, other, 1, j)
                    if j in (4, 5) and on(0):
                        weigh(i, parity, 0, j - 4)
                    if j == 2 and on(1):
                        keys(i + 1)
                    if j == 3 and on(-1):
                        project_out(i - 1, 0)
                    if j == 4 and on(1):
                        queries(i + 1)
                    if j in (5, 6) and on(1):
                        values(i + 1, j - 5)
                    if j == 7 and on(-1):
                        project_out(i - 1, 1)
            run_skewed(eng, units, LEAD, TAIL, body, DRAIN)


SLOTS = 16
ROWS_PER_TILE = P // SLOTS
FF = 1024
FC = FF // P
RMS_EPS = 1e-6
LOWEST = -3.0e38
MAGIC = 12582912.0
TWO_PI = (6.28125, 1.9350051879882812e-03, 3.019916050561733e-07)
PI = 3.1415925


def route_weights(nc, ctx, hbm, tiles):
    W = {name: ctx.enter_context(nc.sbuf_tensor("r_" + name, shape, dt)) for name, shape, dt in (
        ("router", [P, D], F32), ("router_b", [P, 1], F32), ("iota_p", [P, 1], F32), ("own_slot", [P, 2], F32),
        ("pos_i", [P, 4], I32), ("pos_own", [P, tiles, 4], F32), ("inv_freq", [P, HD // 2], F32))}
    W["dma"] = ctx.enter_context(nc.semaphore("r_w_dma"))
    W["count"] = 7 * 16

    def load(sp):
        for n, name in (("iota_p", "iota_p"), ("own_slot", "own_slot"), ("pos_i", "positions"), ("pos_own", "pos_own"), ("inv_freq", "inv_freq")):
            sp.dma_start(W[n][:], hbm[name]).then_inc(W["dma"], 16)
        for n, name in (("router", "router"), ("router_b", "L0_ffn_router_b")):
            sp.dma_start(W[n][:], hbm[name].partition_broadcast(P)).then_inc(W["dma"], 16)
    return W, load


def route_phase(nc, hbm, rows, W, out, ln3_mean, ln3_dot, ident, scratch_idx):
    tiles = rows // ROWS_PER_TILE
    with ExitStack() as ctx:
        sb = lambda name, shape, dt=F32: ctx.enter_context(nc.sbuf_tensor(name, shape, dt))
        ps = lambda name, shape, dt=F32: ctx.enter_context(nc.psum_tensor(name, shape, dt))
        sem = lambda name: ctx.enter_context(nc.semaphore(name))
        router, router_b, iota_p, own_slot, pos_i, pos_own, inv_freq = (
            W[n] for n in ("router", "router_b", "iota_p", "own_slot", "pos_i", "pos_own", "inv_freq"))
        w_dma, NW = W["dma"], W["count"]
        pos_f = sb("r_pos_f", [P, 4])
        rsum = sb("r_rsum", [P, 1])
        w_all = sb("r_w_all", [P, rows])
        wt = sb("r_wt", [P, P])
        wt2 = sb("r_wt2", [P, P])
        idx_u = sb("r_idx_u", [P, SLOTS], U32)
        idx_f = sb("r_idx_f", [P, SLOTS])
        top = sb("r_top", [P, SLOTS])
        keep = sb("r_keep", [P, P])
        idx_b = sb("r_idx_b", [P, rows * SLOTS])
        sel = sb("r_sel", [P, rows * SLOTS])
        idx_c = sb("r_idx_c", [P, tiles])
        pos_s = sb("r_pos_s", [P, tiles])
        turns = sb("r_turns", [P, tiles, HD // 2])
        over = sb("r_over", [P, tiles, HD // 2])
        ang = sb("r_ang", [P, 2, tiles, HD // 2])
        psW = ps("r_psW", [P, 512])
        psK = ps("r_psK", [P, 512])
        psP = ps("r_psP", [P, 512])
        dve = sem("r_dve")
        w_done = sem("r_w_done")
        wt_ps = sem("r_wt_ps")
        top_done = sem("r_top_done")
        keep_ps = sem("r_keep_ps")
        scratch_out = sem("r_scratch_out")
        scratch_in = sem("r_scratch_in")
        sel_done = sem("r_sel_done")
        pos_ps = sem("r_pos_ps")
        ang_done = sem("r_ang_done")
        block = ctx.enter_context(nc.Block())
        scratch_w = nc.dram_tensor("scratch_w", [rows * SLOTS], F32).ap()

        @block.sync
        def _(sp):
            sp.wait_ge(top_done, 1)
            sp.dma_start(scratch_idx.rearrange("(b r) -> b r", r=SLOTS), idx_f[:]).then_inc(scratch_out, 16)
            sp.dma_start(scratch_w.rearrange("(b r) -> b r", r=SLOTS), top[:]).then_inc(scratch_out, 16)
            sp.wait_ge(scratch_out, 32)
            sp.dma_start(idx_b[:], scratch_idx.partition_broadcast(P)).then_inc(scratch_in, 16)
            with nc.allow_non_contiguous_dma(reason="a slot on each partition"):
                sp.dma_start(idx_c[:], scratch_idx.rearrange("(i p) -> p i", p=P)).then_inc(scratch_in, 16)
                sp.dma_start(out["w_sel"][:], scratch_w.rearrange("(i p) -> p i", p=P)).then_inc(scratch_in, 16)

        @block.tensor
        def _(eng):
            eng.wait_ge(w_done, 1)
            eng.transpose(psW[:, 0:P], w_all[:], ident[:]).then_inc(wt_ps, 1)
            eng.wait_ge(top_done, 2)
            eng.transpose(psK[:, 0:P], keep[:], ident[:]).then_inc(keep_ps, 1)
            eng.wait_ge(sel_done, 1)
            for i in range(tiles):
                last = eng.matmul(psP[:, i * 4:(i + 1) * 4], sel[:, i * P:(i + 1) * P], pos_f[:], start=True, stop=True)
            last.then_inc(pos_ps, 1)

        @block.scalar
        def _(eng):
            eng.wait_ge(ang_done, 1)
            eng.activation(out["sin_cos"][:], ang[:], ACT.Sin)

        @block.vector
        def _(eng):
            c = Chain(eng, dve, 0)
            mean = ln3_mean[:]
            eng.wait_ge(w_dma, NW)
            c.link(eng.tensor_reduce(rsum[:], router[:], AX.X, ALU.add))
            c.link(eng.tensor_scalar(w_all[:], mean, rsum[:, 0:1], None, ALU.mult))
            c.link(eng.tensor_tensor(w_all[:], ln3_dot[:], w_all[:], ALU.subtract))
            c.link(eng.tensor_tensor(w_all[:], w_all[:], out["rstd"], ALU.mult))
            eng.tensor_scalar(w_all[:], w_all[:], router_b[:, 0:1], None, ALU.add).then_inc(w_done, 1)
            c.link(eng.scalar_tensor_tensor(out["shift"], mean, -1.0, out["rstd"], ALU.mult, ALU.mult))
            eng.wait_ge(wt_ps, 1)
            c.link(eng.tensor_copy(wt[:], psW[:, 0:P]))
            c.link(eng.max(top[:, 0:8], wt[:]))
            c.link(eng.max_index(idx_u[:, 0:8], top[:, 0:8], wt[:]))
            c.link(eng.match_replace(wt2[:], top[:, 0:8], wt[:], LOWEST))
            c.link(eng.max(top[:, 8:16], wt2[:]))
            c.link(eng.max_index(idx_u[:, 8:16], top[:, 8:16], wt2[:]))
            c.link(eng.tensor_copy(idx_f[:], idx_u[:]))
            eng.memset(idx_f[:, SLOTS - 1:SLOTS], -1.0).then_inc(top_done, 1)
            eng.tensor_scalar(keep[:], wt[:], top[:, SLOTS - 1:SLOTS], None, ALU.is_le).then_inc(top_done, 1)
            c.link(eng.tensor_copy(pos_f[:], pos_i[:]))
            eng.wait_ge(keep_ps, 1)
            c.link(eng.tensor_tensor(out["end_scale"][:], psK[:, 0:rows], out["rstd"], ALU.mult))
            eng.tensor_tensor(out["end_shift"][:], psK[:, 0:rows], out["shift"], ALU.mult)
            c.link(eng.tensor_scalar(out["end_scale"][:], out["end_scale"][:], 1.0, None, ALU.add))
            eng.wait_ge(scratch_in, 48)
            eng.tensor_scalar(sel[:], idx_b[:], iota_p[:, 0:1], None, ALU.is_equal).then_inc(sel_done, 1)
            c.link(eng.tensor_scalar(idx_c[:], idx_c[:], 1.0, None, ALU.add))
            c.link(eng.tensor_tensor(out["idx_own"][:], idx_c[:].unsqueeze(2).broadcast_to([P, tiles, 2]),
                                     own_slot[:].unsqueeze(1).broadcast_to([P, tiles, 2]), ALU.mult))
            c.link(eng.tensor_scalar(out["idx_own"][:], out["idx_own"][:], -1.0, None, ALU.add))
            eng.wait_ge(pos_ps, 1)
            c.link(eng.tensor_tensor(pos_own[:], psP[:, 0:tiles * 4].rearrange("p (i b) -> p i b", b=4), pos_own[:], ALU.mult))
            c.link(eng.tensor_reduce(pos_s[:], pos_own[:], AX.X, ALU.add))
            half = [P, tiles, HD // 2]
            c.link(eng.tensor_tensor(ang[:, 0], pos_s[:].unsqueeze(2).broadcast_to(half), inv_freq[:].unsqueeze(1).broadcast_to(half), ALU.mult))
            c.link(eng.tensor_scalar(turns[:], ang[:, 0], 1.0 / (2.0 * np.pi), MAGIC, ALU.mult, ALU.add))
            c.link(eng.tensor_scalar(turns[:], turns[:], -MAGIC, None, ALU.add))
            for part in TWO_PI:
                c.link(eng.scalar_tensor_tensor(ang[:, 0], turns[:], -part, ang[:, 0], ALU.mult, ALU.add))
            c.link(eng.tensor_scalar(ang[:, 1], ang[:, 0], np.pi / 2, None, ALU.add))
            c.link(eng.tensor_scalar(over[:], ang[:, 1], PI, -2.0 * np.pi, ALU.is_gt, ALU.mult))
            c.link(eng.tensor_tensor(ang[:, 1], ang[:, 1], over[:], ALU.add))
            eng.tensor_scalar(ang[:], ang[:], PI, -PI, ALU.min, ALU.max).then_inc(ang_done, 1)


def ffn_weights(nc, ctx, hbm):
    W = {name: ctx.enter_context(nc.sbuf_tensor("f_" + name, shape, F32)) for name, shape in (
        ("outside", [P, 32]),
        ("odd_scale", [P, 2]),
        ("own_rows", [P, ROWS_PER_TILE]),
        ("iota_p", [P, 1]), ("mhalf", [P, 2]))}
    W["dma"] = ctx.enter_context(nc.semaphore("f_w_dma"))
    W["count"] = 5 * 16

    def load(sp):
        for n, name in (("outside", "outside"), ("odd_scale", "odd_scale"), ("own_rows", "own_rows"),
                        ("iota_p", "iota_p"), ("mhalf", "mhalf")):
            sp.dma_start(W[n][:], hbm[name]).then_inc(W["dma"], 16)
    return W, load


def ffn_phase(nc, hbm, rows, W, r_in, x_all, ident, scratch_idx, x_out):
    tiles = rows // ROWS_PER_TILE
    with ExitStack() as ctx:
        sb = lambda name, shape, dt=F32: ctx.enter_context(nc.sbuf_tensor(name, shape, dt))
        sem = lambda name: ctx.enter_context(nc.semaphore(name))
        W2 = 2
        w_q = sb("f_w_q", [P, DC, D])
        w_k = sb("f_w_k", [P, DC, D])
        w_v = sb("f_w_v", [P, DC, D])
        w_o = sb("f_w_o", [P, DC, D])
        w_1 = sb("f_w_1", [P, DC, FF])
        w_2 = sb("f_w_2", [P, FC, D])
        ln = sb("f_ln", [P, 2, D])
        mask = sb("f_mask", [P, 4, P])
        iota_f = sb("f_iota_f", [P, P])
        mask_dma = sem("f_mask_dma")
        ln_dma = sem("f_ln_dma")
        late_dma = sem("f_late_dma")
        outside, odd_scale, own_rows, iota_p, mhalf = (
            W[n] for n in "outside odd_scale own_rows iota_p mhalf".split())
        w_dma, NW = W["dma"], W["count"]
        idx_b = sb("f_idx_b", [P, W2, P])
        sel = sb("f_sel", [P, W2, P])
        sel_g = sb("f_sel_g", [P, W2, ROWS_PER_TILE, P])
        norms = sb("f_norms", [P, W2, 2, ROWS_PER_TILE])
        sel_t = sb("f_sel_t", [P, W2, 2, P])
        wts = sb("f_wts", [P, W2, HEADS, 32])
        hidden = sb("f_hidden", [P, W2, FC, P])
        rsx = sb("f_rsx", [P, W2, 2])
        xo = sb("f_xo", [P, W2, D])
        xs = sb("f_xs", [P, W2, D])
        hn = sb("f_hn", [P, W2, D])
        hT = sb("f_hT", [P, W2, DC, P])
        vt = sb("f_vt", [P, W2, D])
        qk = sb("f_qk", [P, W2, 2 * D])
        qz = sb("f_qz", [P, W2, 2, DC, P])
        kT = sb("f_kT", [P, W2, DC, P])
        m1 = sb("f_m1", [P, W2, P])
        mk = sb("f_mk", [P, W2, 32])
        ss = sb("f_ss", [P, W2, 2])
        rs = sb("f_rs", [P, W2, 2])
        mx = sb("f_mx", [P, W2, HEADS])
        den = sb("f_den", [P, W2, HEADS])
        ps = ctx.enter_context(nc.psum_tensor("f_ps", [P, W2, 4, 512], F32))

        names = ("idx_dma eq_v sel_v gath_ps m1_a norms_v rsx_v xs_v ss_v rs_v rs_p hn_v msk_ps mk_v z_a hT_ps hT_a qk_ps v_ps rot_v "
                 "sub_v rope_v vt_a qkT_ps qz_a kT_v sc_ps add_v mx_v sc_v ex_a den_v pt_v inv_v pv_ps o_v scat_v oT_ps oT_a "
                 "wo_ps x1_v ss2_v rs2_v rs2_p hn2_v h2T_ps h2T_a w1_ps ge_a w2_ps xo_v proc_v scat_a_ps end_a_v scat_b_ps "
                 "end_v out_dma").split()
        S = {n: sem("f_" + n) for n in names}
        dve_tally = sem("f_dve_tally")
        pool_tally = sem("f_pool_tally")
        setup_v = sem("f_setup_v")
        pe_tally = sem("f_pe_tally")
        out_dma = [S["out_dma"], sem("f_out_dma1")]
        idx_dma = [S["idx_dma"], sem("f_idx_dma1")]
        block = ctx.enter_context(nc.Block())

        def turns(body, eng):
            body(0, False)
            with eng.Fori(1, tiles // W2 - 1) as i:
                body(i, False)
            body(tiles // W2 - 1, True)

        def done(eng, name, i, w):
            eng.wait_ge(S[name], i * W2 + w + 1)

        def used(eng, name, i, w):
            need(eng, S[name], (i - 1) * W2 + w + 1)

        def bank(w, b, lo=0, hi=512):
            return ps[:, w, b, lo:hi]

        def flat(t, w):
            return t[:, w].rearrange("p c s -> p (c s)")

        @block.sync
        def _(sp):
            def slots_of(i):
                for w in range(W2):
                    used(sp, "sel_v", i, w)
                    sp.dma_start(idx_b[:, w, :], scratch_idx[bass.ds((i * W2 + w) * P, P)].partition_broadcast(P)).then_inc(idx_dma[w], 16)

            def body(i, last):
                if not last:
                    slots_of(i + 1)
                for w in range(W2):
                    done(sp, "end_v", i, w)
                    first_row = (i * W2 + w) * ROWS_PER_TILE
                    sp.dma_start(x_out.rearrange("b t d -> t b d")[:, bass.ds(first_row, ROWS_PER_TILE), :],
                                 x_all[:, bass.ds(first_row, ROWS_PER_TILE), :]).then_inc(out_dma[w], 16)
            slots_of(0)
            sp.dma_start(mask[:], hbm["ffn_mask"]).then_inc(mask_dma, 16)
            for k in range(2):
                sp.dma_start(ln[:, k, :], hbm[f"L0_ffn_ln{k + 1}"].partition_broadcast(P)).then_inc(ln_dma, 16)
            sp.dma_start(iota_f[:], hbm["iota_f"]).then_inc(ln_dma, 16)
            for dst, name in ((w_q, "L0_ffn_wq"), (w_k, "L0_ffn_wk"), (w_v, "L0_ffn_wv"), (w_o, "ffn_wo_by_head"), (w_1, "L0_ffn_w1"), (w_2, "L0_ffn_w2")):
                sp.dma_start(dst[:], hbm[name].rearrange("(c p) n -> p c n", p=P)).then_inc(late_dma, 16)
            turns(body, sp)
            for w in range(W2):
                sp.wait_ge(out_dma[w], 16 * (tiles // W2))

        @block.gpsimd
        def _(eng):
            eng.wait_ge(w_dma, NW)

            def rms(i, k, squares, mean, scale, scale_used):
                for w in range(W2):
                    done(eng, squares, i, w)
                    used(eng, scale_used, i, w)
                    settle(eng, pool_tally)
                    eng.tensor_scalar(rs[:, w, k:k + 1], ss[:, w, k:k + 1], 1.0 / D, RMS_EPS, ALU.mult, ALU.add).then_inc(S[mean], 1)
                    done(eng, mean, i, w)
                    eng.tensor_tensor(rs[:, w, k:k + 1], rs[:, w, k:k + 1], mhalf[:, 0:1], ALU.pow).then_inc(S[scale], 1)

            def front(i):
                rms(i, 0, "ss_v", "rs_v", "rs_p", "hn_v")

            def body(i, last):
                rms(i, 1, "ss2_v", "rs2_v", "rs2_p", "hn2_v")
                if not last:
                    front(i + 1)
            front(0)
            turns(body, eng)

        @block.scalar
        def _(eng):
            eng.wait_ge(w_dma, NW)

            def mask_copy(i, w):
                done(eng, "gath_ps", i, w)
                used(eng, "msk_ps", i, w)
                eng.activation(m1[:, w, :], bank(w, 3, 384, 512), ACT.Copy).then_inc(S["m1_a"], 1)

            def copy(name, src_done, i, out, src):
                for w in range(W2):
                    done(eng, src_done, i, w)
                    eng.activation(out(w), src(w), ACT.Copy).then_inc(S[name], 1)

            def kept(i, w):
                done(eng, "gath_ps", i, w)
                for j in range(ROWS_PER_TILE):
                    b = (i * W2 + w) * ROWS_PER_TILE + j
                    last = eng.activation(x_all[:, b, :], x_all[:, b, :], ACT.Identity,
                                          bias=r_in["end_shift"][:, bass.ds(b, 1)], scale=r_in["end_scale"][:, bass.ds(b, 1)])
                last.then_inc(S["z_a"], 1)

            def rows_turned(i):
                copy("hT_a", "hT_ps", i, lambda w: flat(hT, w), lambda w: bank(w, 2, 0, D))

            def body(i, last):
                copy("vt_a", "v_ps", i, lambda w: vt[:, w, :], lambda w: bank(w, 3, 0, D))
                for w in range(W2):
                    done(eng, "qkT_ps", i, w)
                    for odd in range(2):
                        ins = eng.activation(qz[:, w, odd].rearrange("p c s -> p (c s)"), bank(w, 1, 0, D), ACT.Copy, scale=odd_scale[:, odd:odd + 1])
                    ins.then_inc(S["qz_a"], 1)
                for w in range(W2):
                    done(eng, "sc_v", i, w)
                    eng.activation(qk[:, w, :], qk[:, w, :], ACT.Exp).then_inc(S["ex_a"], 1)
                if not last:
                    mask_copy(i + 1, 0)
                copy("oT_a", "oT_ps", i, lambda w: flat(hT, w), lambda w: bank(w, 1, 0, D))
                if not last:
                    mask_copy(i + 1, 1)
                copy("h2T_a", "h2T_ps", i, lambda w: flat(hT, w), lambda w: bank(w, 1, 0, D))
                for w in range(W2):
                    done(eng, "w1_ps", i, w)
                    used(eng, "w2_ps", i, w)
                    eng.activation(hidden[:, w], ps[:, w, 0:2, :].rearrange("p b (f q) -> p (b f) q", q=P), ACT.Gelu_apprx_tanh).then_inc(S["ge_a"], 1)
                for w in range(W2):
                    kept(i, w)
                if not last:
                    rows_turned(i + 1)
            for w in range(W2):
                mask_copy(0, w)
            rows_turned(0)
            turns(body, eng)

        @block.vector
        def _(eng):
            eng.memset(sel_g[:], 0.0).then_inc(setup_v, 1)
            eng.wait_ge(w_dma, NW)
            eng.wait_ge(setup_v, 1)
            tile = lambda i, w: i * W2 + w

            def select(i):
                for w in range(W2):
                    eng.wait_ge(idx_dma[w], i * 16 + 16)
                    used(eng, "sel_v", i, w)
                    used(eng, "msk_ps", i, w)
                    used(eng, "gath_ps", i, w)
                    eng.tensor_scalar(sel[:, w, :], idx_b[:, w, :], iota_p[:, 0:1], None, ALU.is_equal).then_inc(S["eq_v"], 1)
                    done(eng, "eq_v", i, w)
                    diagonal = sel_g[:, w].rearrange("p j s -> p (j s)")
                    for j in range(ROWS_PER_TILE):
                        ins = eng.tensor_copy(diagonal[:, j * (P + SLOTS):j * (P + SLOTS) + SLOTS], sel[:, w, j * SLOTS:(j + 1) * SLOTS])
                    ins.then_inc(S["sel_v"], 1)

            def layer_norm(i):
                for w in range(W2):
                    done(eng, "m1_a", i, w)
                    used(eng, "xs_v", i, w)
                    used(eng, "x1_v", i, w)
                    used(eng, "rsx_v", i, w)
                    eng.tensor_tensor(norms[:, w], bank(w, 3, D, D + 2 * ROWS_PER_TILE).rearrange("p (j k) -> p k j", k=2),
                                      own_rows[:].unsqueeze(1).broadcast_to([P, 2, ROWS_PER_TILE]), ALU.mult).then_inc(S["norms_v"], 1)
                    done(eng, "norms_v", i, w)
                    eng.tensor_reduce(rsx[:, w, :], norms[:, w], AX.X, ALU.add).then_inc(S["rsx_v"], 1)
                    done(eng, "rsx_v", i, w)
                    eng.tensor_scalar(xs[:, w, :], bank(w, 3, 0, D), rsx[:, w, 0:1], rsx[:, w, 1:2], ALU.mult, ALU.add).then_inc(S["xs_v"], 1)
                for w in range(W2):
                    done(eng, "xs_v", i, w)
                    used(eng, "h2T_ps", i, w)
                    eng.tensor_tensor_reduce(hn[:, w, :], xs[:, w, :], xs[:, w, :], 1.0, 0.0, ALU.mult, ALU.add, ss[:, w, 0:1]).then_inc(S["ss_v"], 1)

            def first_norm(i):
                for w in range(W2):
                    done(eng, "ss_v", i, w)
                    done(eng, "rs_p", i, w)
                    eng.scalar_tensor_tensor(hn[:, w, :], xs[:, w, :], rs[:, w, 0:1], ln[:, 0, :], ALU.mult, ALU.mult).then_inc(S["hn_v"], 1)
                for w in range(W2):
                    done(eng, "msk_ps", i, w)
                    used(eng, "add_v", i, w)
                    eng.tensor_tensor(mk[:, w, :], bank(w, 3, 384, 416), outside[:], ALU.add).then_inc(S["mk_v"], 1)

            def body(i, last):
                for w in range(W2):
                    done(eng, "qk_ps", i, w)
                    used(eng, "oT_ps", i, w)
                    used(eng, "inv_v", i, w)
                    rot = qz[:, w].rearrange("p o c s -> p (o c s)")
                    table = [r_in["sin_cos"][:, k, bass.ds(tile(i, w), 1), :].broadcast_to([P, 4 * HEADS, HD // 2]) for k in range(2)]
                    t = bank(w, 2).rearrange("p (n i) -> p n i", i=HD // 2)
                    eng.tensor_tensor(rot.rearrange("p (n i) -> p n i", i=HD // 2), t, table[0], ALU.mult)
                    eng.tensor_tensor(qk[:, w, :].rearrange("p (n i) -> p n i", i=HD // 2), t, table[1], ALU.mult).then_inc(S["rot_v"], 1)
                    done(eng, "rot_v", i, w)
                    halves = qk[:, w, :].rearrange("p (n k i) -> p n k i", k=2, i=HD // 2)
                    others = rot.rearrange("p (n k i) -> p n k i", k=2, i=HD // 2)
                    eng.tensor_tensor(halves[:, :, 0, :], halves[:, :, 0, :], others[:, :, 1, :], ALU.subtract)
                    eng.tensor_tensor(halves[:, :, 1, :], halves[:, :, 1, :], others[:, :, 0, :], ALU.add).then_inc(S["rope_v"], 1)
                for w in range(W2):
                    done(eng, "qkT_ps", i, w)
                    used(eng, "proc_v", i, w)
                    eng.tensor_copy(flat(kT, w), bank(w, 0, 0, D)).then_inc(S["kT_v"], 1)
                if not last:
                    select(i + 1)
                s = [qk[:, w, :].rearrange("p (h k) -> p h k", k=32) for w in range(W2)]
                for w in range(W2):
                    done(eng, "sc_ps", i, w)
                    done(eng, "mk_v", i, w)
                    used(eng, "sc_v", i, w)
                    eng.tensor_tensor(s[w].rearrange("p (q h) k -> p q h k", q=4), ps[:, w, :, 0:P].rearrange("p q (h k) -> p q h k", k=32),
                                      mk[:, w, :].unsqueeze(1).unsqueeze(1).broadcast_to([P, 4, 4, 32]), ALU.add).then_inc(S["add_v"], 1)
                    done(eng, "add_v", i, w)
                    eng.tensor_reduce(mx[:, w, :], s[w], AX.X, ALU.max).then_inc(S["mx_v"], 1)
                    done(eng, "mx_v", i, w)
                    eng.tensor_tensor(s[w], s[w], mx[:, w, :].unsqueeze(2).broadcast_to([P, HEADS, 32]), ALU.subtract).then_inc(S["sc_v"], 1)
                for w in range(W2):
                    used(eng, "scat_b_ps", i, w)
                    shape = [P, 2, P]
                    eng.tensor_tensor(sel_t[:, w], iota_f[:].unsqueeze(1).broadcast_to(shape),
                                      r_in["idx_own"][:, bass.ds(tile(i, w), 1), :].rearrange("p a j -> p (a j)").unsqueeze(2).broadcast_to(shape), ALU.is_equal).then_inc(S["scat_v"], 1)
                for w in range(W2):
                    done(eng, "ex_a", i, w)
                    used(eng, "pv_ps", i, w)
                    used(eng, "o_v", i, w)
                    eng.transpose(wts[:, w].rearrange("p h q -> p (h q)"), qk[:, w, :]).then_inc(S["pt_v"], 1)
                    eng.tensor_reduce(den[:, w, :], s[w], AX.X, ALU.add).then_inc(S["den_v"], 1)
                for w in range(W2):
                    done(eng, "den_v", i, w)
                    eng.reciprocal(den[:, w, :], den[:, w, :]).then_inc(S["inv_v"], 1)
                for w in range(W2):
                    done(eng, "pv_ps", i, w)
                    done(eng, "inv_v", i, w)
                    eng.tensor_tensor(qz[:, w, 0].rearrange("p c s -> p (c s)").rearrange("p (h i) -> p h i", h=HEADS), bank(w, 0, 0, D).rearrange("p (h i) -> p h i", h=HEADS),
                                      den[:, w, :].unsqueeze(2).broadcast_to([P, HEADS, HD]), ALU.mult).then_inc(S["o_v"], 1)
                for w in range(W2):
                    done(eng, "wo_ps", i, w)
                    eng.tensor_tensor(flat(kT, w), bank(w, 2, 0, D), xs[:, w, :], ALU.add).then_inc(S["x1_v"], 1)
                for w in range(W2):
                    done(eng, "x1_v", i, w)
                    eng.tensor_tensor_reduce(hn[:, w, :], flat(kT, w), flat(kT, w), 1.0, 0.0, ALU.mult, ALU.add, ss[:, w, 1:2]).then_inc(S["ss2_v"], 1)
                for w in range(W2):
                    done(eng, "ss2_v", i, w)
                    done(eng, "rs2_p", i, w)
                    eng.scalar_tensor_tensor(hn[:, w, :], flat(kT, w), rs[:, w, 1:2], ln[:, 1, :], ALU.mult, ALU.mult).then_inc(S["hn2_v"], 1)
                if not last:
                    layer_norm(i + 1)
                    first_norm(i + 1)
                for w in range(W2):
                    done(eng, "w2_ps", i, w)
                    used(eng, "scat_b_ps", i, w)
                    eng.tensor_tensor(xo[:, w, :], bank(w, 2, 0, D), flat(kT, w), ALU.add).then_inc(S["xo_v"], 1)
                    done(eng, "xo_v", i, w)
                    eng.tensor_scalar(xo[:, w, :], xo[:, w, :], r_in["w_sel"][:, bass.ds(tile(i, w), 1)], None, ALU.mult).then_inc(S["proc_v"], 1)
                for half, (ready, finished) in enumerate((("scat_a_ps", "end_a_v"), ("scat_b_ps", "end_v"))):
                    for w in range(W2):
                        done(eng, ready, i, w)
                        done(eng, "z_a", i, w)
                        first_row = tile(i, w) * ROWS_PER_TILE + half * 4
                        x_rows = x_all[:, bass.ds(first_row, 4), :].rearrange("p j d -> p (j d)")
                        eng.tensor_tensor(x_rows, ps[:, w, 0:2].rearrange("p b n -> p (b n)"), x_rows, ALU.add).then_inc(S[finished], 1)
            select(0)
            layer_norm(0)
            eng.wait_ge(ln_dma, 48)
            first_norm(0)
            turns(body, eng)

        @block.tensor
        def _(eng):
            eng.wait_ge(w_dma, NW)

            def gather(i, w):
                done(eng, "sel_v", i, w)
                used(eng, "vt_a", i, w)
                used(eng, "add_v", i, w)
                for j in range(ROWS_PER_TILE):
                    eng.matmul(bank(w, 3, 0, D), sel_g[:, w, j, :], x_all[:, (i * W2 + w) * ROWS_PER_TILE + j, :],
                               start=j == 0, stop=j == ROWS_PER_TILE - 1)
                first_row = (i * W2 + w) * ROWS_PER_TILE
                eng.matmul(bank(w, 3, D, D + 2 * ROWS_PER_TILE), sel[:, w, :], r_in["norm"][:, bass.ds(first_row, ROWS_PER_TILE), :],
                           start=True, stop=True)
                alone = 3 if isinstance(i, int) and i == 0 and w == 0 else 0
                for b in range(alone):
                    eng.matmul(bank(w, 3, 384 + b * SLOTS, 384 + (b + 1) * SLOTS), mask[:, b, :], sel[:, w, b * SLOTS:(b + 1) * SLOTS], start=True, stop=True)
                eng.matmul(bank(w, 3, 384 + alone * SLOTS, 512), mask[:, 3, :], sel[:, w, alone * SLOTS:P], start=True, stop=True).then_inc(S["gath_ps"], 1)

            def mask_columns(i):
                for w in range(W2):
                    done(eng, "xs_v", i, w)
                    for q in range(4):
                        g = slice(32 * q, 32 * q + 32)
                        ins = eng.matmul(ps[g, w, 3, 384:416], m1[:, w, g], sel[:, w, g], start=True, stop=True, tile_position=(0, 32 * q))
                    ins.then_inc(S["msk_ps"], 1)

            def turned(out, src):
                for ch in range(DC):
                    ins = eng.transpose(out[:, ch * P:(ch + 1) * P], src[:, ch * P:(ch + 1) * P], ident[:])
                return ins

            def turn_rows(i):
                for w in range(W2):
                    done(eng, "hn_v", i, w)
                    used(eng, "xo_v", i, w)
                    turned(bank(w, 2, 0, D), hn[:, w, :]).then_inc(S["hT_ps"], 1)

            def body(i, last):
                for w in range(W2):
                    done(eng, "hT_a", i, w)
                    done(eng, "mk_v", i, w)
                    for wt, out, ready in ((w_q, bank(w, 2, 0, D), None), (w_k, bank(w, 2, D, 2 * D), "qk_ps"), (w_v, bank(w, 3, 0, D), "v_ps")):
                        for ch in range(DC):
                            ins = eng.matmul(out, hT[:, w, ch, :], wt[:, ch, :], start=ch == 0, stop=ch == DC - 1)
                        if ready:
                            ins.then_inc(S[ready], 1)
                for w in range(W2):
                    done(eng, "rope_v", i, w)
                    used(eng, "end_v", i, w)
                    turned(bank(w, 0, 0, D), qk[:, w, D:2 * D])
                    turned(bank(w, 1, 0, D), qk[:, w, 0:D]).then_inc(S["qkT_ps"], 1)
                for w in range(W2):
                    done(eng, "qz_a", i, w)
                    done(eng, "kT_v", i, w)
                    done(eng, "vt_a", i, w)
                    settle(eng, pe_tally)
                    for q in range(4):
                        rows_q = slice(32 * q, 32 * q + 32)
                        for k in range(4):
                            ch, odd = k // 2, k % 2
                            for g in range(4):
                                slots = slice(32 * g, 32 * g + 32)
                                ins = eng.matmul(ps[slots, w, q, k * 32:(k + 1) * 32], qz[rows_q, w, odd, ch, slots], kT[rows_q, w, ch, slots],
                                                 start=True, stop=True, tile_position=(32 * q, 32 * g))
                    ins.then_inc(S["sc_ps"], 1)
                if not last:
                    gather(i + 1, 0)
                for w in range(W2):
                    done(eng, "pt_v", i, w)
                    settle(eng, pe_tally)
                    for at in range(HEADS):
                        q, ch, odd = at // 4, at % 4 // 2, at % 2
                        h = 8 * ch + 2 * q + odd
                        for g in range(4):
                            slots = slice(32 * g, 32 * g + 32)
                            ins = eng.matmul(ps[slots, w, 0, at * HD:(at + 1) * HD], wts[slots, w, at, :], vt[slots, w, h * HD:(h + 1) * HD],
                                             start=True, stop=True, tile_position=(32 * g, 32 * g))
                    ins.then_inc(S["pv_ps"], 1)
                for w in range(W2):
                    done(eng, "o_v", i, w)
                    turned(bank(w, 1, 0, D), qz[:, w, 0].rearrange("p c s -> p (c s)")).then_inc(S["oT_ps"], 1)
                for w in range(W2):
                    done(eng, "oT_a", i, w)
                    for ch in range(DC):
                        ins = eng.matmul(bank(w, 2, 0, D), hT[:, w, ch, :], w_o[:, ch, :], start=ch == 0, stop=ch == DC - 1)
                    ins.then_inc(S["wo_ps"], 1)
                if not last:
                    gather(i + 1, 1)
                for w in range(W2):
                    done(eng, "hn2_v", i, w)
                    turned(bank(w, 1, 0, D), hn[:, w, :]).then_inc(S["h2T_ps"], 1)
                for w in range(W2):
                    done(eng, "h2T_a", i, w)
                    for f in range(FC):
                        for ch in range(DC):
                            ins = eng.matmul(bank(w, f // 4, (f % 4) * P, (f % 4 + 1) * P), w_1[:, ch, f * P:(f + 1) * P], hT[:, w, ch, :],
                                             start=ch == 0, stop=ch == DC - 1)
                    ins.then_inc(S["w1_ps"], 1)
                if not last:
                    mask_columns(i + 1)
                for w in range(W2):
                    done(eng, "ge_a", i, w)
                    for f in range(FC):
                        ins = eng.matmul(bank(w, 2, 0, D), hidden[:, w, f, :], w_2[:, f, :], start=f == 0, stop=f == FC - 1)
                    ins.then_inc(S["w2_ps"], 1)
                for half, name in enumerate(("scat_a_ps", "scat_b_ps")):
                    if half == 1 and not last:
                        turn_rows(i + 1)
                    for w in range(W2):
                        if half == 0:
                            done(eng, "proc_v", i, w)
                            done(eng, "scat_v", i, w)
                        else:
                            done(eng, "end_a_v", i, w)
                        for k in range(2):
                            for b in range(2):
                                slots = slice(32 * (2 * half + b), 32 * (2 * half + b) + 32)
                                ins = eng.matmul(bank(w, b, k * D, (k + 1) * D), sel_t[slots, w, k, :], xo[slots, w, :], start=True, stop=True)
                        ins.then_inc(S[name], 1)
            eng.wait_ge(mask_dma, 16)
            for w in range(W2):
                gather(0, w)
            mask_columns(0)
            turn_rows(0)
            eng.wait_ge(late_dma, 96)
            turns(body, eng)


def program(nc, hbm, x_out):
    rows = hbm["x"].shape[0]
    tiles = rows // ROWS_PER_TILE
    with ExitStack() as ctx:
        sb = lambda name, shape: ctx.enter_context(nc.sbuf_tensor(name, shape, F32))
        x_all = sb("x_all", [P, rows, D])
        ident = sb("ident", [P, P])
        norm = sb("norm3", [P, rows, 2])
        routed = {
            "norm": norm, "rstd": norm[:, :, 0], "shift": norm[:, :, 1],
            "end_scale": sb("end_scale", [P, rows]), "end_shift": sb("end_shift", [P, rows]),
            "idx_own": sb("idx_own", [P, tiles, 2]), "w_sel": sb("w_sel", [P, tiles]),
            "sin_cos": sb("sin_cos", [P, 2, tiles, HD // 2]),
        }
        scratch_idx = nc.dram_tensor("scratch_idx", [rows * SLOTS], F32).ap()
        f_weights, load_f = ffn_weights(nc, ctx, hbm)
        with ExitStack() as until_routed:
            ln3_mean = until_routed.enter_context(nc.sbuf_tensor("ln3_mean", [P, rows], F32))
            ln3_dot = until_routed.enter_context(nc.sbuf_tensor("ln3_dot", [P, rows], F32))
            r_weights, load_r = route_weights(nc, until_routed, hbm, tiles)
            with ExitStack() as until_attended:
                a_weights, load_a = xattn_weights(nc, until_attended, hbm)
                gla_phase(nc, rows // 2, hbm, x_all, ident, load_a)
                xattn_phase(nc, rows // 2, hbm, a_weights, x_all, ident, ln3_mean, norm[:, :, 0], ln3_dot, (load_r, load_f))
            route_phase(nc, hbm, rows, r_weights, routed, ln3_mean, ln3_dot, ident, scratch_idx)
        ffn_phase(nc, hbm, rows, f_weights, routed, x_all, ident, scratch_idx, x_out)


def shape_constants(rows):
    i = np.arange(P)
    split = np.zeros((P, P), np.int64)
    for k in range(7):
        split[((i[:, None] ^ i[None, :]) >> k) > 0] = 1 << k
    before = i[:, None] < i[None, :]
    near = [(split == h) & before for h in (8, 4, 2, 1)] + [split == 0]
    own = i[:, None] // SLOTS % 2 == np.arange(2)[None, :]
    pos_own = np.zeros((P, rows // ROWS_PER_TILE, 4), np.float32)
    pos_own[:, 1:, 3] = 1.0
    pos_own[i, 0, np.minimum(i // SLOTS, 3)] = 1.0
    k = np.arange(32)
    same = (k[None, :] // SLOTS == (i[:, None] // SLOTS) % 2) & (k[None, :] % SLOTS != SLOTS - 1)
    freq = (1.0 / np.float32(10000.0) ** (np.arange(0, HD, 2, dtype=np.float32) / np.float32(HD))).astype(np.float32)
    odd = (i // HD) % 2
    return {
        "ident": np.eye(P, dtype=np.float32),
        "mask_far": ((split >= 16) & before).astype(np.float32),
        "mask_near": np.ascontiguousarray(np.stack(near, 1).astype(np.int32)),
        "odd_scale": np.stack([(odd == 0) * HD ** -0.5, (odd == 1) * HD ** -0.5], 1).astype(np.float32),
        "half_rows": np.stack([odd == 0, odd == 1], 1).astype(np.float32),
        "mhalf": np.full((P, 2), -0.5, np.float32),
        "iota_p": i[:, None].astype(np.float32),
        "iota_f": np.ascontiguousarray(np.broadcast_to(i[None, :], (P, P)).astype(np.float32)),
        "own_rows": (i[:, None] // SLOTS == np.arange(ROWS_PER_TILE)[None, :]).astype(np.float32),
        "own_slot": own.astype(np.float32),
        "pos_own": pos_own,
        "outside": np.where(same, 0.0, -1e30).astype(np.float32),
        "inv_freq": np.ascontiguousarray(np.broadcast_to(freq[None, :], (P, HD // 2))),
    }


def laid_out(inputs):
    a = {k: np.asarray(v) for k, v in inputs.items()}
    rows = a["x"].shape[0]
    names = ["x", "ctx_1024"] + [f"L0_attn_{n}" for n in ("Wq", "Wk", "Wg", "Wv", "Wo", "bv", "bo")]
    names += [f"L0_xattn_{n}" for n in ("Wq", "Wk", "Wv", "Wo", "bv", "bo")]
    names += [f"L0_ffn_{n}" for n in ("wq", "wk", "wv", "w1", "w2", "ln1", "ln2", "router_b")]
    out = {n: a[n] for n in names}
    out["router"] = a["L0_ffn_router_w"].reshape(D)
    out["attn_bias_cols"] = np.stack([np.tile(a[f"L0_attn_b{n}"], 2) for n in "qkg"], 1)
    out["xattn_bias_cols"] = np.stack([a[f"L0_xattn_b{n}"].reshape(DC, P).T for n in "qk"], 1)
    out["ffn_wo_by_head"] = a["L0_ffn_wo"].reshape(DC, 4, 2, HD, D).transpose(1, 0, 2, 3, 4).reshape(D, D)
    out["ffn_mask"] = a["L0_ffn_attention_mask"][:, 0, :P, :P].transpose(1, 0, 2)
    out["positions"] = a["L0_ffn_position_ids"][:, :P].T
    out.update(shape_constants(rows))
    return {k: np.ascontiguousarray(v) for k, v in out.items()}


def kernel(**inputs):
    import concourse.bacc as bacc
    from concourse.bass_utils import run_bass_kernel_spmd

    nc = bacc.Bacc("TRN2", target_bir_lowering=False, num_devices=1)
    arrays = laid_out(inputs)
    hbm = {k: nc.dram_tensor(f"in_{k}", a.shape, mybir.dt.from_np(a.dtype), kind="ExternalInput").ap() for k, a in arrays.items()}
    x_out = nc.dram_tensor("out_x", arrays["x"].shape, F32, kind="ExternalOutput").ap()
    program(nc, hbm, x_out)
    r = run_bass_kernel_spmd(nc, [{f"in_{k}": a for k, a in arrays.items()}], core_ids=[0])
    return r.results[0]["out_x"]
```
